# Optimizing a Trainium2 kernel written in Bass

```python
import numpy as np
import jax
import jax.numpy as jnp

def _softmax(x, axis=-1):
    return jax.nn.softmax(x, axis=axis)

def _gelu(x):
    return jax.nn.gelu(x, approximate=True)

def _silu(x):
    return jax.nn.silu(x)

def _sigmoid(x):
    return jax.nn.sigmoid(x)

def _layernorm(x, axis=-1, eps=1e-05):
    m = jnp.mean(x, axis=axis, keepdims=True)
    v = jnp.var(x, axis=axis, keepdims=True)
    return (x - m) / jnp.sqrt(v + eps)

def _scatter_add(tgt, idx, src, axis=0):
    return tgt.at[idx].add(src)

def _segment_sum(src, seg, n):
    return jax.ops.segment_sum(src, seg, n)
kernel_name = 'mk_xattn_ffn_d1_seqx_r8_d1c038'

def setup_inputs(seed: int=0):
    np.random.seed(seed)
    _w = jnp.asarray

    def _rec_inputs():
        import jax
        import jax.numpy as jnp
        _rk = jax.random.key(seed)
        x = -0.0003929 + 0.9999 * jax.random.normal(jax.random.fold_in(_rk, 1), (8, 256, 256), jnp.float32)
        _lenS = 256 - jax.random.randint(jax.random.fold_in(_rk, 7), (8,), 0, max(1, 256 // 4) + 1, jnp.int32)
        _lenS2 = 1601 - jax.random.randint(jax.random.fold_in(_rk, 8), (8,), 0, max(1, 1601 // 4) + 1, jnp.int32)
        _ctx_2048P = jax.random.normal(jax.random.fold_in(_rk, 11), (8, 16, 256), jnp.float32)
        _ctx_2048c = jax.random.dirichlet(jax.random.fold_in(_rk, 511), 0.3 * jnp.ones((16,), jnp.float32), (8, 1601))
        _ctx_2048t = jnp.einsum('bsk,bkd->bsd', _ctx_2048c, _ctx_2048P)
        _ctx_2048t = _ctx_2048t * jax.lax.rsqrt(jnp.mean(jnp.square(_ctx_2048t)) + 1e-12) * 0.953939
        ctx_2048 = -1.39393e-06 + 0.999914 * (_ctx_2048t + 0.3 * jax.random.normal(jax.random.fold_in(_rk, 611), (8, 1601, 256), jnp.float32))
        itok_BxS_0_1023 = jax.random.randint(jax.random.fold_in(_rk, 12), (8, 256), 0, 128, jnp.int32)
        return (x, ctx_2048, itok_BxS_0_1023)
    x, ctx_2048, itok_BxS_0_1023 = _rec_inputs()

    def _L0_xattn_setup():
        import jax, jax.numpy as jnp
        import numpy as np
        B, Lq, Lk = (2, 512, 128)
        Q_DIM, KV_DIM = (256, 256)
        H, HD = (16, 128)
        KVC, QC, R = (64, 96, 64)
        LOOKBACK = 8
        NEG = -1e+30

        def _rope(x, L):
            half = x.shape[-1] // 2
            inv_freq = 1.0 / 10000.0 ** (jnp.arange(half, dtype=jnp.float32) / half)
            ang = jnp.arange(L, dtype=jnp.float32)[:, None] * inv_freq
            cos, sin = (jnp.cos(ang), jnp.sin(ang))
            x1, x2 = (x[..., :half], x[..., half:])
            return jnp.concatenate([x1 * cos - x2 * sin, x1 * sin + x2 * cos], axis=-1)
        key = jax.random.key(seed)
        ks = jax.random.split(key, 11)

        def w(k, shape, fan_in):
            return jax.random.normal(k, shape, jnp.float32) / np.sqrt(fan_in).astype(np.float32)
        return {'q': jax.random.normal(ks[0], (B, Lq, Q_DIM), jnp.float32), 'kv': jax.random.normal(ks[1], (B, Lk, KV_DIM), jnp.float32), 'seg_id': jnp.sort(jax.random.randint(ks[2], (B, Lq), 0, Lk), axis=-1), 'W_kvc': w(ks[3], (KV_DIM, KVC), KV_DIM), 'W_dq': w(ks[4], (Q_DIM, QC), Q_DIM), 'W_uq': w(ks[5], (QC, H * HD), QC), 'W_qr': w(ks[6], (QC, H * R), QC), 'W_uk': w(ks[7], (KVC, H * HD), KVC), 'W_kr': w(ks[8], (KVC, R), KVC), 'W_uv': w(ks[9], (KVC, H * HD), KVC), 'W_o': w(ks[10], (H * HD, Q_DIM), H * HD)}
    _L0_xattn_all = _L0_xattn_setup()
    _L0_xattn_in = {k: v for k, v in _L0_xattn_all.items() if k in ('W_kvc', 'W_dq', 'W_uq', 'W_qr', 'W_uk', 'W_kr', 'W_uv', 'W_o')}
    del _L0_xattn_all

    def _L0_ffn_setup():
        import jax, jax.numpy as jnp
        import numpy as np
        N, S, D = (8, 256, 256)
        O = 256
        E = 8
        K = 2
        key = jax.random.key(seed)
        ks = jax.random.split(key, 5)
        scale_in = 1.0 / np.sqrt(D)
        x = jax.random.normal(ks[0], (N, S, D), dtype=jnp.float32)
        gate_w = jax.random.uniform(ks[1], (D, E), dtype=jnp.float32, minval=-scale_in, maxval=scale_in)
        gate_b = jax.random.uniform(ks[2], (E,), dtype=jnp.float32, minval=-scale_in, maxval=scale_in)
        expert_w = jax.random.uniform(ks[3], (E, D, O), dtype=jnp.float32, minval=-scale_in, maxval=scale_in)
        expert_b = jax.random.uniform(ks[4], (E, O), dtype=jnp.float32, minval=-scale_in, maxval=scale_in)
        return {'x': x, 'gate_w': gate_w, 'gate_b': gate_b, 'expert_w': expert_w, 'expert_b': expert_b}
    _L0_ffn_all = _L0_ffn_setup()
    _L0_ffn_in = {k: v for k, v in _L0_ffn_all.items() if k in ('gate_w', 'gate_b', 'expert_w', 'expert_b')}
    del _L0_ffn_all
    return {'x': x, 'ctx_2048': ctx_2048, 'itok_BxS_0_1023': itok_BxS_0_1023, 'L0_xattn_W_kvc': _L0_xattn_in['W_kvc'], 'L0_xattn_W_dq': _L0_xattn_in['W_dq'], 'L0_xattn_W_uq': _L0_xattn_in['W_uq'], 'L0_xattn_W_qr': _L0_xattn_in['W_qr'], 'L0_xattn_W_uk': _L0_xattn_in['W_uk'], 'L0_xattn_W_kr': _L0_xattn_in['W_kr'], 'L0_xattn_W_uv': _L0_xattn_in['W_uv'], 'L0_xattn_W_o': _L0_xattn_in['W_o'], 'L0_ffn_gate_w': _L0_ffn_in['gate_w'], 'L0_ffn_gate_b': _L0_ffn_in['gate_b'], 'L0_ffn_expert_w': _L0_ffn_in['expert_w'], 'L0_ffn_expert_b': _L0_ffn_in['expert_b']}

def reference(x, ctx_2048, itok_BxS_0_1023, L0_xattn_W_kvc, L0_xattn_W_dq, L0_xattn_W_uq, L0_xattn_W_qr, L0_xattn_W_uk, L0_xattn_W_kr, L0_xattn_W_uv, L0_xattn_W_o, L0_ffn_gate_w, L0_ffn_gate_b, L0_ffn_expert_w, L0_ffn_expert_b):
    import jax
    import jax.numpy as jnp

    def _L0_xattn_ref(q, kv, seg_id, W_kvc, W_dq, W_uq, W_qr, W_uk, W_kr, W_uv, W_o):
        import jax, jax.numpy as jnp
        import numpy as np
        B, Lq, Lk = (2, 512, 128)
        Q_DIM, KV_DIM = (256, 256)
        H, HD = (16, 128)
        KVC, QC, R = (64, 96, 64)
        LOOKBACK = 8
        NEG = -1e+30

        def _rope(x, L):
            half = x.shape[-1] // 2
            inv_freq = 1.0 / 10000.0 ** (jnp.arange(half, dtype=jnp.float32) / half)
            ang = jnp.arange(L, dtype=jnp.float32)[:, None] * inv_freq
            cos, sin = (jnp.cos(ang), jnp.sin(ang))
            x1, x2 = (x[..., :half], x[..., half:])
            return jnp.concatenate([x1 * cos - x2 * sin, x1 * sin + x2 * cos], axis=-1)
        b, lq, _ = q.shape
        lk = kv.shape[1]
        kv_c = kv @ W_kvc
        q_c = q @ W_dq
        q_nope = (q_c @ W_uq).reshape(b, lq, H, HD).transpose(0, 2, 1, 3)
        q_rope = (q_c @ W_qr).reshape(b, lq, H, R).transpose(0, 2, 1, 3)
        k_nope = (kv_c @ W_uk).reshape(b, lk, H, HD)
        v = (kv_c @ W_uv).reshape(b, lk, H, HD)
        k_rope = kv_c @ W_kr
        q_rope = _rope(q_rope, lq)
        k_rope = _rope(k_rope, lk)
        scale = 1.0 / np.sqrt(HD + R).astype(np.float32)
        scores = (jnp.einsum('bhqd,bkhd->bhqk', q_nope, k_nope) + jnp.einsum('bhqr,bkr->bhqk', q_rope, k_rope)) * scale
        k_ids = jnp.arange(lk)[None, None, :]
        qs = seg_id[:, :, None]
        good = (k_ids <= qs) & (k_ids >= qs - LOOKBACK)
        scores = jnp.where(good[:, None, :, :], scores, NEG)
        attn = jax.nn.softmax(scores, axis=-1)
        out = jnp.einsum('bhqk,bkhd->bqhd', attn, v).reshape(b, lq, H * HD)
        return out @ W_o

    def _L0_ffn_ref(x, gate_w, gate_b, expert_w, expert_b):
        import jax, jax.numpy as jnp
        import numpy as np
        N, S, D = (8, 256, 256)
        O = 256
        E = 8
        K = 2
        gate_logits = jnp.einsum('nsd,de->nse', x, gate_w) + gate_b
        _, top_idx = jax.lax.top_k(gate_logits, K)
        all_out = jax.nn.relu(jnp.einsum('nsd,edo->nseo', x, expert_w) + expert_b)
        sel = jnp.take_along_axis(all_out, top_idx[..., None], axis=2)
        return sel.mean(axis=2)
    x = x + _L0_xattn_ref(_layernorm(x, axis=-1), ctx_2048, itok_BxS_0_1023, L0_xattn_W_kvc, L0_xattn_W_dq, L0_xattn_W_uq, L0_xattn_W_qr, L0_xattn_W_uk, L0_xattn_W_kr, L0_xattn_W_uv, L0_xattn_W_o)
    x = x + _L0_ffn_ref(_layernorm(x, axis=-1), L0_ffn_gate_w, L0_ffn_gate_b, L0_ffn_expert_w, L0_ffn_expert_b)
    return x

_drawn_inputs = setup_inputs


def setup_inputs(seed=0):
    import zlib

    import numpy as np

    out = dict(_drawn_inputs(seed))
    spreads = {}
    factors = {'L0_ffn_expert_b': 3.963}
    for name, (base, spread) in spreads.items():
        noise = np.random.default_rng([zlib.crc32(name.encode()), seed]).standard_normal(out[name].shape)
        drawn = base * np.exp(spread * noise) if base else spread * noise
        out[name] = jnp.asarray(drawn.astype(out[name].dtype))
    for name, factor in factors.items():
        out[name] = (out[name] * factor).astype(out[name].dtype)
    return out
```

```python
from contextlib import ExitStack

import numpy as np

import concourse.bass as bass
from concourse import mybir

F32 = mybir.dt.float32
F32R = mybir.dt.float32r
BF16 = mybir.dt.bfloat16
I32 = mybir.dt.int32
ALU = mybir.AluOpType
ACT = mybir.ActivationFunctionType
AX = mybir.AxisListType

P = 128
B, L, D = 8, 256, 256
LK = 1601
H, HD = 16, 128
KVC, QC, R = 64, 96, 64
LOOKBACK = 8
NE, O = 8, 256
EPS = 1e-5
NEG = -1e30
SCALE = float(np.float32(1.0) / np.sqrt(HD + R).astype(np.float32))
DC = D // P
TPB = L // P
TILES = B * TPB
HG = 4
GPT = H // HG
GROUPS = TILES * GPT
SLOTS = TPB * GPT
PAIRS = H // 2
KCH = -(-LK // P)
BIG = 3e38


def kernel_program(nc, x, ctx_t, itok, w_kvc, w_dq, w_uq_t, w_qr, w_uk_t, w_kr, w_uv_t, w_o,
                   gate_w, gate_b, expert_w, expert_b, rope, out):
    with ExitStack() as ctx:
        def sb(name, shape, dt=F32):
            return ctx.enter_context(nc.sbuf_tensor(name, shape, dt))

        def sem(name):
            return ctx.enter_context(nc.semaphore(name))

        psum = ctx.enter_context(nc.psum_tensor("psum", [P, 8 * 512], F32))
        bank = [psum[:, 512 * i:512 * i + 512] for i in range(8)]

        x_all = sb("x_all", [P, TILES, D])
        qc_all = sb("qc_all", [QC, B * L])
        wq_hi, wq_lo = sb("wq_hi", [QC, H, P], F32R), sb("wq_lo", [QC, H, P], F32R)
        wo_hi, wo_lo = sb("wo_hi", [P, PAIRS, D], F32R), sb("wo_lo", [P, PAIRS, D], F32R)
        we_hi, we_lo = sb("we_hi", [P, DC, NE * O], F32R), sb("we_lo", [P, DC, NE * O], F32R)
        wg = sb("wg", [P, DC, NE])
        wg_hi, wg_lo = sb("wg_hi", [P, DC, NE], F32R), sb("wg_lo", [P, DC, NE], F32R)
        gate_bias = sb("gate_bias", [P, NE])
        bias3 = sb("bias3", [3, NE * O], BF16)
        ones3 = sb("ones3", [3, P], BF16)
        ident = sb("ident", [P, P])
        kidx = sb("kidx", [P, P])
        ropeq = sb("ropeq", [P, TPB, 2, R])
        wkvc = sb("wkvc", [P, DC, KVC])
        wkr = sb("wkr", [KVC, R])
        kcat = sb("kcat", [P, B, P])
        kT_all = sb("kT_all", [P, B, P])
        seg_i = sb("seg_i", [P, TILES], I32)
        seg = sb("seg", [P, TILES, 2])
        half_neg = sb("half_neg", [P, TILES])
        ones8 = sb("ones8", [P, NE])
        flag = sb("flag", [1, 1], I32)

        block_sems = {}

        def S(name):
            if name not in block_sems:
                block_sems[name] = sem(name)
            return block_sems[name]

        prep_only = ExitStack()

        def tmp(name, shape, dt=F32):
            return prep_only.enter_context(nc.sbuf_tensor(name, shape, dt))

        ctxT = tmp("ctxT", [P, DC, B, P])
        wdq = tmp("wdq", [P, DC, QC])
        wuqT = tmp("wuqT", [P, H, QC])
        wukT = tmp("wukT", [P, H, KVC])
        wuvT = tmp("wuvT", [P, H, KVC])
        wo_raw = tmp("wo_raw", [P, H, D])
        we_raw = tmp("we_raw", [P, DC, NE * O])
        kvT = tmp("kvT", [KVC, B * P])
        wqr = tmp("wqr", [QC, H, R])
        ropek = tmp("ropek", [P, 2, R])
        ka, kb = tmp("ka", [P, B, R]), tmp("kb", [P, B, R])
        xn = tmp("xn", [P, 4, D])
        xnT = tmp("xnT", [P, DC, 4 * P])
        st_all = tmp("st_all", [P, TILES, 6])
        mv_all = tmp("mv_all", [P, TILES, 2])
        veps_all = tmp("veps_all", [P, TILES])
        rstd_all = tmp("rstd_all", [P, TILES])
        eb = tmp("eb", [16, P])
        eb_r = tmp("eb_r", [16, 2, P])
        eb3 = tmp("eb3", [16, 3, P], BF16)
        in_lo, in_both = tmp("in_lo", [P, TILES]), tmp("in_both", [P, TILES])
        row_ok = tmp("row_ok", [P, 1])
        flag_f = tmp("flag_f", [1, 1])
        ones_col = tmp("ones_col", [P, 1])
        kidx_i = tmp("kidx_i", [P, P], I32)

        prep = prep_only.enter_context(nc.Block())

        @prep.sync
        def _(sp):
            sp.dma_start(wkvc[:], w_kvc.rearrange("(c p) n -> p c n", p=P)).then_inc(S("ld_kv"), 16)
            sp.dma_start(wkr[:], w_kr).then_inc(S("ld_kv"), 16)
            sp.dma_start(ropek[:], rope[0:P, :].rearrange("p (a n) -> p a n", a=2)).then_inc(S("ld_kv"), 16)
            for b in range(B):
                sp.dma_start(ctxT[:, :, b, :],
                             ctx_t[b, :, 0:P].rearrange("(c p) k -> p c k", p=P)).then_inc(S("ld_ctx"), 16)
            for i in range(4):
                sp.dma_start(x_all[:, 4 * i:4 * i + 4, :],
                             x[4 * i:4 * i + 4].rearrange("t p d -> p t d")).then_inc(S(f"ld_x{i}"), 16)
            sp.dma_start(wo_raw[:], w_o.rearrange("(h p) n -> p h n", p=P)).then_inc(S("ld_wo"), 16)
            sp.wait_ge(S("eb_step"), 5)
            for r in range(3):
                sp.dma_start(bias3[r:r + 1, :], eb3[:, r, :]).then_inc(S("ld_bias3"), 16)
            sp.wait_ge(S("ld_bias3"), 48)

        @prep.scalar
        def _(act):
            act.dma_start(seg_i[:], itok).then_inc(S("ld_seg"), 16)
            act.dma_start(wdq[:], w_dq.rearrange("(c p) n -> p c n", p=P)).then_inc(S("ld_wdq"), 16)
            act.dma_start(wuqT[:], w_uq_t.rearrange("(h p) n -> p h n", p=P)).then_inc(S("ld_wuq"), 16)
            act.dma_start(wukT[:], w_uk_t.rearrange("(h p) n -> p h n", p=P)).then_inc(S("ld_wuq"), 16)
            act.dma_start(wqr[:], w_qr.rearrange("c (h r) -> c h r", r=R)).then_inc(S("ld_wqr"), 16)
            act.dma_start(wuvT[:], w_uv_t.rearrange("(h p) n -> p h n", p=P)).then_inc(S("ld_wuv"), 16)
            act.dma_start(ropeq[:], rope[0:L, :].rearrange("(t p) (a n) -> p t a n", p=P, a=2)).then_inc(S("ld_small"), 16)
            act.dma_start(wg[:], gate_w.rearrange("(c p) n -> p c n", p=P)).then_inc(S("ld_small"), 16)
            act.dma_start(gate_bias[:], gate_b.partition_broadcast(P)).then_inc(S("ld_small"), 16)
            act.dma_start(eb[:], expert_b.rearrange("e (a n) -> (e a) n", n=P)).then_inc(S("ld_small"), 16)
            for e in range(NE):
                act.dma_start(we_raw[:, :, e * O:(e + 1) * O],
                              expert_w[e].rearrange("(c p) n -> p c n", p=P)).then_inc(S("ld_we"), 16)
            act.wait_ge(S("kvT_mm"), 1)
            for i in range(2):
                act.copy(kvT[:, 512 * i:512 * i + 512], bank[i][0:KVC, :]).then_inc(S("kvT_sb"), 1)
            act.wait_ge(S("fold_q_mm"), 1)
            for i in range(2):
                act.copy(wq_hi[:, 8 * i:8 * i + 8, 0:KVC],
                         bank[4 + i][0:QC, :].rearrange("p (h n) -> p h n", h=8)).then_inc(S("wq_hi_done"), 1)
            act.wait_ge(S("ld_wqr"), 16)
            act.copy(wq_hi[:, :, KVC:P], wqr[:]).then_inc(S("wq_hi_done"), 1)
            act.wait_ge(S("kT_mm"), 1)
            for i in range(2):
                act.copy(kT_all[:, 4 * i:4 * i + 4, :],
                         bank[i][:, :].rearrange("p (b k) -> p b k", b=4)).then_inc(S("kT_sb"), 1)
            for i in range(4):
                act.wait_ge(S("xT_mm"), i + 1)
                if i > 0:
                    act.wait_ge(S("qc_mm"), i)
                act.copy(xnT[:, 0, :], bank[6][:, :]).then_inc(S("xT_sb0"), 1)
                act.wait_ge(S("qc_mm"), i + 1)
                act.copy(qc_all[:, 512 * i:512 * i + 512], bank[2 + i % 2][0:QC, :]).then_inc(S("qc_sb"), 1)
            for i in range(4):
                act.wait_ge(S("fold_o_mm"), i + 1)
                act.copy(wo_hi[:, 2 * i:2 * i + 2, :],
                         bank[(4, 5, 0, 1)[i]][:, :].rearrange("p (q n) -> p q n", q=2)).then_inc(S("wo_hi_done"), 1)
            act.wait_ge(S("ld_we"), 16 * NE)
            for c in range(DC):
                act.copy(we_hi[:, c, :], we_raw[:, c, :]).then_inc(S("we_hi_done"), 1)

        @prep.gpsimd
        def _(pool):
            pool.memset(half_neg[:], -0.5).then_inc(S("half_set"), 1)
            pool.memset(ones_col[:], 1.0).then_inc(S("ones_set"), 1)
            pool.memset(ones3[:], 1.0).then_inc(S("ones_set"), 1)
            pool.memset(ones8[:], 1.0).then_inc(S("ones_set"), 1)
            pool.memset(ident[:], 0.0).then_inc(S("ident_zero"), 1)
            pool.iota(kidx_i[:], [[1, P]], base=0, channel_multiplier=0).then_inc(S("iota_done"), 1)
            pool.wait_ge(S("ident_zero"), 1)
            pool.affine_select(out=ident[:], in_=ident[:], compare_op=ALU.not_equal, fill=1.0, base=0,
                               pattern=[[-1, P]], channel_multiplier=1).then_inc(S("ident_done"), 1)
            pool.wait_ge(S("half_set"), 1)
            for i in range(4):
                pool.wait_ge(S("veps_done"), i + 1)
                t = slice(4 * i, 4 * i + 4)
                pool.tensor_tensor(rstd_all[:, t], veps_all[:, t], half_neg[:, t], ALU.pow).then_inc(S("rstd_done"), 1)

        @prep.vector
        def _(dve):
            dve.wait_ge(S("ld_seg"), 16)
            dve.tensor_copy(seg[:, :, 0], seg_i[:]).then_inc(S("seg_f"), 1)
            dve.wait_ge(S("seg_f"), 1)
            dve.tensor_scalar(seg[:, :, 1], seg[:, :, 0], float(-LOOKBACK), None, ALU.add).then_inc(S("seg_f"), 1)
            dve.tensor_scalar(in_lo[:], seg[:, :, 0], 0.0, None, ALU.is_ge).then_inc(S("seg_f"), 1)
            dve.wait_ge(S("seg_f"), 3)
            dve.scalar_tensor_tensor(out=in_both[:], in0=seg[:, :, 0], scalar=float(P - 1), in1=in_lo[:],
                                     op0=ALU.is_le, op1=ALU.mult).then_inc(S("seg_f"), 1)
            dve.wait_ge(S("seg_f"), 4)
            dve.tensor_reduce(row_ok[:], in_both[:], AX.X, ALU.min).then_inc(S("row_ok_done"), 1)
            dve.wait_ge(S("iota_done"), 1)
            dve.tensor_copy(kidx[:], kidx_i[:]).then_inc(S("kidx_done"), 1)

            def keys():
                dve.wait_ge(S("kv_mm"), 1)
                dve.tensor_copy(kcat[:, :, 0:KVC], bank[2][:, :].rearrange("p (b n) -> p b n", b=B)).then_inc(S("kcat_done"), 1)
                dve.wait_ge(S("kr_mm"), 1)
                kr = bank[3][:, :].rearrange("p (b a n) -> p b a n", b=B, a=2)
                cos = ropek[:, 0:1, :].to_broadcast([P, B, R])
                sin = ropek[:, 1:2, :].to_broadcast([P, B, R]).rearrange("p b (a n) -> p b a n", a=2)
                dve.tensor_tensor(ka[:], bank[3][:, :].rearrange("p (b n) -> p b n", b=B), cos, ALU.mult).then_inc(S("kparts"), 1)
                dve.tensor_tensor(kb[:, :, :].rearrange("p b (a n) -> p b a n", a=2), kr[:, :, ::-1, :], sin,
                                  ALU.mult).then_inc(S("kparts"), 1)
                dve.wait_ge(S("kparts"), 2)
                dve.tensor_tensor(kcat[:, :, KVC:P], ka[:], kb[:], ALU.add).then_inc(S("kcat_done"), 1)

            def norm_stats(i):
                dve.wait_ge(S(f"ld_x{i}"), 16)
                for t in range(4 * i, 4 * i + 4):
                    dve.bn_stats(st_all[:, t, :], x_all[:, t, :]).then_inc(S("st_done"), 1)
                dve.wait_ge(S("st_done"), 4 * i + 4)
                for t in range(4 * i, 4 * i + 4):
                    dve.bn_aggr(mv_all[:, t, :], st_all[:, t, :]).then_inc(S("mv_done"), 1)
                dve.wait_ge(S("mv_done"), 4 * i + 4)
                dve.tensor_scalar(veps_all[:, 4 * i:4 * i + 4], mv_all[:, 4 * i:4 * i + 4, 1], EPS, None,
                                  ALU.add).then_inc(S("veps_done"), 1)

            def norm_apply(i):
                dve.wait_ge(S("rstd_done"), i + 1)
                if i > 0:
                    dve.wait_ge(S("xT_mm"), i)
                for t in range(4 * i, 4 * i + 4):
                    dve.tensor_scalar(xn[:, t % 4, :], x_all[:, t, :], mv_all[:, t, 0:1], rstd_all[:, t:t + 1],
                                      ALU.subtract, ALU.mult).then_inc(S("xn_done"), 1)

            def xT_second(i):
                dve.wait_ge(S("xT_mm"), i + 1)
                if i > 0:
                    dve.wait_ge(S("qc_mm"), i)
                dve.tensor_copy(xnT[:, 1, :], bank[7][:, :]).then_inc(S("xT_sb1"), 1)

            keys()
            norm_stats(0)
            dve.wait_ge(S("wq_hi_done"), 2)
            for i in range(2):
                dve.tensor_tensor(wq_lo[:, 8 * i:8 * i + 8, 0:KVC],
                                  bank[4 + i][0:QC, :].rearrange("p (h n) -> p h n", h=8),
                                  wq_hi[:, 8 * i:8 * i + 8, 0:KVC].bitcast(F32), ALU.subtract).then_inc(S("wq_lo_done"), 1)
            norm_apply(0)
            for i in range(4):
                if i < 3:
                    norm_stats(i + 1)
                xT_second(i)
                if i < 3:
                    norm_apply(i + 1)
            dve.wait_ge(S("wq_hi_done"), 3)
            dve.tensor_tensor(wq_lo[:, :, KVC:P], wqr[:], wq_hi[:, :, KVC:P].bitcast(F32), ALU.subtract).then_inc(S("wq_lo_done"), 1)
            dve.wait_ge(S("ld_small"), 64)
            dve.tensor_copy(wg_hi[:], wg[:]).then_inc(S("wg_done"), 1)
            dve.tensor_copy(eb3[:, 0, :], eb[:]).then_inc(S("eb_step"), 1)
            dve.wait_ge(S("wg_done"), 1)
            dve.tensor_tensor(wg_lo[:], wg[:], wg_hi[:].bitcast(F32), ALU.subtract).then_inc(S("wg_done"), 1)
            for r in range(2):
                dve.wait_ge(S("eb_step"), 2 * r + 1)
                src = eb[:] if r == 0 else eb_r[:, 0, :]
                dve.tensor_tensor(eb_r[:, r, :], src, eb3[:, r, :], ALU.subtract).then_inc(S("eb_step"), 1)
                dve.wait_ge(S("eb_step"), 2 * r + 2)
                dve.tensor_copy(eb3[:, r + 1, :], eb_r[:, r, :]).then_inc(S("eb_step"), 1)
            for i in range(4):
                dve.wait_ge(S("wo_hi_done"), i + 1)
                dve.tensor_tensor(wo_lo[:, 2 * i:2 * i + 2, :],
                                  bank[(4, 5, 0, 1)[i]][:, :].rearrange("p (q n) -> p q n", q=2),
                                  wo_hi[:, 2 * i:2 * i + 2, :].bitcast(F32), ALU.subtract).then_inc(S("wo_lo_done"), 1)
            for c in range(DC):
                dve.wait_ge(S("we_hi_done"), c + 1)
                dve.tensor_tensor(we_lo[:, c, :], we_raw[:, c, :], we_hi[:, c, :].bitcast(F32),
                                  ALU.subtract).then_inc(S("we_lo_done"), 1)
            dve.wait_ge(S("ok_mm"), 1)
            dve.tensor_scalar(flag[:], bank[7][0:1, 0:1], float(P), None, ALU.is_ge).then_inc(S("flag_done"), 1)

        @prep.tensor
        def _(pe):
            pe.wait_ge(S("ld_kv"), 48)
            pe.wait_ge(S("ld_ctx"), 16 * B)
            for i in range(2):
                for c in range(DC):
                    pe.matmul(bank[i][0:KVC, :], wkvc[:, c, :], ctxT[:, c, 4 * i:4 * i + 4, :].rearrange("p b k -> p (b k)"),
                              start=(c == 0), stop=(c == DC - 1))
            mm = None
            for b in range(B):
                for c in range(DC):
                    mm = pe.matmul(bank[2][:, KVC * b:KVC * b + KVC], ctxT[:, c, b, :], wkvc[:, c, :],
                                   start=(c == 0), stop=(c == DC - 1))
                    if b == 0 and c == 0:
                        mm.then_inc(S("kvT_mm"), 1)
            mm.then_inc(S("kv_mm"), 1)
            pe.wait_ge(S("ld_wuq"), 32)
            for h in range(H):
                mm = pe.matmul(bank[4 + h // 8][0:QC, KVC * (h % 8):KVC * (h % 8) + KVC], wuqT[:, h, :], wukT[:, h, :],
                               start=True, stop=True)
            mm.then_inc(S("fold_q_mm"), 1)
            pe.wait_ge(S("kvT_sb"), 2)
            for b in range(B):
                mm = pe.matmul(bank[3][:, R * b:R * b + R], kvT[:, P * b:P * b + P], wkr[:], start=True, stop=True)
            mm.then_inc(S("kr_mm"), 1)
            pe.wait_ge(S("ident_done"), 1)
            pe.wait_ge(S("kcat_done"), 2)
            for b in range(B):
                mm = pe.transpose(bank[b // 4][:, P * (b % 4):P * (b % 4) + P], kcat[:, b, :], ident[:])
            mm.then_inc(S("kT_mm"), 1)
            pe.wait_ge(S("ld_wdq"), 16)
            for i in range(4):
                pe.wait_ge(S("xn_done"), 4 * i + 4)
                if i > 0:
                    pe.wait_ge(S("xT_sb0"), i)
                    pe.wait_ge(S("xT_sb1"), i)
                for t in range(4):
                    for c in range(DC):
                        mm = pe.transpose(bank[6 + c][:, P * t:P * t + P], xn[:, t, P * c:P * c + P], ident[:])
                mm.then_inc(S("xT_mm"), 1)
                pe.wait_ge(S("xT_sb0"), i + 1)
                pe.wait_ge(S("xT_sb1"), i + 1)
                if i > 1:
                    pe.wait_ge(S("qc_sb"), i - 1)
                for c in range(DC):
                    mm = pe.matmul(bank[2 + i % 2][0:QC, :], wdq[:, c, :], xnT[:, c, :], start=(c == 0), stop=(c == DC - 1))
                mm.then_inc(S("qc_mm"), 1)
            pe.wait_ge(S("ld_wuv"), 16)
            pe.wait_ge(S("ld_wo"), 16)
            pe.wait_ge(S("wq_lo_done"), 2)
            pe.wait_ge(S("kT_sb"), 2)
            for i in range(4):
                for q in range(2):
                    for odd in range(2):
                        h = 4 * i + 2 * q + odd
                        mm = pe.matmul(bank[(4, 5, 0, 1)[i]][64 * odd:64 * odd + 64, D * q:D * q + D], wuvT[:, h, :],
                                       wo_raw[:, h, :], start=True, stop=True)
                mm.then_inc(S("fold_o_mm"), 1)
            pe.wait_ge(S("row_ok_done"), 1)
            pe.wait_ge(S("ones_set"), 3)
            pe.wait_ge(S("xT_sb1"), 4)
            pe.matmul(bank[7][0:1, 0:1], row_ok[:], ones_col[:], start=True, stop=True).then_inc(S("ok_mm"), 1)

        prep_only.close()

        qc_hi = [sb(f"qc_hi{i}", [QC, P], F32R) for i in range(2)]
        qc_lo = [sb(f"qc_lo{i}", [QC, P], F32R) for i in range(2)]
        seg_t = sb("seg_t", [P, 2])
        x2 = [sb(f"x2_{i}", [P, D]) for i in range(2)]
        st2, mv2, veps2, rstd2 = sb("st2", [P, 6]), sb("mv2", [P, 2]), sb("veps2", [P, 1]), sb("rstd2", [P, 1])
        x2n = sb("x2n", [P, D])
        xT_hi = [sb(f"xT_hi{i}", [P, DC, P], F32R) for i in range(2)]
        xT_lo = [sb(f"xT_lo{i}", [P, DC, P], F32R) for i in range(2)]
        logit, top8, need = sb("logit", [P, NE]), sb("top8", [P, NE]), sb("need", [P, 1])
        eq2, eq_cum, eq_in, gt2 = sb("eq2", [P, NE]), sb("eq_cum", [P, NE]), sb("eq_in", [P, NE]), sb("gt2", [P, NE])
        gates = [sb(f"gates{i}", [P, NE]) for i in range(2)]
        eout = [sb(f"eout{i}", [P, 2, O]) for i in range(2)]
        acc = [sb(f"acc{i}", [P, D]) for i in range(2)]

        general_mem = ExitStack()

        def gb(name, shape, dt=F32):
            return general_mem.enter_context(nc.sbuf_tensor(name, shape, dt))

        LP = KCH * P
        ctx_l = gb("ctx_l", [P, DC, LP])
        kcat_l, kT_l = gb("kcat_l", [P, KCH, P]), gb("kT_l", [P, LP])
        rope_l = gb("rope_l", [P, KCH, 2, R])
        kidx_l, mask_l, le_l = gb("kidx_l", [P, LP]), gb("mask_l", [P, LP]), gb("le_l", [P, LP])
        sc_l = gb("sc_l", [P, LP])
        kvT_l = sc_l[0:KVC, :]
        pT_l = le_l[:, :].rearrange("p (k n) -> p k n", k=KCH)
        q_l, q_h, qT_h = gb("q_l", [P, H, P]), gb("q_h", [P, P]), gb("qT_h", [P, P])
        ra_l, rb_l = gb("ra_l", [P, 8, R]), gb("rb_l", [P, 8, R])
        mx_l, sum_l, rec_l = gb("mx_l", [P, 1]), gb("sum_l", [P, 1]), gb("rec_l", [P, 1])
        o_l = gb("o_l", [P, H * KVC])
        oT_hi_l, oT_lo_l = gb("oT_hi_l", [P, PAIRS, P], F32R), gb("oT_lo_l", [P, PAIRS, P], F32R)
        general_mem.close()

        q_sb = [sb(f"q_sb{i}", [P, HG, P]) for i in range(2)]
        rope_a = [sb(f"rope_a{i}", [P, HG, R]) for i in range(2)]
        rope_b = [sb(f"rope_b{i}", [P, HG, R]) for i in range(2)]
        qT_hi = [sb(f"qT_hi{i}", [P, HG, P], F32R) for i in range(2)]
        qT_lo = [sb(f"qT_lo{i}", [P, HG, P], F32R) for i in range(2)]
        nsc = [sb(f"nsc{i}", [P, HG, P]) for i in range(2)]
        nmax = [sb(f"nmax{i}", [P, HG]) for i in range(2)]
        prob = [sb(f"prob{i}", [P, HG, P]) for i in range(2)]
        psum_h = [sb(f"psum_h{i}", [P, HG]) for i in range(2)]
        prec = [sb(f"prec{i}", [P, HG]) for i in range(2)]
        pT_hi = [sb(f"pT_hi{i}", [P, HG, P], F32R) for i in range(2)]
        pT_lo = [sb(f"pT_lo{i}", [P, HG, P], F32R) for i in range(2)]
        oT_hi = [sb(f"oT_hi{i}", [P, 2, P], F32R) for i in range(2)]
        oT_lo = [sb(f"oT_lo{i}", [P, 2, P], F32R) for i in range(2)]
        kT_hl = sb("kT_hl", [P, 2, P], F32R)
        s2m = sb("s2m", [P, HG, P])
        v_hi, v_lo = sb("v_hi", [P, 3, KVC], F32R), sb("v_lo", [P, 3, KVC], F32R)
        m_after, m_before, mask = sb("m_after", [P, P]), sb("m_before", [P, P]), sb("mask", [P, P])

        B_Q, B_E, B_QT, B_PT, _, _, B_Y, B_X = bank
        B_S = psum[:, 4 * 512:6 * 512].rearrange("p (h a n) -> p h a n", h=HG, a=2)
        B_O = B_X

        general_names = [
            "g_const", "g_rope_ld", "g_ctx_ld", "g_kvT_mm", "g_kvT_sb", "g_rows_mm", "g_rows_nope", "g_rows_parts",
            "g_rows_sb", "g_kT_mm", "g_kT_sb", "g_mask", "g_qc", "g_q_mm", "g_q_parts", "g_q_sb", "g_qh", "g_qhT_mm", "g_qhT_sb",
            "g_s_mm", "g_masked", "g_max", "g_shifted", "g_exp", "g_rec", "g_prob", "g_pT_mm", "g_pT_sb", "g_pv_mm",
            "g_o_sb", "g_oT_mm", "g_oT_hi", "g_oT_lo", "g_y_mm", "g_ln", "g_rstd", "g_x2n", "g_xT_mm", "g_xT_hi", "g_xT_lo",
            "g_gate_mm", "g_topk", "g_gates", "g_e_mm", "g_relu", "g_acc", "g_stored", "g_carried"]
        names = general_names + ["q_done", "qT_done", "s_done", "pT_done", "pv_done", "y_done", "xT_done", "gate_done", "e_done",
                 "nope_copied", "qT_hi_done", "exp_done", "pT_hi_done", "oT_hi_done", "xT_hi_done", "relu_done",
                 "rope_parts", "qT_lo_done", "score_max", "recip_done", "pT_lo_done", "oT_lo_done", "x2_done",
                 "ln_step", "x2n_done", "xT_lo_done", "gates_ready", "gate_step", "qc_split", "mask_step", "k_split",
                 "v_split", "v_zero", "k_hi_done", "qc_hi_done", "s2_masked", "waits_passed",
                 "rope_joined", "prob_normed", "rstd2_done", "acc_step", "out_stored0", "out_stored1"]
        m = {n: sem(n) for n in names}

        def at_least(eng, name, n):
            if not isinstance(n, int) or n > 0:
                eng.wait_ge(m[name], n)

        def live(i, end):
            return not isinstance(i, int) or 0 <= i < end

        main = ctx.enter_context(nc.Block())

        def walk(eng, slot):
            for k in range(-3, 2 * SLOTS):
                slot(k // SLOTS if k > 0 else 0, k % SLOTS if k > 0 else k)
            with eng.Fori(2, B - 1) as b:
                for k in range(SLOTS):
                    slot(b, k)
            for k in range(SLOTS + 9):
                slot(B - 1, k)

        def mm3(pe, out_ap, l_hi, l_lo, r_hi, r_lo, start=True, stop=True):
            pe.matmul(out_ap, l_hi, r_hi, start=start, stop=False)
            pe.matmul(out_ap, l_hi, r_lo, start=False, stop=False)
            return pe.matmul(out_ap, l_lo, r_hi, start=False, stop=stop)

        PIECES = [(512 * n, min(512, LP - 512 * n)) for n in range(4)]
        SEEN = [(at, min(n, LK - at)) for at, n in PIECES]
        CHUNKS = [(c, min(P, LK - P * c)) for c in range(KCH)]

        def carry(eng):
            eng.sem_inc(m["g_carried"], 1)

        def tiles(eng, batch_steps, tile_steps):
            with eng.Fori(0, B) as b:
                batch_steps(b)
                for j in range(TPB):
                    tile_steps(b, j, TPB * b + j)

        def no_steps(*_):
            pass

        def general_sp(sp):
            sp.dma_start(rope_l[:], rope.rearrange("(c p) (a n) -> p c a n", p=P, a=2)).then_inc(m["g_rope_ld"], 16)
            sp.wait_ge(m["g_const"], 2)

            def batch(b):
                sp.wait_ge(m["g_kT_mm"], b)
                carry(sp)
                for c in range(DC):
                    sp.dma_start(ctx_l[:, c, 0:LK], ctx_t[bass.ds(b, 1), P * c:P * c + P, :].rearrange("a p k -> p (a k)")
                                 ).then_inc(m["g_ctx_ld"], 16)

            def tile(b, j, t):
                sp.wait_ge(m["g_acc"], NE * (t + 1))
                carry(sp)
                sp.dma_start(out[bass.ds(t, 1)].rearrange("a p d -> p (a d)"), acc[0][:]).then_inc(m["g_stored"], 16)
                sp.wait_ge(m["g_stored"], 16 * (t + 1))
                carry(sp)
            tiles(sp, batch, tile)

        def general_pe(pe):
            def batch(b):
                pe.wait_ge(m["g_ctx_ld"], 32 * (b + 1))
                for n, (at, w) in enumerate(PIECES):
                    for c in range(DC):
                        mm = pe.matmul(bank[n][0:KVC, 0:w], wkvc[:, c, :], ctx_l[:, c, at:at + w], start=(c == 0), stop=(c == DC - 1))
                mm.then_inc(m["g_kvT_mm"], 1)
                pe.wait_ge(m["g_kvT_sb"], 4 * (b + 1))
                for k, _ in CHUNKS:
                    at = KVC * (k % 8)
                    for c in range(DC):
                        pe.matmul(bank[4 + k // 8][:, at:at + KVC], ctx_l[:, c, P * k:P * k + P], wkvc[:, c, :],
                                  start=(c == 0), stop=(c == DC - 1))
                    mm = pe.matmul(bank[6 + k // 8][:, at:at + R], kvT_l[:, P * k:P * k + P], wkr[:], start=True, stop=True)
                mm.then_inc(m["g_rows_mm"], 1)
                pe.wait_ge(m["g_rows_sb"], 2 * (b + 1))
                for k, _ in CHUNKS:
                    mm = pe.transpose(bank[k // 4][:, P * (k % 4):P * (k % 4) + P], kcat_l[:, k, :], ident[:])
                mm.then_inc(m["g_kT_mm"], 1)
                pe.wait_ge(m["g_kT_sb"], 4 * (b + 1))

            def tile(b, j, t):
                pe.wait_ge(m["g_qc"], 2 * (t + 1))
                for g in range(GPT):
                    hs = slice(HG * g, HG * g + HG)
                    mm = mm3(pe, bank[g][:, :], qc_hi[0][:], qc_lo[0][:], wq_hi[:, hs, :].rearrange("p h n -> p (h n)"),
                             wq_lo[:, hs, :].rearrange("p h n -> p (h n)"))
                mm.then_inc(m["g_q_mm"], 1)
                pe.wait_ge(m["g_q_sb"], GPT * (t + 1))
                carry(pe)
                with pe.Fori(0, H) as h:
                    n = H * t + h + 1
                    pe.wait_ge(m["g_qh"], n)
                    pe.transpose(bank[4][:, 0:P], q_h[:], ident[:]).then_inc(m["g_qhT_mm"], 1)
                    pe.wait_ge(m["g_qhT_sb"], n)
                    for i, (at, w) in enumerate(SEEN):
                        mm = pe.matmul(bank[i][:, 0:w], qT_h[:], kT_l[:, at:at + w], start=True, stop=True)
                    mm.then_inc(m["g_s_mm"], 1)
                    pe.wait_ge(m["g_prob"], n)
                    for k, w in CHUNKS:
                        mm = pe.transpose(bank[4 + k // 4][0:w, P * (k % 4):P * (k % 4) + P], sc_l[:, P * k:P * k + w], ident[:])
                    mm.then_inc(m["g_pT_mm"], 1)
                    pe.wait_ge(m["g_pT_sb"], KCH * n)
                    for k, w in CHUNKS:
                        mm = pe.matmul(bank[0][:, 0:KVC], pT_l[0:w, k, :], kcat_l[0:w, k, 0:KVC], start=(k == 0), stop=(k == KCH - 1))
                    mm.then_inc(m["g_pv_mm"], 1)
                pe.wait_ge(m["g_o_sb"], H * (t + 1))
                for q in range(PAIRS):
                    mm = pe.transpose(bank[4 + q // 4][:, P * (q % 4):P * (q % 4) + P], o_l[:, P * q:P * q + P], ident[:])
                mm.then_inc(m["g_oT_mm"], 1)
                pe.wait_ge(m["g_oT_lo"], 2 * (t + 1))
                for q in range(PAIRS):
                    mm = mm3(pe, B_Y[:, 0:D], oT_hi_l[:, q, :], oT_lo_l[:, q, :], wo_hi[:, q, :], wo_lo[:, q, :],
                             start=(q == 0), stop=(q == PAIRS - 1))
                mm.then_inc(m["g_y_mm"], 1)
                pe.wait_ge(m["g_x2n"], t + 1)
                for c in range(DC):
                    mm = pe.transpose(B_X[:, P * c:P * c + P], x2n[:, P * c:P * c + P], ident[:])
                mm.then_inc(m["g_xT_mm"], 1)
                pe.wait_ge(m["g_xT_lo"], t + 1)
                for c in range(DC):
                    mm = mm3(pe, B_X[:, D:D + NE], xT_hi[0][:, c, :], xT_lo[0][:, c, :], wg_hi[:, c, :], wg_lo[:, c, :],
                             start=(c == 0), stop=(c == DC - 1))
                mm.then_inc(m["g_gate_mm"], 1)
                for kc in range(GPT):
                    cols = slice(512 * kc, 512 * kc + 512)
                    pe.matmul(bank[kc][:, :], ones3[:], bias3[:, cols], start=True, stop=False)
                    for c in range(DC):
                        mm = mm3(pe, bank[kc][:, :], xT_hi[0][:, c, :], xT_lo[0][:, c, :], we_hi[:, c, cols], we_lo[:, c, cols],
                                 start=False, stop=(c == DC - 1))
                mm.then_inc(m["g_e_mm"], 1)
                pe.wait_ge(m["g_relu"], NE * (t + 1))
            tiles(pe, batch, tile)

        def general_act(act):
            def batch(b):
                act.wait_ge(m["g_kvT_mm"], b + 1)
                for n, (at, w) in enumerate(PIECES):
                    act.copy(kvT_l[:, at:at + w], bank[n][0:KVC, 0:w]).then_inc(m["g_kvT_sb"], 1)
                act.wait_ge(m["g_kT_mm"], b + 1)
                for n, (at, w) in enumerate(PIECES):
                    act.copy(kT_l[:, at:at + w], bank[n][:, 0:w]).then_inc(m["g_kT_sb"], 1)

            def tile(b, j, t):
                with act.Fori(0, H) as h:
                    n = H * t + h + 1
                    act.wait_ge(m["g_qhT_mm"], n)
                    act.copy(qT_h[:], bank[4][:, 0:P]).then_inc(m["g_qhT_sb"], 1)
                    act.wait_ge(m["g_shifted"], n)
                    act.activation(sc_l[:, 0:LK], sc_l[:, 0:LK], ACT.Exp, accum_out=sum_l[:]).then_inc(m["g_exp"], 1)
                    act.wait_ge(m["g_pT_mm"], n)
                    for k, w in CHUNKS:
                        act.copy(pT_l[0:w, k, :], bank[4 + k // 4][0:w, P * (k % 4):P * (k % 4) + P]).then_inc(m["g_pT_sb"], 1)
                act.wait_ge(m["g_oT_mm"], t + 1)
                for n in range(2):
                    act.copy(oT_hi_l[:, 4 * n:4 * n + 4, :], bank[4 + n][:, :].rearrange("p (q n) -> p q n", q=4)
                             ).then_inc(m["g_oT_hi"], 1)
                act.wait_ge(m["g_xT_mm"], t + 1)
                act.copy(xT_hi[0][:], B_X[:, 0:D].rearrange("p (c n) -> p c n", c=DC)).then_inc(m["g_xT_hi"], 1)
                act.wait_ge(m["g_gates"], t + 1)
                act.wait_ge(m["g_e_mm"], t + 1)
                for e in range(NE):
                    act.wait_ge(m["g_acc"], NE * t + e)
                    act.activation(eout[0][:, 0, :], bank[e // 2][:, O * (e % 2):O * (e % 2) + O], ACT.Relu,
                                   scale=gates[0][:, e:e + 1]).then_inc(m["g_relu"], 1)
            tiles(act, batch, tile)

        def general_pool(pool):
            pool.iota(le_l[:].bitcast(I32), [[1, LP]], base=0, channel_multiplier=0).then_inc(m["g_const"], 1)

            def tile(b, j, t):
                pool.wait_ge(m["g_ln"], 4 * (t + 1))
                pool.tensor_tensor(rstd2[:], veps2[:], half_neg[:, 0:1], ALU.pow).then_inc(m["g_rstd"], 1)
            tiles(pool, no_steps, tile)

        def general_dve(dve, carry_wait, top_two):
            for c in range(DC):
                mset = dve.memset(ctx_l[:, c, LK:LP], 0.0)
            mset.then_inc(m["g_const"], 1)
            dve.wait_ge(m["g_const"], 2)
            dve.tensor_copy(kidx_l[:], le_l[:].bitcast(I32)).then_inc(m["g_const"], 1)
            dve.wait_ge(m["g_const"], 3)
            dve.wait_ge(m["g_rope_ld"], 16)

            def rotate(out_ap, src, cos, sin, n, parts, count):
                dve.tensor_tensor(ra_l[:, 0:n, :], src, cos, ALU.mult)
                dve.tensor_tensor(rb_l[:, 0:n, :].rearrange("p h (a n) -> p h a n", a=2),
                                  src.rearrange("p h (a n) -> p h a n", a=2)[:, :, ::-1, :],
                                  sin.rearrange("p h (a n) -> p h a n", a=2), ALU.mult).then_inc(m[parts], 1)
                dve.wait_ge(m[parts], count)
                return dve.tensor_tensor(out_ap, ra_l[:, 0:n, :], rb_l[:, 0:n, :], ALU.add)

            def batch(b):
                dve.wait_ge(m["g_rows_mm"], b + 1)
                for i, n in enumerate((8, KCH - 8)):
                    ks = slice(8 * i, 8 * i + n)
                    rows = bank[4 + i][:, 0:KVC * n].rearrange("p (k n) -> p k n", k=n)
                    dve.tensor_copy(kcat_l[:, ks, 0:KVC], rows).then_inc(m["g_rows_nope"], 1)
                    rot = bank[6 + i][:, 0:R * n].rearrange("p (k n) -> p k n", k=n)
                    rotate(kcat_l[:, ks, KVC:P], rot, rope_l[:, ks, 0, :], rope_l[:, ks, 1, :], n, "g_rows_parts",
                           2 * b + i + 1).then_inc(m["g_rows_sb"], 1)
                    dve.wait_ge(m["g_rows_sb"], 2 * b + i + 1)

            def tile(b, j, t):
                dve.tensor_copy(seg_t[:], seg[:, bass.ds(t, 1), :].rearrange("p a n -> p (a n)")).then_inc(m["g_mask"], 1)
                dve.wait_ge(m["g_mask"], 4 * t + 1)
                dve.tensor_scalar(le_l[:], kidx_l[:], seg_t[:, 0:1], None, ALU.is_le).then_inc(m["g_mask"], 1)
                dve.wait_ge(m["g_mask"], 4 * t + 2)
                dve.scalar_tensor_tensor(out=mask_l[:], in0=kidx_l[:], scalar=seg_t[:, 1:2], in1=le_l[:], op0=ALU.is_ge,
                                         op1=ALU.mult).then_inc(m["g_mask"], 1)
                dve.wait_ge(m["g_mask"], 4 * t + 3)
                dve.tensor_scalar(mask_l[:], mask_l[:], -1.0, -NEG, ALU.add, ALU.mult).then_inc(m["g_mask"], 1)
                q = qc_all[:, bass.ds(P * t, P)]
                dve.tensor_copy(qc_hi[0][:], q).then_inc(m["g_qc"], 1)
                dve.wait_ge(m["g_qc"], 2 * t + 1)
                dve.tensor_tensor(qc_lo[0][:], q, qc_hi[0][:].bitcast(F32), ALU.subtract).then_inc(m["g_qc"], 1)
                dve.wait_ge(m["g_q_mm"], t + 1)
                cos = ropeq[:, j, 0:1, :].to_broadcast([P, HG, R])
                sin = ropeq[:, j, 1:2, :].to_broadcast([P, HG, R])
                for g in range(GPT):
                    hs, src = slice(HG * g, HG * g + HG), bank[g][:, :].rearrange("p (h n) -> p h n", h=HG)
                    dve.tensor_copy(q_l[:, hs, 0:KVC], src[:, :, 0:KVC])
                    rotate(q_l[:, hs, KVC:P], src[:, :, KVC:P], cos, sin, HG, "g_q_parts", GPT * t + g + 1
                           ).then_inc(m["g_q_sb"], 1)
                    dve.wait_ge(m["g_q_sb"], GPT * t + g + 1)
                carry(dve)
                with dve.Fori(0, H) as h:
                    n = H * t + h + 1
                    dve.tensor_copy(q_h[:], q_l[:, bass.ds(h, 1), :].rearrange("p a n -> p (a n)")).then_inc(m["g_qh"], 1)
                    dve.wait_ge(m["g_s_mm"], n)
                    for i, (at, w) in enumerate(SEEN):
                        e = dve.tensor_tensor(sc_l[:, at:at + w], bank[i][:, 0:w], mask_l[:, at:at + w], ALU.add)
                    e.then_inc(m["g_masked"], 1)
                    dve.wait_ge(m["g_masked"], n)
                    dve.tensor_reduce(mx_l[:], sc_l[:, 0:LK], AX.X, ALU.max).then_inc(m["g_max"], 1)
                    dve.wait_ge(m["g_max"], n)
                    dve.tensor_scalar(sc_l[:, 0:LK], sc_l[:, 0:LK], mx_l[:], SCALE, ALU.subtract, ALU.mult
                                      ).then_inc(m["g_shifted"], 1)
                    dve.wait_ge(m["g_exp"], n)
                    dve.reciprocal(rec_l[:], sum_l[:]).then_inc(m["g_rec"], 1)
                    dve.wait_ge(m["g_rec"], n)
                    dve.tensor_scalar(sc_l[:, 0:LK], sc_l[:, 0:LK], rec_l[:], None, ALU.mult).then_inc(m["g_prob"], 1)
                    dve.wait_ge(m["g_pv_mm"], n)
                    dve.tensor_copy(o_l[:, bass.ds(KVC * h, KVC)], bank[0][:, 0:KVC]).then_inc(m["g_o_sb"], 1)
                for n in range(2):
                    dve.wait_ge(m["g_oT_hi"], 2 * (t + 1))
                    dve.tensor_tensor(oT_lo_l[:, 4 * n:4 * n + 4, :], bank[4 + n][:, :].rearrange("p (q n) -> p q n", q=4),
                                      oT_hi_l[:, 4 * n:4 * n + 4, :].bitcast(F32), ALU.subtract).then_inc(m["g_oT_lo"], 1)
                dve.wait_ge(m["g_y_mm"], t + 1)
                dve.tensor_tensor(x2[0][:], B_Y[:, 0:D], x_all[:, bass.ds(t, 1), :].rearrange("p a d -> p (a d)"),
                                  ALU.add).then_inc(m["g_ln"], 1)
                dve.wait_ge(m["g_ln"], 4 * t + 1)
                dve.bn_stats(st2[:], x2[0][:]).then_inc(m["g_ln"], 1)
                dve.wait_ge(m["g_ln"], 4 * t + 2)
                carry_wait()
                dve.bn_aggr(mv2[:], st2[:]).then_inc(m["g_ln"], 1)
                dve.wait_ge(m["g_ln"], 4 * t + 3)
                dve.tensor_scalar(veps2[:], mv2[:, 1:2], EPS, None, ALU.add).then_inc(m["g_ln"], 1)
                dve.wait_ge(m["g_rstd"], t + 1)
                dve.tensor_scalar(x2n[:], x2[0][:], mv2[:, 0:1], rstd2[:], ALU.subtract, ALU.mult).then_inc(m["g_x2n"], 1)
                dve.wait_ge(m["g_xT_hi"], t + 1)
                dve.tensor_tensor(xT_lo[0][:], B_X[:, 0:D].rearrange("p (c n) -> p c n", c=DC), xT_hi[0][:].bitcast(F32),
                                  ALU.subtract).then_inc(m["g_xT_lo"], 1)
                dve.wait_ge(m["g_gate_mm"], t + 1)
                top_two("g_topk", 6 * t)
                dve.tensor_scalar(gates[0][:], gt2[:], 0.5, None, ALU.mult).then_inc(m["g_gates"], 1)
                for e in range(NE):
                    dve.wait_ge(m["g_relu"], NE * t + e + 1)
                    if e == 0:
                        dve.wait_ge(m["g_stored"], 16 * t)
                    else:
                        dve.wait_ge(m["g_acc"], NE * t + e)
                    dve.tensor_tensor(acc[0][:], x2[0][:] if e == 0 else acc[0][:], eout[0][:, 0, :], ALU.add
                                      ).then_inc(m["g_acc"], 1)
            tiles(dve, batch, tile)

        @main.tensor
        def _(pe):
            def slot(b, k):
                i, g, t = SLOTS * b + k, k % GPT, TPB * b + k // GPT
                r = k % 2
                if live(i + 1, GROUPS):
                    g1, j1 = (k + 1) % GPT, ((k + 1) // GPT) % 2
                    if g1 == 0:
                        at_least(pe, "qc_split", TPB * b + (k + 1) // GPT + 1)
                    at_least(pe, "nope_copied", i + 1)
                    at_least(pe, "rope_parts", i + 1)
                    hs = slice(HG * g1, HG * g1 + HG)
                    mm3(pe, B_Q[:, :], qc_hi[j1][:], qc_lo[j1][:], wq_hi[:, hs, :].rearrange("p h n -> p (h n)"),
                        wq_lo[:, hs, :].rearrange("p h n -> p (h n)")).then_inc(m["q_done"], 1)
                if live(i, GROUPS):
                    if k % SLOTS == 0:
                        at_least(pe, "k_split", b + k // SLOTS + 1)
                    at_least(pe, "qT_hi_done", i + 1)
                    at_least(pe, "qT_lo_done", i + 1)
                    at_least(pe, "score_max", i)
                    for h in range(HG):
                        pe.matmul(B_S[:, h, :, :], qT_hi[r][:, h, :], kT_hl[:], start=True, stop=False)
                        mm = pe.matmul(B_S[:, h, 0, :], qT_lo[r][:, h, :], kT_hl[:, 0, :], start=False, stop=True)
                    mm.then_inc(m["s_done"], 1)
                if live(i - 1, GROUPS):
                    at_least(pe, "prob_normed", i)
                    at_least(pe, "pT_hi_done", i - 1)
                    at_least(pe, "pT_lo_done", i - 1)
                    for h in range(HG):
                        mm = pe.transpose(B_PT[:, P * h:P * h + P], prob[1 - r][:, h, :], ident[:])
                    mm.then_inc(m["pT_done"], 1)
                if live(i - 2, GROUPS):
                    gp = (k - 2) % GPT
                    at_least(pe, "oT_hi_done", i - 1)
                    at_least(pe, "oT_lo_done", i - 1)
                    if gp == 0:
                        at_least(pe, "x2_done", TPB * b + (k - 2) // GPT)
                    for q in range(2):
                        mm = mm3(pe, B_Y[:, 0:D], oT_hi[r][:, q, :], oT_lo[r][:, q, :], wo_hi[:, 2 * gp + q, :],
                                 wo_lo[:, 2 * gp + q, :], start=(gp == 0 and q == 0), stop=(gp == GPT - 1 and q == 1))
                    mm.then_inc(m["y_done"], 1)
                if g == 0 and live(t - 2, TILES):
                    j = (k // GPT - 2) % 2
                    at_least(pe, "xT_hi_done", t - 1)
                    at_least(pe, "xT_lo_done", t - 1)
                    for c in range(DC):
                        mm = mm3(pe, B_X[:, D:D + NE], xT_hi[j][:, c, :], xT_lo[j][:, c, :], wg_hi[:, c, :], wg_lo[:, c, :],
                                 start=(c == 0), stop=(c == DC - 1))
                    mm.then_inc(m["gate_done"], 1)
                if live(i + 1, GROUPS):
                    at_least(pe, "rope_joined", i + 2)
                    at_least(pe, "nope_copied", i + 2)
                    at_least(pe, "qT_hi_done", i + 1)
                    at_least(pe, "qT_lo_done", i + 1)
                    for h in range(HG):
                        mm = pe.transpose(B_QT[:, P * h:P * h + P], q_sb[1 - r][:, h, :], ident[:])
                    mm.then_inc(m["qT_done"], 1)
                if g == 3 and live(t - 1, TILES):
                    at_least(pe, "x2n_done", t)
                    last = i - 1 if not isinstance(i, int) else min(i - 1, GROUPS)
                    at_least(pe, "oT_hi_done", last)
                    at_least(pe, "oT_lo_done", last)
                    for c in range(DC):
                        mm = pe.transpose(B_X[:, P * c:P * c + P], x2n[:, P * c:P * c + P], ident[:])
                    mm.then_inc(m["xT_done"], 1)
                f = i - 8
                if live(f, GROUPS):
                    kc, j = (k - 8) % GPT, ((k - 8) // GPT) % 2
                    at_least(pe, "relu_done", f)
                    cols = slice(512 * kc, 512 * kc + 512)
                    pe.matmul(B_E[:, :], ones3[:], bias3[:, cols], start=True, stop=False)
                    for c in range(DC):
                        mm = mm3(pe, B_E[:, :], xT_hi[j][:, c, :], xT_lo[j][:, c, :], we_hi[:, c, cols], we_lo[:, c, cols],
                                 start=False, stop=(c == DC - 1))
                    mm.then_inc(m["e_done"], 1)
                if live(i - 1, GROUPS):
                    if (k - 1) % SLOTS == 0:
                        at_least(pe, "v_split", b + (k - 1) // SLOTS + 1)
                    at_least(pe, "pT_hi_done", i)
                    at_least(pe, "pT_lo_done", i)
                    at_least(pe, "oT_hi_done", i - 1)
                    at_least(pe, "oT_lo_done", i - 1)
                    if g == 3 and live(t - 1, TILES):
                        at_least(pe, "xT_lo_done", t)
                    if g == 0 and live(t - 2, TILES):
                        at_least(pe, "gate_step", 6 * (t - 2) + 1)
                    q1 = 1 - r
                    o = B_O[:, 0:D]
                    for odd in range(2):
                        w = slice(KVC - KVC * odd, P + KVC - KVC * odd)
                        vh = v_hi[:].rearrange("p a n -> p (a n)")[:, w]
                        vl = v_lo[:].rearrange("p a n -> p (a n)")[:, w]
                        mm = mm3(pe, o, vh, vl, pT_hi[q1][:, odd::2, :], pT_lo[q1][:, odd::2, :],
                                 start=(odd == 0), stop=(odd == 1))
                    mm.then_inc(m["pv_done"], 1)

            near = pe.value_load(flag[0:1, 0:1], min_val=0, max_val=1)
            with pe.If(near == 1):
                walk(pe, slot)
            with pe.Else():
                general_pe(pe)

        @main.scalar
        def _(act):
            def slot(b, k):
                i, g, t = SLOTS * b + k, k % GPT, TPB * b + k // GPT
                r = k % 2
                if live(i + 1, GROUPS):
                    at_least(act, "rope_parts", i + 2)
                    at_least(act, "qT_done", i)
                    act.copy(q_sb[1 - r][:, :, 0:KVC],
                             B_Q[:, :].rearrange("p (h n) -> p h n", h=HG)[:, :, 0:KVC]).then_inc(m["nope_copied"], 1)
                if live(i - 1, GROUPS):
                    at_least(act, "pT_done", i)
                    at_least(act, "pv_done", i - 2)
                    act.copy(pT_hi[1 - r][:], B_PT[:, :].rearrange("p (h n) -> p h n", h=HG)).then_inc(m["pT_hi_done"], 1)
                if live(i + 1, GROUPS):
                    at_least(act, "qT_done", i + 2)
                    at_least(act, "s_done", i)
                    act.copy(qT_hi[1 - r][:], B_QT[:, :].rearrange("p (h n) -> p h n", h=HG)).then_inc(m["qT_hi_done"], 1)
                if g == 3 and live(t - 1, TILES):
                    j = (k // GPT - 1) % 2
                    at_least(act, "xT_done", t)
                    at_least(act, "e_done", GPT * (t - 2))
                    act.copy(xT_hi[j][:], B_X[:, 0:D].rearrange("p (c n) -> p c n", c=DC)).then_inc(m["xT_hi_done"], 1)
                if live(i, GROUPS):
                    at_least(act, "score_max", i + 1)
                    at_least(act, "pT_done", i - 1)
                    at_least(act, "recip_done", i - 1)
                    for h in range(HG):
                        e = act.activation(prob[r][:, h, :], nsc[r][:, h, :], ACT.Exp, bias=nmax[r][:, h:h + 1], scale=-1.0,
                                           accum_out=psum_h[r][:, h:h + 1])
                    e.then_inc(m["exp_done"], 1)
                if live(i - 1, GROUPS):
                    at_least(act, "pv_done", i)
                    at_least(act, "y_done", i - 2)
                    act.copy(oT_hi[1 - r][:], B_O[:, 0:D].rearrange("p (q n) -> p q n", q=2)).then_inc(m["oT_hi_done"], 1)
                f = i - 8
                if live(f, GROUPS):
                    kc, tile = (k - 8) % GPT, TPB * b + (k - 8) // GPT
                    j = ((k - 8) // GPT) % 2
                    at_least(act, "e_done", f + 1)
                    if kc == 0:
                        at_least(act, "gates_ready", tile + 1)
                    at_least(act, "acc_step", 2 * (f - 1))
                    for e in range(2):
                        a = act.activation(eout[r][:, e, :], B_E[:, O * e:O * e + O], ACT.Relu,
                                           scale=gates[j][:, 2 * kc + e:2 * kc + e + 1])
                    a.then_inc(m["relu_done"], 1)

            near = act.value_load(flag[0:1, 0:1], min_val=0, max_val=1)
            with act.If(near == 1):
                walk(act, slot)
            with act.Else():
                general_act(act)

        @main.gpsimd
        def _(pool):
            def slot(b, k):
                i, g, t = SLOTS * b + k, k % GPT, TPB * b + k // GPT
                r = k % 2
                if live(i + 1, GROUPS):
                    at_least(pool, "rope_parts", i + 2)
                    at_least(pool, "qT_done", i)
                    pool.tensor_tensor(q_sb[1 - r][:, :, KVC:P], rope_a[1 - r][:], rope_b[1 - r][:],
                                       ALU.add).then_inc(m["rope_joined"], 1)
                f = i - 9
                if live(f, GROUPS):
                    kc, j = (k - 9) % GPT, ((k - 9) // GPT) % 2
                    at_least(pool, "relu_done", f + 1)
                    if kc == 0:
                        at_least(pool, f"out_stored{j}", 16 * (b + (k - 9) // SLOTS))
                    else:
                        at_least(pool, "acc_step", 2 * f)
                    pool.tensor_tensor(acc[j][:], x2[j][:] if kc == 0 else acc[j][:], eout[1 - r][:, 0, :],
                                       ALU.add).then_inc(m["acc_step"], 1)
                    at_least(pool, "acc_step", 2 * f + 1)
                    pool.tensor_tensor(acc[j][:], acc[j][:], eout[1 - r][:, 1, :], ALU.add).then_inc(m["acc_step"], 1)
                if g == 2 and live(t - 1, TILES):
                    at_least(pool, "ln_step", 3 * t)
                    at_least(pool, "x2n_done", t - 1)
                    pool.tensor_tensor(rstd2[:], veps2[:], half_neg[:, 0:1], ALU.pow).then_inc(m["rstd2_done"], 1)
                tq = TPB * b + k // GPT + 1
                if g == 1 and live(tq, TILES):
                    pool.tensor_copy(seg_t[:], seg[:, bass.ds(tq, 1), :].rearrange("p a n -> p (a n)")).then_inc(m["mask_step"], 1)
                    at_least(pool, "mask_step", 4 * tq + 1)
                    pool.sem_inc(m["waits_passed"], 1)
                    pool.tensor_scalar(m_after[:], kidx[:], seg_t[:, 0:1], NEG, ALU.is_gt, ALU.mult).then_inc(m["mask_step"], 1)
                if g == 2 and live(tq, TILES):
                    at_least(pool, "mask_step", 4 * tq + 1)
                    pool.sem_inc(m["waits_passed"], 1)
                    pool.tensor_scalar(m_before[:], kidx[:], seg_t[:, 1:2], NEG, ALU.is_lt, ALU.mult).then_inc(m["mask_step"], 1)
                if g == 3 and live(tq, TILES):
                    at_least(pool, "mask_step", 4 * tq + 3)
                    at_least(pool, "s2_masked", i + 1)
                    pool.tensor_tensor(mask[:], m_before[:], m_after[:], ALU.add).then_inc(m["mask_step"], 1)
                if live(i, GROUPS):
                    at_least(pool, "recip_done", i + 1)
                    p = prob[r]
                    pool.tensor_tensor(p[:], p[:], prec[r][:, :].unsqueeze(2).to_broadcast([P, HG, P]),
                                       ALU.mult).then_inc(m["prob_normed"], 1)

            near = pool.value_load(flag[0:1, 0:1], min_val=0, max_val=1)
            with pool.If(near == 1):
                walk(pool, slot)
            with pool.Else():
                general_pool(pool)

        @main.vector
        def _(dve):
            dve.memset(v_hi[:].bitcast(F32), 0.0).then_inc(m["v_zero"], 1)
            dve.memset(v_lo[:].bitcast(F32), 0.0).then_inc(m["v_zero"], 1)
            dve.wait_ge(m["v_zero"], 2)

            def carry_wait():
                dve.sem_inc(m["waits_passed"], 1)

            def top_two(step_sem, n, steps=range(7)):
                for step in steps:
                    if step > 0:
                        dve.wait_ge(m[step_sem], n + step)
                    if step == 0:
                        dve.tensor_tensor(logit[:], B_X[:, D:D + NE], gate_bias[:], ALU.add).then_inc(m[step_sem], 1)
                    elif step == 1:
                        carry_wait()
                        dve.max(top8[:], logit[:]).then_inc(m[step_sem], 1)
                    elif step == 2:
                        dve.tensor_scalar(need[:], top8[:, 0:1], top8[:, 1:2], 1.0, ALU.is_equal, ALU.add)
                        dve.tensor_scalar(gt2[:], logit[:], top8[:, 1:2], None, ALU.is_gt)
                        dve.tensor_scalar(eq2[:], logit[:], top8[:, 1:2], None, ALU.is_equal).then_inc(m[step_sem], 1)
                    elif step == 3:
                        dve.tensor_tensor_scan(eq_cum[:], ones8[:], eq2[:], 0.0, ALU.mult, ALU.add).then_inc(m[step_sem], 1)
                    elif step == 4:
                        dve.scalar_tensor_tensor(out=eq_in[:], in0=eq_cum[:], scalar=need[:], in1=eq2[:],
                                                 op0=ALU.is_le, op1=ALU.mult).then_inc(m[step_sem], 1)
                    elif step == 5:
                        dve.tensor_tensor(gt2[:], gt2[:], eq_in[:], ALU.add).then_inc(m[step_sem], 1)

            def slot(b, k):
                i, g, t = SLOTS * b + k, k % GPT, TPB * b + k // GPT
                r = k % 2
                bv = b + (k - 1) // SLOTS
                if live(i - 2, GROUPS):
                    at_least(dve, "oT_hi_done", i - 1)
                    at_least(dve, "y_done", i - 3)
                    dve.tensor_tensor(oT_lo[r][:], B_O[:, 0:D].rearrange("p (q n) -> p q n", q=2),
                                      oT_hi[r][:].bitcast(F32), ALU.subtract).then_inc(m["oT_lo_done"], 1)
                if live(i + 1, GROUPS):
                    j1 = ((k + 1) // GPT) % 2
                    at_least(dve, "q_done", i + 2)
                    at_least(dve, "rope_joined", i)
                    a = B_Q[:, :].rearrange("p (h n) -> p h n", h=HG)[:, :, KVC:P]
                    cos = ropeq[:, j1, 0:1, :].to_broadcast([P, HG, R])
                    sin = ropeq[:, j1, 1:2, :].to_broadcast([P, HG, R]).rearrange("p h (a n) -> p h a n", a=2)
                    dve.tensor_tensor(rope_a[1 - r][:], a, cos, ALU.mult)
                    dve.tensor_tensor(rope_b[1 - r][:].rearrange("p h (a n) -> p h a n", a=2),
                                      a.rearrange("p h (a n) -> p h a n", a=2)[:, :, ::-1, :], sin,
                                      ALU.mult).then_inc(m["rope_parts"], 1)
                if (k - 1) % SLOTS == 0 and live(bv, B):
                    at_least(dve, "pv_done", SLOTS * bv)
                    kv = kcat[:, bass.ds(bv, 1), 0:KVC]
                    dve.tensor_copy(v_hi[:, 1:2, :], kv).then_inc(m["v_zero"], 1)
                    dve.wait_ge(m["v_zero"], bv + 3)
                    dve.tensor_tensor(v_lo[:, 1:2, :], kv, v_hi[:, 1:2, :].bitcast(F32), ALU.subtract).then_inc(m["v_split"], 1)
                if live(i, GROUPS):
                    at_least(dve, "s_done", i + 1)
                    if g == 0:
                        at_least(dve, "mask_step", 4 * (t + 1))
                    dve.tensor_tensor(s2m[:], B_S[:, :, 1, :], mask[:, :].unsqueeze(1).to_broadcast([P, HG, P]),
                                      ALU.add).then_inc(m["s2_masked"], 1)
                if live(i, GROUPS):
                    at_least(dve, "s2_masked", i + 1)
                    at_least(dve, "exp_done", i - 1)
                    carry_wait()
                    for h in range(HG):
                        e = dve.tensor_tensor_reduce(nsc[r][:, h, :], B_S[:, h, 0, :], s2m[:, h, :], -SCALE, BIG,
                                                     ALU.add, ALU.min, nmax[r][:, h:h + 1])
                    e.then_inc(m["score_max"], 1)
                if g == 1 and live(t - 1, TILES):
                    j = (k // GPT - 1) % 2
                    at_least(dve, "y_done", GPT * t)
                    at_least(dve, "acc_step", 2 * GPT * (t - 3) + 1)
                    dve.tensor_tensor(x2[j][:], B_Y[:, 0:D], x_all[:, bass.ds(t - 1, 1), :].rearrange("p a d -> p (a d)"),
                                      ALU.add).then_inc(m["x2_done"], 1)
                if g == 0 and live(t - 2, TILES):
                    at_least(dve, "gate_done", t - 1)
                    top_two("gate_step", 6 * (t - 2), [0])
                if live(i - 1, GROUPS):
                    at_least(dve, "pT_hi_done", i)
                    at_least(dve, "pv_done", i - 2)
                    dve.tensor_tensor(pT_lo[1 - r][:], B_PT[:, :].rearrange("p (h n) -> p h n", h=HG),
                                      pT_hi[1 - r][:].bitcast(F32), ALU.subtract).then_inc(m["pT_lo_done"], 1)
                if g == 0 and live(t - 2, TILES):
                    top_two("gate_step", 6 * (t - 2), [1])
                if g == 1 and live(t - 1, TILES):
                    dve.wait_ge(m["x2_done"], t)
                    dve.bn_stats(st2[:], x2[j][:]).then_inc(m["ln_step"], 1)
                if g == 3 and live(t - 1, TILES):
                    j = (k // GPT - 1) % 2
                    at_least(dve, "xT_hi_done", t)
                    at_least(dve, "e_done", GPT * (t - 2))
                    dve.tensor_tensor(xT_lo[j][:], B_X[:, 0:D].rearrange("p (c n) -> p c n", c=DC), xT_hi[j][:].bitcast(F32),
                                      ALU.subtract).then_inc(m["xT_lo_done"], 1)
                if live(i + 1, GROUPS):
                    at_least(dve, "qT_hi_done", i + 2)
                    at_least(dve, "s_done", i)
                    dve.tensor_tensor(qT_lo[1 - r][:], B_QT[:, :].rearrange("p (h n) -> p h n", h=HG), qT_hi[1 - r][:].bitcast(F32),
                                      ALU.subtract).then_inc(m["qT_lo_done"], 1)
                if g == 0 and live(t - 2, TILES):
                    top_two("gate_step", 6 * (t - 2), [2])
                if g == 1 and live(t - 1, TILES):
                    dve.wait_ge(m["ln_step"], 3 * t - 2)
                    at_least(dve, "x2n_done", t - 1)
                    carry_wait()
                    dve.bn_aggr(mv2[:], st2[:]).then_inc(m["ln_step"], 1)
                if g == 0 and live(t - 2, TILES):
                    top_two("gate_step", 6 * (t - 2), [3, 4])
                bk = b + (k + 1) // SLOTS
                if (k + 1) % SLOTS == 0 and live(bk, B):
                    at_least(dve, "s_done", SLOTS * bk)
                    kk = kT_all[:, bass.ds(bk, 1), :].rearrange("p a n -> p (a n)")
                    dve.tensor_copy(kT_hl[:, 0, :], kk).then_inc(m["k_hi_done"], 1)
                    dve.wait_ge(m["k_hi_done"], bk + 1)
                    dve.tensor_tensor(kT_hl[:, 1, :], kk, kT_hl[:, 0, :].bitcast(F32), ALU.subtract).then_inc(m["k_split"], 1)
                tq = TPB * b + k // GPT + 1
                if g == 2 and live(tq, TILES):
                    jq = (k // GPT + 1) % 2
                    at_least(dve, "q_done", GPT * (tq - 1))
                    q = qc_all[:, bass.ds(P * tq, P)]
                    dve.tensor_copy(qc_hi[jq][:], q).then_inc(m["qc_hi_done"], 1)
                    dve.wait_ge(m["qc_hi_done"], tq + 1)
                    dve.tensor_tensor(qc_lo[jq][:], q, qc_hi[jq][:].bitcast(F32), ALU.subtract).then_inc(m["qc_split"], 1)
                if g == 1 and live(t - 1, TILES):
                    dve.wait_ge(m["ln_step"], 3 * t - 1)
                    dve.tensor_scalar(veps2[:], mv2[:, 1:2], EPS, None, ALU.add).then_inc(m["ln_step"], 1)
                if live(i, GROUPS):
                    at_least(dve, "exp_done", i + 1)
                    at_least(dve, "prob_normed", i - 1)
                    dve.reciprocal(prec[r][:], psum_h[r][:]).then_inc(m["recip_done"], 1)
                if g == 0 and live(t - 2, TILES):
                    j = (k // GPT - 2) % 2
                    top_two("gate_step", 6 * (t - 2), [5, 6])
                    at_least(dve, "relu_done", GPT * (t - 3))
                    dve.tensor_scalar(gates[j][:], gt2[:], 0.5, None, ALU.mult).then_inc(m["gates_ready"], 1)
                if g == 2 and live(t - 1, TILES):
                    j = (k // GPT - 1) % 2
                    at_least(dve, "rstd2_done", t)
                    at_least(dve, "xT_done", t - 1)
                    dve.tensor_scalar(x2n[:], x2[j][:], mv2[:, 0:1], rstd2[:], ALU.subtract, ALU.mult).then_inc(m["x2n_done"], 1)

            near = dve.value_load(flag[0:1, 0:1], min_val=0, max_val=1)
            with dve.If(near == 1):
                walk(dve, slot)
            with dve.Else():
                general_dve(dve, carry_wait, top_two)

        @main.sync
        def _(sp):
            near = sp.value_load(flag[0:1, 0:1], min_val=0, max_val=1)
            with sp.If(near == 1):
                with sp.Fori(0, B) as b:
                    for j in range(TPB):
                        sp.wait_ge(m["acc_step"], 2 * GPT * (TPB * b + j) + 2 * GPT)
                        sp.dma_start(out[bass.ds(TPB * b + j, 1)].rearrange("a p d -> p (a d)"),
                                     acc[j][:]).then_inc(m[f"out_stored{j}"], 16)
                for j in range(TPB):
                    sp.wait_ge(m[f"out_stored{j}"], 16 * B)
            with sp.Else():
                general_sp(sp)


_INS = ["x", "ctx_t", "itok", "w_kvc", "w_dq", "w_uq_t", "w_qr", "w_uk_t", "w_kr", "w_uv_t", "w_o",
        "gate_w", "gate_b", "expert_w", "expert_b", "rope"]


def rope_table():
    half = R // 2
    inv_freq = (1.0 / np.power(np.float32(10000.0), np.arange(half, dtype=np.float32) / np.float32(half))).astype(np.float32)
    ang = (np.arange(KCH * P, dtype=np.float32)[:, None] * inv_freq).astype(np.float64)
    cos, sin = np.cos(ang).astype(np.float32), np.sin(ang).astype(np.float32)
    return np.ascontiguousarray(np.concatenate([cos, cos, -sin, sin], axis=1))


def kernel(x, ctx_2048, itok_BxS_0_1023, L0_xattn_W_kvc, L0_xattn_W_dq, L0_xattn_W_uq, L0_xattn_W_qr, L0_xattn_W_uk,
           L0_xattn_W_kr, L0_xattn_W_uv, L0_xattn_W_o, L0_ffn_gate_w, L0_ffn_gate_b, L0_ffn_expert_w, L0_ffn_expert_b):
    import concourse.bacc as bacc
    from concourse.bass_utils import run_bass_kernel_spmd

    arrays = {
        "x": np.asarray(x).reshape(TILES, P, D),
        "ctx_t": np.asarray(ctx_2048).transpose(0, 2, 1),
        "itok": np.asarray(itok_BxS_0_1023).reshape(TILES, P).T,
        "w_kvc": L0_xattn_W_kvc, "w_dq": L0_xattn_W_dq, "w_uq_t": np.asarray(L0_xattn_W_uq).T, "w_qr": L0_xattn_W_qr,
        "w_uk_t": np.asarray(L0_xattn_W_uk).T, "w_kr": L0_xattn_W_kr, "w_uv_t": np.asarray(L0_xattn_W_uv).T,
        "w_o": L0_xattn_W_o, "gate_w": L0_ffn_gate_w, "gate_b": L0_ffn_gate_b, "expert_w": L0_ffn_expert_w,
        "expert_b": L0_ffn_expert_b, "rope": rope_table(),
    }
    nc = bacc.Bacc("TRN2", target_bir_lowering=False, num_devices=1)
    arrays = {n: np.ascontiguousarray(arrays[n]) for n in _INS}
    args = [nc.dram_tensor(f"in_{n}", a.shape, mybir.dt.from_np(a.dtype), kind="ExternalInput").ap()
            for n, a in arrays.items()]
    out = nc.dram_tensor("out", (TILES, P, D), F32, kind="ExternalOutput").ap()
    kernel_program(nc, *args, out)
    r = run_bass_kernel_spmd(nc, [{f"in_{n}": a for n, a in arrays.items()}], core_ids=[0])
    return r.results[0]["out"].reshape(B, L, D)
```

```python
from contextlib import ExitStack

import numpy as np

import concourse.bass as bass
from concourse import mybir

F32 = mybir.dt.float32
F32R = mybir.dt.float32r
BF16 = mybir.dt.bfloat16
I32 = mybir.dt.int32
ALU = mybir.AluOpType
ACT = mybir.ActivationFunctionType
AX = mybir.AxisListType

P = 128
B, L, D = 8, 256, 256
LK = 1601
H, HD = 16, 128
KVC, QC, R = 64, 96, 64
LOOKBACK = 8
NE, O = 8, 256
EPS = 1e-5
NEG = -1e30
SCALE = float(np.float32(1.0) / np.sqrt(HD + R).astype(np.float32))
DC = D // P
TPB = L // P
TILES = B * TPB
HG = 4
GPT = H // HG
GROUPS = TILES * GPT
SLOTS = TPB * GPT
PAIRS = H // 2
KCH = -(-LK // P)
BIG = 3e38


def kernel_program(nc, x, ctx_t, itok, w_kvc, w_dq, w_uq_t, w_qr, w_uk_t, w_kr, w_uv_t, w_o,
                   gate_w, gate_b, expert_w, expert_b, rope, w_kvc_t, out):
    with ExitStack() as ctx:
        def sb(name, shape, dt=F32):
            return ctx.enter_context(nc.sbuf_tensor(name, shape, dt))

        def sem(name):
            return ctx.enter_context(nc.semaphore(name))

        psum = ctx.enter_context(nc.psum_tensor("psum", [P, 8 * 512], F32))
        bank = [psum[:, 512 * i:512 * i + 512] for i in range(8)]

        x_all = sb("x_all", [P, TILES, D])
        qc_all = sb("qc_all", [QC, B * L])
        wq_hi, wq_lo = sb("wq_hi", [QC, H, P], F32R), sb("wq_lo", [QC, H, P], F32R)
        wo_hi, wo_lo = sb("wo_hi", [P, PAIRS, D], F32R), sb("wo_lo", [P, PAIRS, D], F32R)
        we_hi, we_lo = sb("we_hi", [P, DC, NE * O], F32R), sb("we_lo", [P, DC, NE * O], F32R)
        wg = sb("wg", [P, DC, NE])
        wg_hi, wg_lo = sb("wg_hi", [P, DC, NE], F32R), sb("wg_lo", [P, DC, NE], F32R)
        gate_bias = sb("gate_bias", [P, NE])
        bias3 = sb("bias3", [3, NE * O], BF16)
        ones3 = sb("ones3", [3, P], BF16)
        ident = sb("ident", [P, P])
        kidx = sb("kidx", [P, P])
        ropeq = sb("ropeq", [P, TPB, 2, R])
        wcat = sb("wcat", [P, DC, P])
        wkvc = wcat[:, :, 0:KVC]
        wkr = sb("wkr", [KVC, R])
        kcat = sb("kcat", [P, B, P])
        kT_all = sb("kT_all", [P, B, P])
        seg_i = sb("seg_i", [P, TILES], I32)
        seg = sb("seg", [P, TILES, 2])
        half_neg = sb("half_neg", [P, TILES])
        ones8 = sb("ones8", [P, NE])
        flag = sb("flag", [1, 1], I32)

        v_hi, v_lo = sb("v_hi", [P, 3, KVC], F32R), sb("v_lo", [P, 3, KVC], F32R)

        block_sems = {}

        def S(name):
            if name not in block_sems:
                block_sems[name] = sem(name)
            return block_sems[name]

        qc_hi = [sb(f"qc_hi{i}", [QC, P], F32R) for i in range(2)]
        qc_lo = [sb(f"qc_lo{i}", [QC, P], F32R) for i in range(2)]
        seg_t = sb("seg_t", [P, 2])
        x2 = [sb(f"x2_{i}", [P, D]) for i in range(2)]
        st2, mv2, veps2, rstd2 = sb("st2", [P, 6]), sb("mv2", [P, 2]), sb("veps2", [P, 1]), sb("rstd2", [P, 1])
        x2n = sb("x2n", [P, D])
        xT_hi = [sb(f"xT_hi{i}", [P, DC, P], F32R) for i in range(2)]
        xT_lo = [sb(f"xT_lo{i}", [P, DC, P], F32R) for i in range(2)]
        logit, top8, need = sb("logit", [P, NE]), sb("top8", [P, NE]), sb("need", [P, 1])
        eq2, eq_cum, eq_in, gt2 = sb("eq2", [P, NE]), sb("eq_cum", [P, NE]), sb("eq_in", [P, NE]), sb("gt2", [P, NE])
        gates = [sb(f"gates{i}", [P, NE]) for i in range(2)]
        eout = [sb(f"eout{i}", [P, 2, O]) for i in range(2)]
        acc = [sb(f"acc{i}", [P, D]) for i in range(2)]
        prep_only = ExitStack()

        def tmp(name, shape, dt=F32):
            return prep_only.enter_context(nc.sbuf_tensor(name, shape, dt))

        ctxT = tmp("ctxT", [P, DC, B, P])
        wkvcT = tmp("wkvcT", [KVC, D])
        wdq = tmp("wdq", [P, DC, QC])
        wuqT = tmp("wuqT", [P, H, QC])
        wukT = tmp("wukT", [P, H, KVC])
        wqr = tmp("wqr", [QC, H, R])
        ropek = tmp("ropek", [P, 2, R])
        ka, kb = tmp("ka", [P, B // 2, R]), tmp("kb", [P, B // 2, R])
        xn = [tmp(f"xn{i}", [P, 4, D]) for i in range(2)]
        xnT = [tmp(f"xnT{i}", [P, DC, 4 * P]) for i in range(2)]
        st_all = tmp("st_all", [P, TILES, 6])
        mv_all = tmp("mv_all", [P, TILES, 2])
        veps_all = tmp("veps_all", [P, TILES])
        rstd_all = tmp("rstd_all", [P, TILES])
        eb = tmp("eb", [16, P])
        eb_r = tmp("eb_r", [16, 2, P])
        eb3 = tmp("eb3", [16, 3, P], BF16)
        in_lo, in_both = tmp("in_lo", [P, TILES]), tmp("in_both", [P, TILES])
        row_ok = tmp("row_ok", [P, 1])
        ones_col = tmp("ones_col", [P, 1])
        table_probe = tmp("table_probe", [P, 1])
        kidx_i = tmp("kidx_i", [P, P], I32)
        wuvT = tmp("wuvT", [P, H, KVC])
        wo_raw = tmp("wo_raw", [P, H, D])
        we_raw = tmp("we_raw", [P, DC, NE * O])

        prep = prep_only.enter_context(nc.Block())

        @prep.sync
        def _(sp):
            def load_x(i):
                sp.dma_start(x_all[:, 4 * i:4 * i + 4, :], x[4 * i:4 * i + 4].rearrange("t p d -> p t d")
                             ).then_inc(S(f"ld_x{i}"), 16)
            load_x(0)
            for c in range(DC):
                sp.dma_start(ctxT[:, c, :, :], ctx_t[P * c:P * c + P, :, 0:P]).then_inc(S("ld_ctx"), 16)
            load_x(1)
            sp.dma_start(wukT[:], w_uk_t.rearrange("(h p) n -> p h n", p=P)).then_inc(S("ld_wuq"), 16)
            load_x(2)
            sp.dma_start(ropeq[:], rope[0:L, :].rearrange("(t p) (a n) -> p t a n", p=P, a=2)).then_inc(S("ld_ropeq"), 16)
            load_x(3)
            sp.dma_start(wuvT[:], w_uv_t.rearrange("(h p) n -> p h n", p=P)).then_inc(S("ld_wuv"), 16)
            sp.dma_start(wo_raw[:, 0:H // 2, :], w_o[0:H // 2 * HD, :].rearrange("(h p) n -> p h n", p=P)).then_inc(S("ld_wo0"), 16)
            sp.dma_start(wo_raw[:, H // 2:H, :], w_o[H // 2 * HD:H * HD, :].rearrange("(h p) n -> p h n", p=P)).then_inc(S("ld_wo1"), 16)
            sp.dma_start(we_raw[:], expert_w.rearrange("(c p) n -> p c n", p=P)).then_inc(S("ld_we"), 16)
            sp.wait_ge(S("eb_step"), 5)
            for r in range(3):
                sp.dma_start(bias3[r:r + 1, :], eb3[:, r, :]).then_inc(S("ld_bias3"), 16)

        @prep.scalar
        def _(act):
            act.dma_start(wkvcT[:], w_kvc_t).then_inc(S("ld_kv"), 16)
            act.dma_start(wkr[:], w_kr).then_inc(S("ld_kv"), 16)
            act.dma_start(wkvc, w_kvc.rearrange("(c p) n -> p c n", p=P)).then_inc(S("ld_kv"), 16)
            act.dma_start(wdq[:], w_dq.rearrange("(c p) n -> p c n", p=P)).then_inc(S("ld_wdq"), 16)
            act.dma_start(wuqT[:], w_uq_t.rearrange("(h p) n -> p h n", p=P)).then_inc(S("ld_wuq"), 16)
            act.dma_start(wqr[:], w_qr.rearrange("c (h r) -> c h r", r=R)).then_inc(S("ld_wqr"), 16)
            act.wait_ge(S("ones_set"), 3)
            act.copy(table_probe[:], ones_col[:]).then_inc(S("table_loaded"), 1)

            def copy_xT(i):
                act.wait_ge(S("xT_mm"), i + 1)
                if i > 1:
                    act.wait_ge(S("qc_mm"), i - 1)
                for c in range(DC):
                    act.copy(xnT[i % 2][:, c, :], bank[6 + c]).then_inc(S("xT_sb"), 1)

            def copy_qc(i):
                act.wait_ge(S("qc_mm"), i + 1)
                act.copy(qc_all[:, 512 * i:512 * i + 512], bank[2 + i % 2][0:QC, :]).then_inc(S("qc_sb"), 1)

            copy_xT(0)
            copy_xT(1)
            copy_qc(0)
            act.wait_ge(S("fold_q_mm"), 1)
            for i in range(2):
                act.copy(wq_hi[:, 8 * i:8 * i + 8, 0:KVC],
                         bank[4 + i][0:QC, :].rearrange("p (h n) -> p h n", h=8)).then_inc(S("wq_hi_done"), 1)
            copy_xT(2)
            copy_qc(1)
            act.wait_ge(S("kT_mm"), 1)
            for i in range(2):
                act.copy(kT_all[:, 4 * i:4 * i + 4, :],
                         bank[i].rearrange("p (b k) -> p b k", b=4)).then_inc(S("kT_sb"), 1)
            act.wait_ge(S("ld_wqr"), 16)
            act.copy(wq_hi[:, :, KVC:P], wqr[:]).then_inc(S("wq_hi_done"), 1)
            copy_xT(3)
            copy_qc(2)
            copy_qc(3)

        @prep.gpsimd
        def _(pool):
            pool.memset(half_neg[:], -0.5).then_inc(S("half_set"), 1)
            pool.memset(ident[:], 0.0).then_inc(S("ident_zero"), 1)
            pool.iota(kidx_i[:], [[1, P]], base=0, channel_multiplier=0).then_inc(S("iota_done"), 1)
            pool.wait_ge(S("ident_zero"), 1)
            pool.affine_select(out=ident[:], in_=ident[:], compare_op=ALU.not_equal, fill=1.0, base=0,
                               pattern=[[-1, P]], channel_multiplier=1).then_inc(S("ident_done"), 1)
            pool.memset(ones_col[:], 1.0).then_inc(S("ones_set"), 1)
            pool.memset(ones3[:], 1.0).then_inc(S("ones_set"), 1)
            pool.memset(ones8[:], 1.0).then_inc(S("ones_set"), 1)
            pool.memset(v_hi[:].bitcast(F32), 0.0).then_inc(S("v_zero"), 1)
            pool.memset(v_lo[:].bitcast(F32), 0.0).then_inc(S("v_zero"), 1)
            pool.dma_start(ropek[:], rope[0:P, :].rearrange("p (a n) -> p a n", a=2)).then_inc(S("ld_rope"), 16)
            pool.dma_start(seg_i[:], itok).then_inc(S("ld_seg"), 16)
            pool.dma_start(wg[:], gate_w.rearrange("(c p) n -> p c n", p=P)).then_inc(S("ld_eb_wg"), 16)
            pool.wait_ge(S("half_set"), 1)
            for i in range(4):
                pool.wait_ge(S("veps_done"), i + 1)
                t = slice(4 * i, 4 * i + 4)
                pool.tensor_tensor(rstd_all[:, t], veps_all[:, t], half_neg[:, t], ALU.pow).then_inc(S("rstd_done"), 1)
                if i == 0:
                    pool.dma_start(eb[:], expert_b.rearrange("e (a n) -> (e a) n", n=P)).then_inc(S("ld_eb_wg"), 16)
                    pool.dma_start(gate_bias[:], gate_b.partition_broadcast(P)).then_inc(S("ld_gate_bias"), 16)
            pool.wait_ge(S("wq_hi_done"), 3)
            pool.tensor_tensor(wq_lo[:, :, KVC:P], wqr[:], wq_hi[:, :, KVC:P].bitcast(F32), ALU.subtract).then_inc(S("wq_lo_done"), 1)

        @prep.vector
        def _(dve):
            def norm_stats(i):
                dve.wait_ge(S(f"ld_x{i}"), 16)
                for t in range(4 * i, 4 * i + 4):
                    dve.bn_stats(st_all[:, t, :], x_all[:, t, :]).then_inc(S("st_done"), 1)
                dve.wait_ge(S("st_done"), 4 * i + 4)
                for t in range(4 * i, 4 * i + 4):
                    dve.bn_aggr(mv_all[:, t, :], st_all[:, t, :]).then_inc(S("mv_done"), 1)
                dve.wait_ge(S("mv_done"), 4 * i + 4)
                dve.tensor_scalar(veps_all[:, 4 * i:4 * i + 4], mv_all[:, 4 * i:4 * i + 4, 1], EPS, None,
                                  ALU.add).then_inc(S("veps_done"), 1)

            def norm_apply(i):
                dve.wait_ge(S("rstd_done"), i + 1)
                if i > 1:
                    dve.wait_ge(S("xT_mm"), i - 1)
                for t in range(4 * i, 4 * i + 4):
                    dve.tensor_scalar(xn[i % 2][:, t % 4, :], x_all[:, t, :], mv_all[:, t, 0:1], rstd_all[:, t:t + 1],
                                      ALU.subtract, ALU.mult).then_inc(S("xn_done"), 1)

            norm_stats(0)
            norm_apply(0)
            norm_stats(1)
            dve.wait_ge(S("wkk_mm"), 1)
            dve.tensor_copy(wcat[:, :, KVC:P], bank[4][:, 0:DC * R].rearrange("p (c n) -> p c n", c=DC)).then_inc(S("wkk_sb"), 1)
            dve.wait_ge(S("ld_seg"), 16)
            dve.tensor_copy(seg[:, :, 0], seg_i[:]).then_inc(S("seg_f"), 1)
            dve.wait_ge(S("seg_f"), 1)
            dve.tensor_scalar(seg[:, :, 1], seg[:, :, 0], float(-LOOKBACK), None, ALU.add).then_inc(S("seg_f"), 1)
            dve.tensor_scalar(in_lo[:], seg[:, :, 0], 0.0, None, ALU.is_ge).then_inc(S("seg_f"), 1)
            dve.wait_ge(S("seg_f"), 3)
            dve.scalar_tensor_tensor(out=in_both[:], in0=seg[:, :, 0], scalar=float(P - 1), in1=in_lo[:],
                                     op0=ALU.is_le, op1=ALU.mult).then_inc(S("seg_f"), 1)
            dve.wait_ge(S("seg_f"), 4)
            dve.tensor_reduce(row_ok[:], in_both[:], AX.X, ALU.min).then_inc(S("row_ok_done"), 1)
            dve.wait_ge(S("iota_done"), 1)
            dve.tensor_copy(kidx[:], kidx_i[:]).then_inc(S("kidx_done"), 1)
            norm_apply(1)
            dve.wait_ge(S("ld_rope"), 16)
            for i in range(2):
                dve.wait_ge(S("k_mm"), i + 1)
                bs = slice(4 * i, 4 * i + 4)
                rows = bank[i].rearrange("p (b n) -> p b n", b=4)
                dve.tensor_copy(kcat[:, bs, 0:KVC], rows[:, :, 0:KVC]).then_inc(S("kcat_done"), 1)
                kr = rows[:, :, KVC:P]
                cos = ropek[:, 0:1, :].to_broadcast([P, 4, R])
                sin = ropek[:, 1:2, :].to_broadcast([P, 4, R]).rearrange("p b (a n) -> p b a n", a=2)
                if i > 0:
                    dve.wait_ge(S("kcat_done"), 2)
                dve.tensor_tensor(ka[:], kr, cos, ALU.mult).then_inc(S("kparts"), 1)
                dve.tensor_tensor(kb[:].rearrange("p b (a n) -> p b a n", a=2),
                                  kr.rearrange("p b (a n) -> p b a n", a=2)[:, :, ::-1, :], sin, ALU.mult
                                  ).then_inc(S("kparts"), 1)
                dve.wait_ge(S("kparts"), 2 * i + 2)
                dve.tensor_tensor(kcat[:, bs, KVC:P], ka[:], kb[:], ALU.add).then_inc(S("kcat_done"), 1)
            dve.wait_ge(S("ok_mm"), 1)
            dve.tensor_scalar(flag[:], bank[5][0:1, 0:1], float(P), None, ALU.is_ge).then_inc(S("flag_done"), 1)
            norm_stats(2)
            norm_apply(2)
            norm_stats(3)
            for i in range(2):
                dve.wait_ge(S("wq_hi_done"), i + 1)
                dve.tensor_tensor(wq_lo[:, 8 * i:8 * i + 8, 0:KVC],
                                  bank[4 + i][0:QC, :].rearrange("p (h n) -> p h n", h=8),
                                  wq_hi[:, 8 * i:8 * i + 8, 0:KVC].bitcast(F32), ALU.subtract).then_inc(S("wq_lo_done"), 1)
            dve.wait_ge(S("ld_eb_wg"), 32)
            dve.tensor_copy(wg_hi[:], wg[:]).then_inc(S("wg_done"), 1)
            dve.tensor_copy(eb3[:, 0, :], eb[:]).then_inc(S("eb_step"), 1)
            dve.wait_ge(S("wg_done"), 1)
            dve.tensor_tensor(wg_lo[:], wg[:], wg_hi[:].bitcast(F32), ALU.subtract).then_inc(S("wg_done"), 1)
            for r in range(2):
                dve.wait_ge(S("eb_step"), 2 * r + 1)
                src = eb[:] if r == 0 else eb_r[:, 0, :]
                dve.tensor_tensor(eb_r[:, r, :], src, eb3[:, r, :], ALU.subtract).then_inc(S("eb_step"), 1)
                dve.wait_ge(S("eb_step"), 2 * r + 2)
                dve.tensor_copy(eb3[:, r + 1, :], eb_r[:, r, :]).then_inc(S("eb_step"), 1)
            norm_apply(3)

        @prep.tensor
        def _(pe):
            pe.wait_ge(S("ident_done"), 1)

            def xT(i):
                pe.wait_ge(S("xn_done"), 4 * i + 4)
                if i > 0:
                    pe.wait_ge(S("xT_sb"), DC * i)
                for t in range(4):
                    for c in range(DC):
                        mm = pe.transpose(bank[6 + c][:, P * t:P * t + P], xn[i % 2][:, t, P * c:P * c + P], ident[:])
                mm.then_inc(S("xT_mm"), 1)

            def q_latent(i):
                pe.wait_ge(S("xT_sb"), DC * (i + 1))
                if i > 1:
                    pe.wait_ge(S("qc_sb"), i - 1)
                for c in range(DC):
                    mm = pe.matmul(bank[2 + i % 2][0:QC, :], wdq[:, c, :], xnT[i % 2][:, c, :], start=(c == 0), stop=(c == DC - 1))
                mm.then_inc(S("qc_mm"), 1)

            pe.wait_ge(S("ld_kv"), 48)
            for c in range(DC):
                mm = pe.matmul(bank[4][:, R * c:R * c + R], wkvcT[:, P * c:P * c + P], wkr[:], start=True, stop=True)
            mm.then_inc(S("wkk_mm"), 1)
            xT(0)
            pe.wait_ge(S("ld_ctx"), 16 * DC)
            pe.wait_ge(S("wkk_sb"), 1)
            for b in range(B):
                for c in range(DC):
                    mm = pe.matmul(bank[b // 4][:, P * (b % 4):P * (b % 4) + P], ctxT[:, c, b, :], wcat[:, c, :],
                                   start=(c == 0), stop=(c == DC - 1))
                if b % 4 == 3:
                    mm.then_inc(S("k_mm"), 1)
            pe.wait_ge(S("row_ok_done"), 1)
            pe.wait_ge(S("ones_set"), 3)
            pe.matmul(bank[5][0:1, 0:1], row_ok[:], ones_col[:], start=True, stop=True).then_inc(S("ok_mm"), 1)
            xT(1)
            pe.wait_ge(S("ld_wdq"), 16)
            q_latent(0)
            pe.wait_ge(S("ld_wuq"), 32)
            pe.wait_ge(S("wkk_sb"), 1)
            pe.wait_ge(S("flag_done"), 1)
            for h in range(H):
                mm = pe.matmul(bank[4 + h // 8][0:QC, KVC * (h % 8):KVC * (h % 8) + KVC], wuqT[:, h, :], wukT[:, h, :],
                               start=True, stop=True)
            mm.then_inc(S("fold_q_mm"), 1)
            xT(2)
            q_latent(1)
            pe.wait_ge(S("kcat_done"), 4)
            for b in range(B):
                mm = pe.transpose(bank[b // 4][:, P * (b % 4):P * (b % 4) + P], kcat[:, b, :], ident[:])
            mm.then_inc(S("kT_mm"), 1)
            xT(3)
            q_latent(2)
            q_latent(3)

        prep_only.close()

        general_mem = ExitStack()

        def gb(name, shape, dt=F32):
            return general_mem.enter_context(nc.sbuf_tensor(name, shape, dt))

        LP = KCH * P
        ctx_l = gb("ctx_l", [P, DC, LP])
        kcat_l, kT_l = gb("kcat_l", [P, KCH, P]), gb("kT_l", [P, LP])
        rope_l = gb("rope_l", [P, KCH, 2, R])
        kidx_l, mask_l, le_l = gb("kidx_l", [P, LP]), gb("mask_l", [P, LP]), gb("le_l", [P, LP])
        sc_l = gb("sc_l", [P, LP])
        kvT_l = sc_l[0:KVC, :]
        pT_l = le_l[:, :].rearrange("p (k n) -> p k n", k=KCH)
        q_l, q_h, qT_h = gb("q_l", [P, H, P]), gb("q_h", [P, P]), gb("qT_h", [P, P])
        ra_l, rb_l = gb("ra_l", [P, 8, R]), gb("rb_l", [P, 8, R])
        mx_l, sum_l, rec_l = gb("mx_l", [P, 1]), gb("sum_l", [P, 1]), gb("rec_l", [P, 1])
        o_l = gb("o_l", [P, H * KVC])
        oT_hi_l, oT_lo_l = gb("oT_hi_l", [P, PAIRS, P], F32R), gb("oT_lo_l", [P, PAIRS, P], F32R)
        general_mem.close()

        q_sb = [sb(f"q_sb{i}", [P, HG, P]) for i in range(2)]
        rope_a = [sb(f"rope_a{i}", [P, HG, R]) for i in range(2)]
        rope_b = [sb(f"rope_b{i}", [P, HG, R]) for i in range(2)]
        qT_hi = [sb(f"qT_hi{i}", [P, HG, P], F32R) for i in range(2)]
        qT_lo = [sb(f"qT_lo{i}", [P, HG, P], F32R) for i in range(2)]
        nsc = [sb(f"nsc{i}", [P, HG, P]) for i in range(2)]
        nmax = [sb(f"nmax{i}", [P, HG]) for i in range(2)]
        prob = [sb(f"prob{i}", [P, HG, P]) for i in range(2)]
        psum_h = [sb(f"psum_h{i}", [P, HG]) for i in range(2)]
        prec = [sb(f"prec{i}", [P, HG]) for i in range(2)]
        pT_hi = [sb(f"pT_hi{i}", [P, HG, P], F32R) for i in range(2)]
        pT_lo = [sb(f"pT_lo{i}", [P, HG, P], F32R) for i in range(2)]
        oT_hi = [sb(f"oT_hi{i}", [P, 2, P], F32R) for i in range(2)]
        oT_lo = [sb(f"oT_lo{i}", [P, 2, P], F32R) for i in range(2)]
        kT_hl = sb("kT_hl", [P, 2, P], F32R)
        s2m = sb("s2m", [P, HG, P])
        m_after, m_before, mask = sb("m_after", [P, P]), sb("m_before", [P, P]), sb("mask", [P, P])

        B_Q, B_E, B_QT, B_PT, _, _, B_Y, B_X = bank
        B_S = psum[:, 4 * 512:6 * 512].rearrange("p (h a n) -> p h a n", h=HG, a=2)
        B_O = B_X

        general_names = [
            "g_const", "g_rope_ld", "g_ctx_ld", "g_kvT_mm", "g_kvT_sb", "g_rows_mm", "g_rows_nope", "g_rows_parts",
            "g_rows_sb", "g_kT_mm", "g_kT_sb", "g_mask", "g_qc", "g_q_mm", "g_q_parts", "g_q_sb", "g_qh", "g_qhT_mm", "g_qhT_sb",
            "g_s_mm", "g_masked", "g_max", "g_shifted", "g_exp", "g_rec", "g_prob", "g_pT_mm", "g_pT_sb", "g_pv_mm",
            "g_o_sb", "g_oT_mm", "g_oT_hi", "g_oT_lo", "g_y_mm", "g_ln", "g_rstd", "g_x2n", "g_xT_mm", "g_xT_hi", "g_xT_lo",
            "g_gate_mm", "g_topk", "g_gates", "g_e_mm", "g_relu", "g_acc", "g_stored", "g_carried"]
        names = general_names + ["q_done", "qT_done", "s_done", "pT_done", "pv_done", "y_done", "xT_done", "gate_done", "e_done",
                 "nope_copied", "qT_hi_done", "exp_done", "pT_hi_done", "oT_hi_done", "xT_hi_done", "relu_done",
                 "rope_parts", "qT_lo_done", "score_max", "recip_done", "pT_lo_done", "oT_lo_done", "x2_done",
                 "ln_step", "x2n_done", "xT_lo_done", "gates_ready", "gate_step", "qc_split", "mask_step", "k_split",
                 "v_split", "v_hi_done", "wo_hi_done", "wo_lo_done", "fold_o_mm", "we_hi_done", "we_lo_done", "k_hi_done", "qc_hi_done", "s2_masked", "waits_passed",
                 "rope_joined", "prob_normed", "rstd2_done", "acc_step", "out_stored0", "out_stored1"]
        m = {n: sem(n) for n in names}

        def at_least(eng, name, n):
            if not isinstance(n, int) or n > 0:
                eng.wait_ge(m[name], n)

        def live(i, end):
            return not isinstance(i, int) or 0 <= i < end

        fold_bank = [B_E, B_Y]

        def fold_o(pe, n):
            pe.wait_ge(S("ld_wuv"), 16)
            pe.wait_ge(S(f"ld_wo{n // 2}"), 16)
            if n > 1:
                pe.wait_ge(m["wo_lo_done"], n - 1)
            for q in range(2):
                for odd in range(2):
                    h = 4 * n + 2 * q + odd
                    mm = pe.matmul(fold_bank[n % 2][64 * odd:64 * odd + 64, D * q:D * q + D], wuvT[:, h, :], wo_raw[:, h, :],
                                   start=True, stop=True)
            mm.then_inc(m["fold_o_mm"], 1)

        def wo_high(act, n):
            act.wait_ge(m["fold_o_mm"], n + 1)
            act.copy(wo_hi[:, 2 * n:2 * n + 2, :], fold_bank[n % 2].rearrange("p (q n) -> p q n", q=2)).then_inc(m["wo_hi_done"], 1)

        def wo_low(dve, n):
            dve.wait_ge(m["wo_hi_done"], n + 1)
            dve.tensor_tensor(wo_lo[:, 2 * n:2 * n + 2, :], fold_bank[n % 2].rearrange("p (q n) -> p q n", q=2),
                              wo_hi[:, 2 * n:2 * n + 2, :].bitcast(F32), ALU.subtract).then_inc(m["wo_lo_done"], 1)

        def expert_piece(n):
            return n % DC, slice(512 * (n // DC), 512 * (n // DC) + 512)

        def we_high(act, n):
            c, cols = expert_piece(n)
            if n == 0:
                act.wait_ge(S("ld_we"), 16)
            act.copy(we_hi[:, c, cols], we_raw[:, c, cols]).then_inc(m["we_hi_done"], 1)

        def we_low(pool, n):
            c, cols = expert_piece(n)
            pool.wait_ge(m["we_hi_done"], n + 1)
            pool.tensor_tensor(we_lo[:, c, cols], we_raw[:, c, cols], we_hi[:, c, cols].bitcast(F32), ALU.subtract
                               ).then_inc(m["we_lo_done"], 1)

        FOLD_SLOTS = (-3, -1)
        FOLDS, EXPERT_PIECES = PAIRS // 2, DC * NE // 2

        def piece_of(i, count):
            return isinstance(i, int) and 0 <= i < count

        main = ctx.enter_context(nc.Block())

        def expert_bank(f):
            return B_Q if isinstance(f, int) and f > GROUPS - 8 and f % 2 else B_E

        def walk(eng, slot):
            for k in range(-3, 2 * SLOTS):
                slot(k // SLOTS if k > 0 else 0, k % SLOTS if k > 0 else k)
            with eng.Fori(2, B - 1) as b:
                for k in range(SLOTS):
                    slot(b, k)
            for k in range(SLOTS + 9):
                slot(B - 1, k)

        def mm3(pe, out_ap, l_hi, l_lo, r_hi, r_lo, start=True, stop=True):
            pe.matmul(out_ap, l_hi, r_hi, start=start, stop=False)
            pe.matmul(out_ap, l_hi, r_lo, start=False, stop=False)
            return pe.matmul(out_ap, l_lo, r_hi, start=False, stop=stop)

        PIECES = [(512 * n, min(512, LP - 512 * n)) for n in range(4)]
        SEEN = [(at, min(n, LK - at)) for at, n in PIECES]
        CHUNKS = [(c, min(P, LK - P * c)) for c in range(KCH)]

        def carry(eng):
            eng.sem_inc(m["g_carried"], 1)

        def tiles(eng, batch_steps, tile_steps):
            with eng.Fori(0, B) as b:
                batch_steps(b)
                for j in range(TPB):
                    tile_steps(b, j, TPB * b + j)

        def no_steps(*_):
            pass

        def general_sp(sp):
            sp.wait_ge(m["fold_o_mm"], FOLDS)
            sp.wait_ge(m["we_lo_done"], EXPERT_PIECES)
            sp.dma_start(rope_l[:], rope.rearrange("(c p) (a n) -> p c a n", p=P, a=2)).then_inc(m["g_rope_ld"], 16)
            sp.wait_ge(m["g_const"], 2)

            def batch(b):
                sp.wait_ge(m["g_kT_mm"], b)
                carry(sp)
                for c in range(DC):
                    sp.dma_start(ctx_l[:, c, 0:LK], ctx_t[P * c:P * c + P, bass.ds(b, 1), :].rearrange("p a k -> p (a k)")
                                 ).then_inc(m["g_ctx_ld"], 16)

            def tile(b, j, t):
                sp.wait_ge(m["g_acc"], NE * (t + 1))
                carry(sp)
                sp.dma_start(out[bass.ds(t, 1)].rearrange("a p d -> p (a d)"), acc[0][:]).then_inc(m["g_stored"], 16)
                sp.wait_ge(m["g_stored"], 16 * (t + 1))
                carry(sp)
            tiles(sp, batch, tile)

        def general_pe(pe):
            for n in range(FOLDS):
                fold_o(pe, n)
            pe.wait_ge(m["wo_lo_done"], FOLDS)
            pe.wait_ge(m["we_lo_done"], EXPERT_PIECES)
            pe.wait_ge(S("ld_bias3"), 48)

            def batch(b):
                pe.wait_ge(m["g_ctx_ld"], 32 * (b + 1))
                for n, (at, w) in enumerate(PIECES):
                    for c in range(DC):
                        mm = pe.matmul(bank[n][0:KVC, 0:w], wkvc[:, c, :], ctx_l[:, c, at:at + w], start=(c == 0), stop=(c == DC - 1))
                mm.then_inc(m["g_kvT_mm"], 1)
                pe.wait_ge(m["g_kvT_sb"], 4 * (b + 1))
                for k, _ in CHUNKS:
                    at = KVC * (k % 8)
                    for c in range(DC):
                        pe.matmul(bank[4 + k // 8][:, at:at + KVC], ctx_l[:, c, P * k:P * k + P], wkvc[:, c, :],
                                  start=(c == 0), stop=(c == DC - 1))
                    mm = pe.matmul(bank[6 + k // 8][:, at:at + R], kvT_l[:, P * k:P * k + P], wkr[:], start=True, stop=True)
                mm.then_inc(m["g_rows_mm"], 1)
                pe.wait_ge(m["g_rows_sb"], 2 * (b + 1))
                for k, _ in CHUNKS:
                    mm = pe.transpose(bank[k // 4][:, P * (k % 4):P * (k % 4) + P], kcat_l[:, k, :], ident[:])
                mm.then_inc(m["g_kT_mm"], 1)
                pe.wait_ge(m["g_kT_sb"], 4 * (b + 1))

            def tile(b, j, t):
                pe.wait_ge(m["g_qc"], 2 * (t + 1))
                for g in range(GPT):
                    hs = slice(HG * g, HG * g + HG)
                    mm = mm3(pe, bank[g][:, :], qc_hi[0][:], qc_lo[0][:], wq_hi[:, hs, :].rearrange("p h n -> p (h n)"),
                             wq_lo[:, hs, :].rearrange("p h n -> p (h n)"))
                mm.then_inc(m["g_q_mm"], 1)
                pe.wait_ge(m["g_q_sb"], GPT * (t + 1))
                carry(pe)
                with pe.Fori(0, H) as h:
                    n = H * t + h + 1
                    pe.wait_ge(m["g_qh"], n)
                    pe.transpose(bank[4][:, 0:P], q_h[:], ident[:]).then_inc(m["g_qhT_mm"], 1)
                    pe.wait_ge(m["g_qhT_sb"], n)
                    for i, (at, w) in enumerate(SEEN):
                        mm = pe.matmul(bank[i][:, 0:w], qT_h[:], kT_l[:, at:at + w], start=True, stop=True)
                    mm.then_inc(m["g_s_mm"], 1)
                    pe.wait_ge(m["g_prob"], n)
                    for k, w in CHUNKS:
                        mm = pe.transpose(bank[4 + k // 4][0:w, P * (k % 4):P * (k % 4) + P], sc_l[:, P * k:P * k + w], ident[:])
                    mm.then_inc(m["g_pT_mm"], 1)
                    pe.wait_ge(m["g_pT_sb"], KCH * n)
                    for k, w in CHUNKS:
                        mm = pe.matmul(bank[0][:, 0:KVC], pT_l[0:w, k, :], kcat_l[0:w, k, 0:KVC], start=(k == 0), stop=(k == KCH - 1))
                    mm.then_inc(m["g_pv_mm"], 1)
                pe.wait_ge(m["g_o_sb"], H * (t + 1))
                for q in range(PAIRS):
                    mm = pe.transpose(bank[4 + q // 4][:, P * (q % 4):P * (q % 4) + P], o_l[:, P * q:P * q + P], ident[:])
                mm.then_inc(m["g_oT_mm"], 1)
                pe.wait_ge(m["g_oT_lo"], 2 * (t + 1))
                for q in range(PAIRS):
                    mm = mm3(pe, B_Y[:, 0:D], oT_hi_l[:, q, :], oT_lo_l[:, q, :], wo_hi[:, q, :], wo_lo[:, q, :],
                             start=(q == 0), stop=(q == PAIRS - 1))
                mm.then_inc(m["g_y_mm"], 1)
                pe.wait_ge(m["g_x2n"], t + 1)
                for c in range(DC):
                    mm = pe.transpose(B_X[:, P * c:P * c + P], x2n[:, P * c:P * c + P], ident[:])
                mm.then_inc(m["g_xT_mm"], 1)
                pe.wait_ge(m["g_xT_lo"], t + 1)
                for c in range(DC):
                    mm = mm3(pe, B_X[:, D:D + NE], xT_hi[0][:, c, :], xT_lo[0][:, c, :], wg_hi[:, c, :], wg_lo[:, c, :],
                             start=(c == 0), stop=(c == DC - 1))
                mm.then_inc(m["g_gate_mm"], 1)
                for kc in range(GPT):
                    cols = slice(512 * kc, 512 * kc + 512)
                    pe.matmul(bank[kc][:, :], ones3[:], bias3[:, cols], start=True, stop=False)
                    for c in range(DC):
                        mm = mm3(pe, bank[kc][:, :], xT_hi[0][:, c, :], xT_lo[0][:, c, :], we_hi[:, c, cols], we_lo[:, c, cols],
                                 start=False, stop=(c == DC - 1))
                mm.then_inc(m["g_e_mm"], 1)
                pe.wait_ge(m["g_relu"], NE * (t + 1))
            tiles(pe, batch, tile)

        def general_act(act):
            for n in range(FOLDS):
                wo_high(act, n)
            for n in range(EXPERT_PIECES):
                we_high(act, n)

            def batch(b):
                act.wait_ge(m["g_kvT_mm"], b + 1)
                for n, (at, w) in enumerate(PIECES):
                    act.copy(kvT_l[:, at:at + w], bank[n][0:KVC, 0:w]).then_inc(m["g_kvT_sb"], 1)
                act.wait_ge(m["g_kT_mm"], b + 1)
                for n, (at, w) in enumerate(PIECES):
                    act.copy(kT_l[:, at:at + w], bank[n][:, 0:w]).then_inc(m["g_kT_sb"], 1)

            def tile(b, j, t):
                with act.Fori(0, H) as h:
                    n = H * t + h + 1
                    act.wait_ge(m["g_qhT_mm"], n)
                    act.copy(qT_h[:], bank[4][:, 0:P]).then_inc(m["g_qhT_sb"], 1)
                    act.wait_ge(m["g_shifted"], n)
                    act.activation(sc_l[:, 0:LK], sc_l[:, 0:LK], ACT.Exp, accum_out=sum_l[:]).then_inc(m["g_exp"], 1)
                    act.wait_ge(m["g_pT_mm"], n)
                    for k, w in CHUNKS:
                        act.copy(pT_l[0:w, k, :], bank[4 + k // 4][0:w, P * (k % 4):P * (k % 4) + P]).then_inc(m["g_pT_sb"], 1)
                act.wait_ge(m["g_oT_mm"], t + 1)
                for n in range(2):
                    act.copy(oT_hi_l[:, 4 * n:4 * n + 4, :], bank[4 + n][:, :].rearrange("p (q n) -> p q n", q=4)
                             ).then_inc(m["g_oT_hi"], 1)
                act.wait_ge(m["g_xT_mm"], t + 1)
                act.copy(xT_hi[0][:], B_X[:, 0:D].rearrange("p (c n) -> p c n", c=DC)).then_inc(m["g_xT_hi"], 1)
                act.wait_ge(m["g_gates"], t + 1)
                act.wait_ge(m["g_e_mm"], t + 1)
                for e in range(NE):
                    act.wait_ge(m["g_acc"], NE * t + e)
                    act.activation(eout[0][:, 0, :], bank[e // 2][:, O * (e % 2):O * (e % 2) + O], ACT.Relu,
                                   scale=gates[0][:, e:e + 1]).then_inc(m["g_relu"], 1)
            tiles(act, batch, tile)

        def general_pool(pool):
            for n in range(EXPERT_PIECES):
                we_low(pool, n)
            pool.wait_ge(m["fold_o_mm"], FOLDS)
            pool.wait_ge(m["we_lo_done"], EXPERT_PIECES)
            pool.iota(le_l[:].bitcast(I32), [[1, LP]], base=0, channel_multiplier=0).then_inc(m["g_const"], 1)

            def tile(b, j, t):
                pool.wait_ge(m["g_ln"], 4 * (t + 1))
                pool.tensor_tensor(rstd2[:], veps2[:], half_neg[:, 0:1], ALU.pow).then_inc(m["g_rstd"], 1)
            tiles(pool, no_steps, tile)

        def general_dve(dve, carry_wait, top_two):
            for n in range(FOLDS):
                wo_low(dve, n)
            dve.wait_ge(m["fold_o_mm"], FOLDS)
            dve.wait_ge(m["we_lo_done"], EXPERT_PIECES)
            for c in range(DC):
                mset = dve.memset(ctx_l[:, c, LK:LP], 0.0)
            mset.then_inc(m["g_const"], 1)
            dve.wait_ge(m["g_const"], 2)
            dve.tensor_copy(kidx_l[:], le_l[:].bitcast(I32)).then_inc(m["g_const"], 1)
            dve.wait_ge(m["g_const"], 3)
            dve.wait_ge(m["g_rope_ld"], 16)

            def rotate(out_ap, src, cos, sin, n, parts, count):
                dve.tensor_tensor(ra_l[:, 0:n, :], src, cos, ALU.mult)
                dve.tensor_tensor(rb_l[:, 0:n, :].rearrange("p h (a n) -> p h a n", a=2),
                                  src.rearrange("p h (a n) -> p h a n", a=2)[:, :, ::-1, :],
                                  sin.rearrange("p h (a n) -> p h a n", a=2), ALU.mult).then_inc(m[parts], 1)
                dve.wait_ge(m[parts], count)
                return dve.tensor_tensor(out_ap, ra_l[:, 0:n, :], rb_l[:, 0:n, :], ALU.add)

            def batch(b):
                dve.wait_ge(m["g_rows_mm"], b + 1)
                for i, n in enumerate((8, KCH - 8)):
                    ks = slice(8 * i, 8 * i + n)
                    rows = bank[4 + i][:, 0:KVC * n].rearrange("p (k n) -> p k n", k=n)
                    dve.tensor_copy(kcat_l[:, ks, 0:KVC], rows).then_inc(m["g_rows_nope"], 1)
                    rot = bank[6 + i][:, 0:R * n].rearrange("p (k n) -> p k n", k=n)
                    rotate(kcat_l[:, ks, KVC:P], rot, rope_l[:, ks, 0, :], rope_l[:, ks, 1, :], n, "g_rows_parts",
                           2 * b + i + 1).then_inc(m["g_rows_sb"], 1)
                    dve.wait_ge(m["g_rows_sb"], 2 * b + i + 1)

            def tile(b, j, t):
                dve.tensor_copy(seg_t[:], seg[:, bass.ds(t, 1), :].rearrange("p a n -> p (a n)")).then_inc(m["g_mask"], 1)
                dve.wait_ge(m["g_mask"], 4 * t + 1)
                dve.tensor_scalar(le_l[:], kidx_l[:], seg_t[:, 0:1], None, ALU.is_le).then_inc(m["g_mask"], 1)
                dve.wait_ge(m["g_mask"], 4 * t + 2)
                dve.scalar_tensor_tensor(out=mask_l[:], in0=kidx_l[:], scalar=seg_t[:, 1:2], in1=le_l[:], op0=ALU.is_ge,
                                         op1=ALU.mult).then_inc(m["g_mask"], 1)
                dve.wait_ge(m["g_mask"], 4 * t + 3)
                dve.tensor_scalar(mask_l[:], mask_l[:], -1.0, -NEG, ALU.add, ALU.mult).then_inc(m["g_mask"], 1)
                q = qc_all[:, bass.ds(P * t, P)]
                dve.tensor_copy(qc_hi[0][:], q).then_inc(m["g_qc"], 1)
                dve.wait_ge(m["g_qc"], 2 * t + 1)
                dve.tensor_tensor(qc_lo[0][:], q, qc_hi[0][:].bitcast(F32), ALU.subtract).then_inc(m["g_qc"], 1)
                dve.wait_ge(m["g_q_mm"], t + 1)
                cos = ropeq[:, j, 0:1, :].to_broadcast([P, HG, R])
                sin = ropeq[:, j, 1:2, :].to_broadcast([P, HG, R])
                for g in range(GPT):
                    hs, src = slice(HG * g, HG * g + HG), bank[g][:, :].rearrange("p (h n) -> p h n", h=HG)
                    dve.tensor_copy(q_l[:, hs, 0:KVC], src[:, :, 0:KVC])
                    rotate(q_l[:, hs, KVC:P], src[:, :, KVC:P], cos, sin, HG, "g_q_parts", GPT * t + g + 1
                           ).then_inc(m["g_q_sb"], 1)
                    dve.wait_ge(m["g_q_sb"], GPT * t + g + 1)
                carry(dve)
                with dve.Fori(0, H) as h:
                    n = H * t + h + 1
                    dve.tensor_copy(q_h[:], q_l[:, bass.ds(h, 1), :].rearrange("p a n -> p (a n)")).then_inc(m["g_qh"], 1)
                    dve.wait_ge(m["g_s_mm"], n)
                    for i, (at, w) in enumerate(SEEN):
                        e = dve.tensor_tensor(sc_l[:, at:at + w], bank[i][:, 0:w], mask_l[:, at:at + w], ALU.add)
                    e.then_inc(m["g_masked"], 1)
                    dve.wait_ge(m["g_masked"], n)
                    dve.tensor_reduce(mx_l[:], sc_l[:, 0:LK], AX.X, ALU.max).then_inc(m["g_max"], 1)
                    dve.wait_ge(m["g_max"], n)
                    dve.tensor_scalar(sc_l[:, 0:LK], sc_l[:, 0:LK], mx_l[:], SCALE, ALU.subtract, ALU.mult
                                      ).then_inc(m["g_shifted"], 1)
                    dve.wait_ge(m["g_exp"], n)
                    dve.reciprocal(rec_l[:], sum_l[:]).then_inc(m["g_rec"], 1)
                    dve.wait_ge(m["g_rec"], n)
                    dve.tensor_scalar(sc_l[:, 0:LK], sc_l[:, 0:LK], rec_l[:], None, ALU.mult).then_inc(m["g_prob"], 1)
                    dve.wait_ge(m["g_pv_mm"], n)
                    dve.tensor_copy(o_l[:, bass.ds(KVC * h, KVC)], bank[0][:, 0:KVC]).then_inc(m["g_o_sb"], 1)
                for n in range(2):
                    dve.wait_ge(m["g_oT_hi"], 2 * (t + 1))
                    dve.tensor_tensor(oT_lo_l[:, 4 * n:4 * n + 4, :], bank[4 + n][:, :].rearrange("p (q n) -> p q n", q=4),
                                      oT_hi_l[:, 4 * n:4 * n + 4, :].bitcast(F32), ALU.subtract).then_inc(m["g_oT_lo"], 1)
                dve.wait_ge(m["g_y_mm"], t + 1)
                dve.tensor_tensor(x2[0][:], B_Y[:, 0:D], x_all[:, bass.ds(t, 1), :].rearrange("p a d -> p (a d)"),
                                  ALU.add).then_inc(m["g_ln"], 1)
                dve.wait_ge(m["g_ln"], 4 * t + 1)
                dve.bn_stats(st2[:], x2[0][:]).then_inc(m["g_ln"], 1)
                dve.wait_ge(m["g_ln"], 4 * t + 2)
                carry_wait()
                dve.bn_aggr(mv2[:], st2[:]).then_inc(m["g_ln"], 1)
                dve.wait_ge(m["g_ln"], 4 * t + 3)
                dve.tensor_scalar(veps2[:], mv2[:, 1:2], EPS, None, ALU.add).then_inc(m["g_ln"], 1)
                dve.wait_ge(m["g_rstd"], t + 1)
                dve.tensor_scalar(x2n[:], x2[0][:], mv2[:, 0:1], rstd2[:], ALU.subtract, ALU.mult).then_inc(m["g_x2n"], 1)
                dve.wait_ge(m["g_xT_hi"], t + 1)
                dve.tensor_tensor(xT_lo[0][:], B_X[:, 0:D].rearrange("p (c n) -> p c n", c=DC), xT_hi[0][:].bitcast(F32),
                                  ALU.subtract).then_inc(m["g_xT_lo"], 1)
                dve.wait_ge(m["g_gate_mm"], t + 1)
                top_two("g_topk", 6 * t)
                dve.tensor_scalar(gates[0][:], gt2[:], 0.5, None, ALU.mult).then_inc(m["g_gates"], 1)
                for e in range(NE):
                    dve.wait_ge(m["g_relu"], NE * t + e + 1)
                    if e == 0:
                        dve.wait_ge(m["g_stored"], 16 * t)
                    else:
                        dve.wait_ge(m["g_acc"], NE * t + e)
                    dve.tensor_tensor(acc[0][:], x2[0][:] if e == 0 else acc[0][:], eout[0][:, 0, :], ALU.add
                                      ).then_inc(m["g_acc"], 1)
            tiles(dve, batch, tile)

        @main.tensor
        def _(pe):
            def slot(b, k):
                i, g, t = SLOTS * b + k, k % GPT, TPB * b + k // GPT
                r = k % 2
                if live(i + 1, GROUPS):
                    g1, j1 = (k + 1) % GPT, ((k + 1) // GPT) % 2
                    if g1 == 0:
                        at_least(pe, "qc_split", TPB * b + (k + 1) // GPT + 1)
                    at_least(pe, "nope_copied", i + 1)
                    at_least(pe, "rope_parts", i + 1)
                    hs = slice(HG * g1, HG * g1 + HG)
                    mm3(pe, B_Q[:, :], qc_hi[j1][:], qc_lo[j1][:], wq_hi[:, hs, :].rearrange("p h n -> p (h n)"),
                        wq_lo[:, hs, :].rearrange("p h n -> p (h n)")).then_inc(m["q_done"], 1)
                if live(i, GROUPS):
                    if k % SLOTS == 0:
                        at_least(pe, "k_split", b + k // SLOTS + 1)
                    at_least(pe, "qT_hi_done", i + 1)
                    at_least(pe, "qT_lo_done", i + 1)
                    at_least(pe, "score_max", i)
                    for h in range(HG):
                        pe.matmul(B_S[:, h, :, :], qT_hi[r][:, h, :], kT_hl[:], start=True, stop=False)
                        mm = pe.matmul(B_S[:, h, 0, :], qT_lo[r][:, h, :], kT_hl[:, 0, :], start=False, stop=True)
                    mm.then_inc(m["s_done"], 1)
                if live(i - 1, GROUPS):
                    at_least(pe, "prob_normed", i)
                    at_least(pe, "pT_hi_done", i - 1)
                    at_least(pe, "pT_lo_done", i - 1)
                    for h in range(HG):
                        mm = pe.transpose(B_PT[:, P * h:P * h + P], prob[1 - r][:, h, :], ident[:])
                    mm.then_inc(m["pT_done"], 1)
                if live(i - 2, GROUPS):
                    gp = (k - 2) % GPT
                    at_least(pe, "oT_hi_done", i - 1)
                    at_least(pe, "oT_lo_done", i - 1)
                    if isinstance(i, int) and i - 2 < FOLDS:
                        pe.wait_ge(m["wo_lo_done"], FOLDS)
                    if gp == 0:
                        at_least(pe, "x2_done", TPB * b + (k - 2) // GPT)
                    for q in range(2):
                        mm = mm3(pe, B_Y[:, 0:D], oT_hi[r][:, q, :], oT_lo[r][:, q, :], wo_hi[:, 2 * gp + q, :],
                                 wo_lo[:, 2 * gp + q, :], start=(gp == 0 and q == 0), stop=(gp == GPT - 1 and q == 1))
                    mm.then_inc(m["y_done"], 1)
                if g == 0 and live(t - 2, TILES):
                    j = (k // GPT - 2) % 2
                    at_least(pe, "xT_hi_done", t - 1)
                    at_least(pe, "xT_lo_done", t - 1)
                    for c in range(DC):
                        mm = mm3(pe, B_X[:, D:D + NE], xT_hi[j][:, c, :], xT_lo[j][:, c, :], wg_hi[:, c, :], wg_lo[:, c, :],
                                 start=(c == 0), stop=(c == DC - 1))
                    mm.then_inc(m["gate_done"], 1)
                if live(i + 1, GROUPS):
                    at_least(pe, "rope_joined", i + 2)
                    at_least(pe, "nope_copied", i + 2)
                    at_least(pe, "qT_hi_done", i + 1)
                    at_least(pe, "qT_lo_done", i + 1)
                    for h in range(HG):
                        mm = pe.transpose(B_QT[:, P * h:P * h + P], q_sb[1 - r][:, h, :], ident[:])
                    mm.then_inc(m["qT_done"], 1)
                if g == 3 and live(t - 1, TILES):
                    at_least(pe, "x2n_done", t)
                    last = i - 1 if not isinstance(i, int) else min(i - 1, GROUPS)
                    at_least(pe, "oT_hi_done", last)
                    at_least(pe, "oT_lo_done", last)
                    for c in range(DC):
                        mm = pe.transpose(B_X[:, P * c:P * c + P], x2n[:, P * c:P * c + P], ident[:])
                    mm.then_inc(m["xT_done"], 1)
                if isinstance(i, int) and i in FOLD_SLOTS:
                    fold_o(pe, i + 3)
                    fold_o(pe, i + 4)
                f = i - 8
                if live(f, GROUPS):
                    kc, j = (k - 8) % GPT, ((k - 8) // GPT) % 2
                    at_least(pe, "relu_done", f - 1 if isinstance(f, int) and f > GROUPS - 8 else f)
                    if isinstance(f, int) and f < GPT:
                        pe.wait_ge(S("ld_bias3"), 48)
                        pe.wait_ge(m["we_lo_done"], DC * (f + 1))
                    cols = slice(512 * kc, 512 * kc + 512)
                    z = expert_bank(f)
                    pe.matmul(z, ones3[:], bias3[:, cols], start=True, stop=False)
                    for c in range(DC):
                        mm = mm3(pe, z, xT_hi[j][:, c, :], xT_lo[j][:, c, :], we_hi[:, c, cols], we_lo[:, c, cols],
                                 start=False, stop=(c == DC - 1))
                    mm.then_inc(m["e_done"], 1)
                if live(i - 1, GROUPS):
                    if (k - 1) % SLOTS == 0:
                        at_least(pe, "v_split", b + (k - 1) // SLOTS + 1)
                    at_least(pe, "pT_hi_done", i)
                    at_least(pe, "pT_lo_done", i)
                    at_least(pe, "oT_hi_done", i - 1)
                    at_least(pe, "oT_lo_done", i - 1)
                    if g == 3 and live(t - 1, TILES):
                        at_least(pe, "xT_lo_done", t)
                    if g == 0 and live(t - 2, TILES):
                        at_least(pe, "gate_step", 6 * (t - 2) + 1)
                    q1 = 1 - r
                    o = B_O[:, 0:D]
                    for odd in range(2):
                        w = slice(KVC - KVC * odd, P + KVC - KVC * odd)
                        vh = v_hi[:].rearrange("p a n -> p (a n)")[:, w]
                        vl = v_lo[:].rearrange("p a n -> p (a n)")[:, w]
                        mm = mm3(pe, o, vh, vl, pT_hi[q1][:, odd::2, :], pT_lo[q1][:, odd::2, :],
                                 start=(odd == 0), stop=(odd == 1))
                    mm.then_inc(m["pv_done"], 1)

            near = pe.value_load(flag[0:1, 0:1], min_val=0, max_val=1)
            with pe.If(near == 1):
                walk(pe, slot)
            with pe.Else():
                general_pe(pe)

        @main.scalar
        def _(act):
            def slot(b, k):
                i, g, t = SLOTS * b + k, k % GPT, TPB * b + k // GPT
                r = k % 2
                if isinstance(i, int) and i - 1 in FOLD_SLOTS:
                    wo_high(act, i + 2)
                    wo_high(act, i + 3)
                if live(i + 1, GROUPS):
                    at_least(act, "rope_parts", i + 2)
                    at_least(act, "qT_done", i)
                    act.copy(q_sb[1 - r][:, :, 0:KVC],
                             B_Q[:, :].rearrange("p (h n) -> p h n", h=HG)[:, :, 0:KVC]).then_inc(m["nope_copied"], 1)
                if live(i - 1, GROUPS):
                    at_least(act, "pT_done", i)
                    at_least(act, "pv_done", i - 2)
                    act.copy(pT_hi[1 - r][:], B_PT[:, :].rearrange("p (h n) -> p h n", h=HG)).then_inc(m["pT_hi_done"], 1)
                if live(i + 1, GROUPS):
                    at_least(act, "qT_done", i + 2)
                    at_least(act, "s_done", i)
                    act.copy(qT_hi[1 - r][:], B_QT[:, :].rearrange("p (h n) -> p h n", h=HG)).then_inc(m["qT_hi_done"], 1)
                if g == 3 and live(t - 1, TILES):
                    j = (k // GPT - 1) % 2
                    at_least(act, "xT_done", t)
                    at_least(act, "e_done", GPT * (t - 2))
                    act.copy(xT_hi[j][:], B_X[:, 0:D].rearrange("p (c n) -> p c n", c=DC)).then_inc(m["xT_hi_done"], 1)
                if live(i, GROUPS):
                    at_least(act, "score_max", i + 1)
                    at_least(act, "pT_done", i - 1)
                    at_least(act, "recip_done", i - 1)
                    for h in range(HG):
                        e = act.activation(prob[r][:, h, :], nsc[r][:, h, :], ACT.Exp, bias=nmax[r][:, h:h + 1], scale=-1.0,
                                           accum_out=psum_h[r][:, h:h + 1])
                    e.then_inc(m["exp_done"], 1)
                if piece_of(i, EXPERT_PIECES):
                    we_high(act, i)
                if live(i - 1, GROUPS):
                    at_least(act, "pv_done", i)
                    at_least(act, "y_done", i - 2)
                    act.copy(oT_hi[1 - r][:], B_O[:, 0:D].rearrange("p (q n) -> p q n", q=2)).then_inc(m["oT_hi_done"], 1)
                f = i - 8
                if live(f, GROUPS):
                    kc, tile = (k - 8) % GPT, TPB * b + (k - 8) // GPT
                    j = ((k - 8) // GPT) % 2
                    at_least(act, "e_done", f + 1)
                    if kc == 0:
                        at_least(act, "gates_ready", tile + 1)
                    at_least(act, "acc_step", 2 * (f - 1))
                    for e in range(2):
                        a = act.activation(eout[r][:, e, :], expert_bank(f)[:, O * e:O * e + O], ACT.Relu,
                                           scale=gates[j][:, 2 * kc + e:2 * kc + e + 1])
                    a.then_inc(m["relu_done"], 1)

            near = act.value_load(flag[0:1, 0:1], min_val=0, max_val=1)
            with act.If(near == 1):
                walk(act, slot)
            with act.Else():
                general_act(act)

        @main.gpsimd
        def _(pool):
            def slot(b, k):
                i, g, t = SLOTS * b + k, k % GPT, TPB * b + k // GPT
                r = k % 2
                if live(i + 1, GROUPS):
                    at_least(pool, "rope_parts", i + 2)
                    at_least(pool, "qT_done", i)
                    pool.tensor_tensor(q_sb[1 - r][:, :, KVC:P], rope_a[1 - r][:], rope_b[1 - r][:],
                                       ALU.add).then_inc(m["rope_joined"], 1)
                if piece_of(i - 1, EXPERT_PIECES):
                    we_low(pool, i - 1)
                def second_norm():
                    if g == 2 and live(t - 1, TILES):
                        at_least(pool, "ln_step", 3 * t)
                        at_least(pool, "x2n_done", t - 1)
                        pool.tensor_tensor(rstd2[:], veps2[:], half_neg[:, 0:1], ALU.pow).then_inc(m["rstd2_done"], 1)

                draining = isinstance(i, int) and i >= GROUPS
                if draining:
                    second_norm()
                f = i - 9
                if live(f, GROUPS):
                    kc, j = (k - 9) % GPT, ((k - 9) // GPT) % 2
                    at_least(pool, "relu_done", f + 1)
                    if kc == 0:
                        at_least(pool, f"out_stored{j}", 16 * (b + (k - 9) // SLOTS))
                    else:
                        at_least(pool, "acc_step", 2 * f)
                    pool.tensor_tensor(acc[j][:], x2[j][:] if kc == 0 else acc[j][:], eout[1 - r][:, 0, :],
                                       ALU.add).then_inc(m["acc_step"], 1)
                    at_least(pool, "acc_step", 2 * f + 1)
                    pool.tensor_tensor(acc[j][:], acc[j][:], eout[1 - r][:, 1, :], ALU.add).then_inc(m["acc_step"], 1)
                if not draining:
                    second_norm()
                tq = TPB * b + k // GPT + 1
                if g == 1 and live(tq, TILES):
                    pool.tensor_copy(seg_t[:], seg[:, bass.ds(tq, 1), :].rearrange("p a n -> p (a n)")).then_inc(m["mask_step"], 1)
                    at_least(pool, "mask_step", 4 * tq + 1)
                    pool.sem_inc(m["waits_passed"], 1)
                    pool.tensor_scalar(m_after[:], kidx[:], seg_t[:, 0:1], NEG, ALU.is_gt, ALU.mult).then_inc(m["mask_step"], 1)
                if g == 2 and live(tq, TILES):
                    at_least(pool, "mask_step", 4 * tq + 1)
                    pool.sem_inc(m["waits_passed"], 1)
                    pool.tensor_scalar(m_before[:], kidx[:], seg_t[:, 1:2], NEG, ALU.is_lt, ALU.mult).then_inc(m["mask_step"], 1)
                if g == 3 and live(tq, TILES):
                    at_least(pool, "mask_step", 4 * tq + 3)
                    at_least(pool, "s2_masked", i + 1)
                    pool.tensor_tensor(mask[:], m_before[:], m_after[:], ALU.add).then_inc(m["mask_step"], 1)
                if live(i, GROUPS):
                    at_least(pool, "recip_done", i + 1)
                    p = prob[r]
                    pool.tensor_tensor(p[:], p[:], prec[r][:, :].unsqueeze(2).to_broadcast([P, HG, P]),
                                       ALU.mult).then_inc(m["prob_normed"], 1)

            near = pool.value_load(flag[0:1, 0:1], min_val=0, max_val=1)
            with pool.If(near == 1):
                walk(pool, slot)
            with pool.Else():
                general_pool(pool)

        @main.vector
        def _(dve):
            dve.wait_ge(S("ld_ropeq"), 16)
            dve.wait_ge(S("ld_gate_bias"), 16)


            def carry_wait():
                dve.sem_inc(m["waits_passed"], 1)

            def top_two(step_sem, n, steps=range(7)):
                for step in steps:
                    if step > 0:
                        dve.wait_ge(m[step_sem], n + step)
                    if step == 0:
                        dve.tensor_tensor(logit[:], B_X[:, D:D + NE], gate_bias[:], ALU.add).then_inc(m[step_sem], 1)
                    elif step == 1:
                        carry_wait()
                        dve.max(top8[:], logit[:]).then_inc(m[step_sem], 1)
                    elif step == 2:
                        dve.tensor_scalar(need[:], top8[:, 0:1], top8[:, 1:2], 1.0, ALU.is_equal, ALU.add)
                        dve.tensor_scalar(gt2[:], logit[:], top8[:, 1:2], None, ALU.is_gt)
                        dve.tensor_scalar(eq2[:], logit[:], top8[:, 1:2], None, ALU.is_equal).then_inc(m[step_sem], 1)
                    elif step == 3:
                        dve.tensor_tensor_scan(eq_cum[:], ones8[:], eq2[:], 0.0, ALU.mult, ALU.add).then_inc(m[step_sem], 1)
                    elif step == 4:
                        dve.scalar_tensor_tensor(out=eq_in[:], in0=eq_cum[:], scalar=need[:], in1=eq2[:],
                                                 op0=ALU.is_le, op1=ALU.mult).then_inc(m[step_sem], 1)
                    elif step == 5:
                        dve.tensor_tensor(gt2[:], gt2[:], eq_in[:], ALU.add).then_inc(m[step_sem], 1)

            def slot(b, k):
                i, g, t = SLOTS * b + k, k % GPT, TPB * b + k // GPT
                r = k % 2
                bv = b + (k - 1) // SLOTS
                if live(i - 2, GROUPS):
                    at_least(dve, "oT_hi_done", i - 1)
                    at_least(dve, "y_done", i - 3)
                    dve.tensor_tensor(oT_lo[r][:], B_O[:, 0:D].rearrange("p (q n) -> p q n", q=2),
                                      oT_hi[r][:].bitcast(F32), ALU.subtract).then_inc(m["oT_lo_done"], 1)
                if live(i + 1, GROUPS):
                    j1 = ((k + 1) // GPT) % 2
                    at_least(dve, "q_done", i + 2)
                    at_least(dve, "rope_joined", i)
                    a = B_Q[:, :].rearrange("p (h n) -> p h n", h=HG)[:, :, KVC:P]
                    cos = ropeq[:, j1, 0:1, :].to_broadcast([P, HG, R])
                    sin = ropeq[:, j1, 1:2, :].to_broadcast([P, HG, R]).rearrange("p h (a n) -> p h a n", a=2)
                    dve.tensor_tensor(rope_a[1 - r][:], a, cos, ALU.mult)
                    dve.tensor_tensor(rope_b[1 - r][:].rearrange("p h (a n) -> p h a n", a=2),
                                      a.rearrange("p h (a n) -> p h a n", a=2)[:, :, ::-1, :], sin,
                                      ALU.mult).then_inc(m["rope_parts"], 1)
                if (k - 1) % SLOTS == 0 and live(bv, B):
                    at_least(dve, "pv_done", SLOTS * bv)
                    kv = kcat[:, bass.ds(bv, 1), 0:KVC]
                    dve.tensor_copy(v_hi[:, 1:2, :], kv).then_inc(m["v_hi_done"], 1)
                    dve.wait_ge(m["v_hi_done"], bv + 1)
                    dve.tensor_tensor(v_lo[:, 1:2, :], kv, v_hi[:, 1:2, :].bitcast(F32), ALU.subtract).then_inc(m["v_split"], 1)
                if live(i, GROUPS):
                    at_least(dve, "s_done", i + 1)
                    if g == 0:
                        at_least(dve, "mask_step", 4 * (t + 1))
                    dve.tensor_tensor(s2m[:], B_S[:, :, 1, :], mask[:, :].unsqueeze(1).to_broadcast([P, HG, P]),
                                      ALU.add).then_inc(m["s2_masked"], 1)
                if live(i, GROUPS):
                    at_least(dve, "s2_masked", i + 1)
                    at_least(dve, "exp_done", i - 1)
                    carry_wait()
                    for h in range(HG):
                        e = dve.tensor_tensor_reduce(nsc[r][:, h, :], B_S[:, h, 0, :], s2m[:, h, :], -SCALE, BIG,
                                                     ALU.add, ALU.min, nmax[r][:, h:h + 1])
                    e.then_inc(m["score_max"], 1)
                if isinstance(i, int) and i - 2 in FOLD_SLOTS:
                    wo_low(dve, i + 1)
                    wo_low(dve, i + 2)
                if g == 1 and live(t - 1, TILES):
                    j = (k // GPT - 1) % 2
                    at_least(dve, "y_done", GPT * t)
                    at_least(dve, "acc_step", 2 * GPT * (t - 3) + 1)
                    dve.tensor_tensor(x2[j][:], B_Y[:, 0:D], x_all[:, bass.ds(t - 1, 1), :].rearrange("p a d -> p (a d)"),
                                      ALU.add).then_inc(m["x2_done"], 1)
                if g == 0 and live(t - 2, TILES):
                    at_least(dve, "gate_done", t - 1)
                    top_two("gate_step", 6 * (t - 2), [0])
                if live(i - 1, GROUPS):
                    at_least(dve, "pT_hi_done", i)
                    at_least(dve, "pv_done", i - 2)
                    dve.tensor_tensor(pT_lo[1 - r][:], B_PT[:, :].rearrange("p (h n) -> p h n", h=HG),
                                      pT_hi[1 - r][:].bitcast(F32), ALU.subtract).then_inc(m["pT_lo_done"], 1)
                if g == 0 and live(t - 2, TILES):
                    top_two("gate_step", 6 * (t - 2), [1])
                if g == 1 and live(t - 1, TILES):
                    dve.wait_ge(m["x2_done"], t)
                    dve.bn_stats(st2[:], x2[j][:]).then_inc(m["ln_step"], 1)
                if g == 3 and live(t - 1, TILES):
                    j = (k // GPT - 1) % 2
                    at_least(dve, "xT_hi_done", t)
                    at_least(dve, "e_done", GPT * (t - 2))
                    dve.tensor_tensor(xT_lo[j][:], B_X[:, 0:D].rearrange("p (c n) -> p c n", c=DC), xT_hi[j][:].bitcast(F32),
                                      ALU.subtract).then_inc(m["xT_lo_done"], 1)
                if live(i + 1, GROUPS):
                    at_least(dve, "qT_hi_done", i + 2)
                    at_least(dve, "s_done", i)
                    dve.tensor_tensor(qT_lo[1 - r][:], B_QT[:, :].rearrange("p (h n) -> p h n", h=HG), qT_hi[1 - r][:].bitcast(F32),
                                      ALU.subtract).then_inc(m["qT_lo_done"], 1)
                if g == 0 and live(t - 2, TILES):
                    top_two("gate_step", 6 * (t - 2), [2])
                if g == 1 and live(t - 1, TILES):
                    dve.wait_ge(m["ln_step"], 3 * t - 2)
                    at_least(dve, "x2n_done", t - 1)
                    carry_wait()
                    dve.bn_aggr(mv2[:], st2[:]).then_inc(m["ln_step"], 1)
                if g == 0 and live(t - 2, TILES):
                    top_two("gate_step", 6 * (t - 2), [3, 4])
                bk = b + (k + 1) // SLOTS
                if (k + 1) % SLOTS == 0 and live(bk, B):
                    at_least(dve, "s_done", SLOTS * bk)
                    kk = kT_all[:, bass.ds(bk, 1), :].rearrange("p a n -> p (a n)")
                    dve.tensor_copy(kT_hl[:, 0, :], kk).then_inc(m["k_hi_done"], 1)
                    dve.wait_ge(m["k_hi_done"], bk + 1)
                    dve.tensor_tensor(kT_hl[:, 1, :], kk, kT_hl[:, 0, :].bitcast(F32), ALU.subtract).then_inc(m["k_split"], 1)
                tq = TPB * b + k // GPT + 1
                if g == 2 and live(tq, TILES):
                    jq = (k // GPT + 1) % 2
                    at_least(dve, "q_done", GPT * (tq - 1))
                    q = qc_all[:, bass.ds(P * tq, P)]
                    dve.tensor_copy(qc_hi[jq][:], q).then_inc(m["qc_hi_done"], 1)
                    dve.wait_ge(m["qc_hi_done"], tq + 1)
                    dve.tensor_tensor(qc_lo[jq][:], q, qc_hi[jq][:].bitcast(F32), ALU.subtract).then_inc(m["qc_split"], 1)
                if g == 1 and live(t - 1, TILES):
                    dve.wait_ge(m["ln_step"], 3 * t - 1)
                    dve.tensor_scalar(veps2[:], mv2[:, 1:2], EPS, None, ALU.add).then_inc(m["ln_step"], 1)
                if live(i, GROUPS):
                    at_least(dve, "exp_done", i + 1)
                    at_least(dve, "prob_normed", i - 1)
                    dve.reciprocal(prec[r][:], psum_h[r][:]).then_inc(m["recip_done"], 1)
                if g == 0 and live(t - 2, TILES):
                    j = (k // GPT - 2) % 2
                    top_two("gate_step", 6 * (t - 2), [5, 6])
                    at_least(dve, "relu_done", GPT * (t - 3))
                    dve.tensor_scalar(gates[j][:], gt2[:], 0.5, None, ALU.mult).then_inc(m["gates_ready"], 1)
                if g == 2 and live(t - 1, TILES):
                    j = (k // GPT - 1) % 2
                    at_least(dve, "rstd2_done", t)
                    at_least(dve, "xT_done", t - 1)
                    dve.tensor_scalar(x2n[:], x2[j][:], mv2[:, 0:1], rstd2[:], ALU.subtract, ALU.mult).then_inc(m["x2n_done"], 1)

            near = dve.value_load(flag[0:1, 0:1], min_val=0, max_val=1)
            with dve.If(near == 1):
                walk(dve, slot)
            with dve.Else():
                general_dve(dve, carry_wait, top_two)

        @main.sync
        def _(sp):
            near = sp.value_load(flag[0:1, 0:1], min_val=0, max_val=1)
            with sp.If(near == 1):
                with sp.Fori(0, B) as b:
                    for j in range(TPB):
                        sp.wait_ge(m["acc_step"], 2 * GPT * (TPB * b + j) + 2 * GPT)
                        sp.dma_start(out[bass.ds(TPB * b + j, 1)].rearrange("a p d -> p (a d)"),
                                     acc[j][:]).then_inc(m[f"out_stored{j}"], 16)
                for j in range(TPB):
                    sp.wait_ge(m[f"out_stored{j}"], 16 * B)
            with sp.Else():
                general_sp(sp)


_INS = ["x", "ctx_t", "itok", "w_kvc", "w_dq", "w_uq_t", "w_qr", "w_uk_t", "w_kr", "w_uv_t", "w_o",
        "gate_w", "gate_b", "expert_w", "expert_b", "rope", "w_kvc_t"]


def rope_table():
    half = R // 2
    inv_freq = (1.0 / np.power(np.float32(10000.0), np.arange(half, dtype=np.float32) / np.float32(half))).astype(np.float32)
    ang = (np.arange(KCH * P, dtype=np.float32)[:, None] * inv_freq).astype(np.float64)
    cos, sin = np.cos(ang).astype(np.float32), np.sin(ang).astype(np.float32)
    return np.ascontiguousarray(np.concatenate([cos, cos, -sin, sin], axis=1))


def kernel(x, ctx_2048, itok_BxS_0_1023, L0_xattn_W_kvc, L0_xattn_W_dq, L0_xattn_W_uq, L0_xattn_W_qr, L0_xattn_W_uk,
           L0_xattn_W_kr, L0_xattn_W_uv, L0_xattn_W_o, L0_ffn_gate_w, L0_ffn_gate_b, L0_ffn_expert_w, L0_ffn_expert_b):
    import concourse.bacc as bacc
    from concourse.bass_utils import run_bass_kernel_spmd

    arrays = {
        "x": np.asarray(x).reshape(TILES, P, D),
        "ctx_t": np.asarray(ctx_2048).transpose(2, 0, 1),
        "itok": np.asarray(itok_BxS_0_1023).reshape(TILES, P).T,
        "w_kvc": L0_xattn_W_kvc, "w_dq": L0_xattn_W_dq, "w_uq_t": np.asarray(L0_xattn_W_uq).T, "w_qr": L0_xattn_W_qr,
        "w_uk_t": np.asarray(L0_xattn_W_uk).T, "w_kr": L0_xattn_W_kr, "w_uv_t": np.asarray(L0_xattn_W_uv).T,
        "w_o": L0_xattn_W_o, "gate_w": L0_ffn_gate_w, "gate_b": L0_ffn_gate_b, "expert_w": np.asarray(L0_ffn_expert_w).transpose(1, 0, 2).reshape(D, NE * O),
        "expert_b": L0_ffn_expert_b, "rope": rope_table(), "w_kvc_t": np.asarray(L0_xattn_W_kvc).T,
    }
    nc = bacc.Bacc("TRN2", target_bir_lowering=False, num_devices=1)
    arrays = {n: np.ascontiguousarray(arrays[n]) for n in _INS}
    args = [nc.dram_tensor(f"in_{n}", a.shape, mybir.dt.from_np(a.dtype), kind="ExternalInput").ap()
            for n, a in arrays.items()]
    out = nc.dram_tensor("out", (TILES, P, D), F32, kind="ExternalOutput").ap()
    kernel_program(nc, *args, out)
    r = run_bass_kernel_spmd(nc, [{f"in_{n}": a for n, a in arrays.items()}], core_ids=[0])
    return r.results[0]["out"].reshape(B, L, D)
```

```python
from contextlib import ExitStack

import numpy as np

import concourse.bass as bass
from concourse import mybir

F32 = mybir.dt.float32
F32R = mybir.dt.float32r
BF16 = mybir.dt.bfloat16
I32 = mybir.dt.int32
ALU = mybir.AluOpType
ACT = mybir.ActivationFunctionType
AX = mybir.AxisListType

P = 128
B, L, D = 8, 256, 256
LK = 1601
H, HD = 16, 128
KVC, QC, R = 64, 96, 64
LOOKBACK = 8
NE, O = 8, 256
EPS = 1e-5
NEG = -1e30
SCALE = float(np.float32(1.0) / np.sqrt(HD + R).astype(np.float32))
DC = D // P
TPB = L // P
TILES = B * TPB
HG = 4
GPT = H // HG
GROUPS = TILES * GPT
SLOTS = TPB * GPT
PAIRS = H // 2
KCH = -(-LK // P)
BIG = 3e38


def kernel_program(nc, x, ctx_t, itok, w_kvc, w_dq, w_uq_t, w_qr, w_uk_t, w_kr, w_uv_t, w_o,
                   gate_w, gate_b, expert_w, expert_b, rope, w_kvc_t, out):
    with ExitStack() as ctx:
        def sb(name, shape, dt=F32):
            return ctx.enter_context(nc.sbuf_tensor(name, shape, dt))

        def sem(name):
            return ctx.enter_context(nc.semaphore(name))

        psum = ctx.enter_context(nc.psum_tensor("psum", [P, 8 * 512], F32))
        bank = [psum[:, 512 * i:512 * i + 512] for i in range(8)]

        x_all = sb("x_all", [P, TILES, D])
        qc_all = sb("qc_all", [QC, B * L])
        wq_hi, wq_lo = sb("wq_hi", [QC, H, P], F32R), sb("wq_lo", [QC, H, P], F32R)
        wo_hi, wo_lo = sb("wo_hi", [P, PAIRS, D], F32R), sb("wo_lo", [P, PAIRS, D], F32R)
        we_hi, we_lo = sb("we_hi", [P, DC, NE * O], F32R), sb("we_lo", [P, DC, NE * O], F32R)
        wg = sb("wg", [P, DC, NE])
        wg_hl = sb("wg_hl", [P, DC, 2, NE], F32R)
        gate_bias = sb("gate_bias", [P, NE])
        bias3 = sb("bias3", [3, NE * O], BF16)
        ones3 = sb("ones3", [3, P], BF16)
        ident = sb("ident", [P, P])
        kidx = sb("kidx", [P, P])
        ropeq = sb("ropeq", [P, TPB, 2, R])
        wcat = sb("wcat", [P, DC, P])
        wkvc = wcat[:, :, 0:KVC]
        wkr = sb("wkr", [KVC, R])
        kcat = sb("kcat", [P, B, P])
        kT_all = sb("kT_all", [P, B, P])
        seg_i = sb("seg_i", [P, TILES], I32)
        seg = sb("seg", [P, TILES, 2])
        half_neg = sb("half_neg", [P, TILES])
        ones8 = sb("ones8", [P, NE])
        flag = sb("flag", [1, 1], I32)

        v_hi, v_lo = sb("v_hi", [P, 3, KVC], F32R), sb("v_lo", [P, 3, KVC], F32R)

        block_sems = {}

        def S(name):
            if name not in block_sems:
                block_sems[name] = sem(name)
            return block_sems[name]

        qc_hi = [sb(f"qc_hi{i}", [QC, P], F32R) for i in range(2)]
        qc_lo = [sb(f"qc_lo{i}", [QC, P], F32R) for i in range(2)]
        seg_t = sb("seg_t", [P, 2])
        x2 = [sb(f"x2_{i}", [P, D]) for i in range(2)]
        st2, mv2, veps2, rstd2 = sb("st2", [P, 6]), sb("mv2", [P, 2]), sb("veps2", [P, 1]), sb("rstd2", [P, 1])
        x2n = sb("x2n", [P, D])
        xT_hi = [sb(f"xT_hi{i}", [P, DC, P], F32R) for i in range(2)]
        xT_lo = [sb(f"xT_lo{i}", [P, DC, P], F32R) for i in range(2)]
        logit, top8, need = sb("logit", [P, NE]), sb("top8", [P, NE]), sb("need", [P, 1])
        eq2, eq_cum, eq_in, gt2 = sb("eq2", [P, NE]), sb("eq_cum", [P, NE]), sb("eq_in", [P, NE]), sb("gt2", [P, NE])
        gates = [sb(f"gates{i}", [P, NE]) for i in range(2)]
        eout = [sb(f"eout{i}", [P, 2, O]) for i in range(2)]
        acc = [sb(f"acc{i}", [P, D]) for i in range(2)]
        prep_only = ExitStack()

        def tmp(name, shape, dt=F32):
            return prep_only.enter_context(nc.sbuf_tensor(name, shape, dt))

        ctxT = tmp("ctxT", [P, DC, B, P])
        wkvcT = tmp("wkvcT", [KVC, D])
        wuqT = tmp("wuqT", [P, H, QC])
        wukT = tmp("wukT", [P, H, KVC])
        wqr = tmp("wqr", [QC, H, R])
        ropek = tmp("ropek", [P, 2, R])
        ka, kb = tmp("ka", [P, B // 2, R]), tmp("kb", [P, B // 2, R])
        eb = tmp("eb", [16, P])
        eb_r = tmp("eb_r", [16, 2, P])
        in_lo, in_both = tmp("in_lo", [P, TILES]), tmp("in_both", [P, TILES])
        row_ok = tmp("row_ok", [P, 1])
        ones_col = tmp("ones_col", [P, 1])
        table_probe = tmp("table_probe", [P, 1])
        kidx_i = tmp("kidx_i", [P, P], I32)
        tmp("ring_room", [P, 26 * P])
        wdq = tmp("wdq", [P, DC, QC])
        st_all = tmp("st_all", [P, TILES, 6])
        mv_all = tmp("mv_all", [P, TILES, 2])
        veps_all = tmp("veps_all", [P, TILES])
        rstd_all = tmp("rstd_all", [P, TILES])
        xn = [tmp(f"xn{i}", [P, TPB, D]) for i in range(2)]
        xnT = tmp("xnT", [P, DC, TPB * P])
        eb3 = tmp("eb3", [16, 3, P], BF16)
        wuvT = tmp("wuvT", [P, H, KVC])
        wo_raw = tmp("wo_raw", [P, H, D])
        we_raw = tmp("we_raw", [P, DC, NE * O])

        X_PARTS = [slice(0, TPB), slice(TPB, 6), slice(6, 11), slice(11, TILES)]

        def norm_stats(dve, ts):
            for t in range(ts.start, ts.stop):
                dve.bn_stats(st_all[:, t, :], x_all[:, t, :]).then_inc(S("st_done"), 1)
            dve.wait_ge(S("st_done"), ts.stop)
            for t in range(ts.start, ts.stop):
                dve.bn_aggr(mv_all[:, t, :], st_all[:, t, :]).then_inc(S("mv_done"), 1)

        def add_eps(dve, ts):
            dve.wait_ge(S("mv_done"), ts.stop)
            dve.tensor_scalar(veps_all[:, ts], mv_all[:, ts, 1], EPS, None, ALU.add).then_inc(S("veps_done"), 1)

        prep = prep_only.enter_context(nc.Block())

        @prep.sync
        def _(sp):
            def load_x(i):
                ts = X_PARTS[i]
                sp.dma_start(x_all[:, ts, :], x[ts].rearrange("t p d -> p t d")).then_inc(S(f"ld_x{i}"), 16)
            load_x(0)
            for c in range(DC):
                sp.dma_start(ctxT[:, c, :, :], ctx_t[P * c:P * c + P, :, 0:P]).then_inc(S("ld_ctx"), 16)
            sp.dma_start(wukT[:], w_uk_t.rearrange("(h p) n -> p h n", p=P)).then_inc(S("ld_wuq"), 16)
            load_x(1)
            sp.dma_start(gate_bias[:], gate_b.partition_broadcast(P)).then_inc(S("ld_gate_bias"), 16)
            sp.dma_start(ropeq[:], rope[0:L, :].rearrange("(t p) (a n) -> p t a n", p=P, a=2)).then_inc(S("ld_ropeq"), 16)
            sp.dma_start(wuvT[:], w_uv_t.rearrange("(h p) n -> p h n", p=P)).then_inc(S("ld_wuv"), 16)
            sp.dma_start(wo_raw[:, 0:H // 2, :], w_o[0:H // 2 * HD, :].rearrange("(h p) n -> p h n", p=P)).then_inc(S("ld_wo0"), 16)
            load_x(2)
            load_x(3)
            sp.dma_start(wo_raw[:, H // 2:H, :], w_o[H // 2 * HD:H * HD, :].rearrange("(h p) n -> p h n", p=P)).then_inc(S("ld_wo1"), 16)
            sp.dma_start(we_raw[:], expert_w.rearrange("(c p) n -> p c n", p=P)).then_inc(S("ld_we"), 16)

        @prep.scalar
        def _(act):
            act.dma_start(wkvcT[:], w_kvc_t).then_inc(S("ld_kv"), 16)
            act.dma_start(wkr[:], w_kr).then_inc(S("ld_kv"), 16)
            act.dma_start(wkvc, w_kvc.rearrange("(c p) n -> p c n", p=P)).then_inc(S("ld_kv"), 16)
            act.dma_start(wdq[:], w_dq.rearrange("(c p) n -> p c n", p=P)).then_inc(S("ld_wdq"), 16)
            act.dma_start(wuqT[:], w_uq_t.rearrange("(h p) n -> p h n", p=P)).then_inc(S("ld_wuq"), 16)
            act.dma_start(wqr[:], w_qr.rearrange("c (h r) -> c h r", r=R)).then_inc(S("ld_wqr"), 16)
            act.wait_ge(S("ones_set"), 3)
            act.copy(table_probe[:], ones_col[:]).then_inc(S("table_loaded"), 1)

            act.wait_ge(S("xT_mm"), 1)
            act.copy(xnT[:].rearrange("p c n -> p (c n)"), bank[6]).then_inc(S("xT_sb"), 1)
            act.wait_ge(S("qc_mm"), 1)
            act.copy(qc_all[:, 0:L], bank[2][0:QC, 0:L]).then_inc(S("qc_sb"), 1)
            act.wait_ge(S("ld_wqr"), 16)
            act.copy(wq_hi[:, :, KVC:P], wqr[:]).then_inc(S("wqr_hi_done"), 1)
            act.wait_ge(S("fold_q_mm"), 1)
            for i in range(2):
                act.copy(wq_hi[:, 8 * i:8 * i + 8, 0:KVC],
                         bank[4 + i][0:QC, :].rearrange("p (h n) -> p h n", h=8)).then_inc(S("wq_hi_done"), 1)
            act.wait_ge(S("kT_mm"), 1)
            for i in range(2):
                act.copy(kT_all[:, 4 * i:4 * i + 4, :],
                         bank[i].rearrange("p (b k) -> p b k", b=4)).then_inc(S("kT_sb"), 1)

        @prep.gpsimd
        def _(pool):
            pool.memset(half_neg[:], -0.5).then_inc(S("half_set"), 1)
            pool.memset(ident[:], 0.0).then_inc(S("ident_zero"), 1)
            pool.iota(kidx_i[:], [[1, P]], base=0, channel_multiplier=0).then_inc(S("iota_done"), 1)
            pool.wait_ge(S("ident_zero"), 1)
            pool.affine_select(out=ident[:], in_=ident[:], compare_op=ALU.not_equal, fill=1.0, base=0,
                               pattern=[[-1, P]], channel_multiplier=1).then_inc(S("ident_done"), 1)
            pool.memset(ones_col[:], 1.0).then_inc(S("ones_set"), 1)
            pool.memset(ones3[:], 1.0).then_inc(S("ones_set"), 1)
            pool.memset(ones8[:], 1.0).then_inc(S("ones_set"), 1)
            pool.memset(v_hi[:].bitcast(F32), 0.0).then_inc(S("v_zero"), 1)
            pool.memset(v_lo[:].bitcast(F32), 0.0).then_inc(S("v_zero"), 1)
            pool.dma_start(ropek[:], rope[0:P, :].rearrange("p (a n) -> p a n", a=2)).then_inc(S("ld_rope"), 16)
            pool.dma_start(seg_i[:], itok).then_inc(S("ld_seg"), 16)
            pool.dma_start(wg[:], gate_w.rearrange("(c p) n -> p c n", p=P)).then_inc(S("ld_eb_wg"), 16)
            pool.wait_ge(S("half_set"), 1)
            pool.wait_ge(S("veps_done"), 1)
            pool.tensor_tensor(rstd_all[:, 0:TPB], veps_all[:, 0:TPB], half_neg[:, 0:TPB], ALU.pow).then_inc(S("rstd_done"), 1)
            pool.dma_start(eb[:], expert_b.rearrange("e (a n) -> (e a) n", n=P)).then_inc(S("ld_eb_wg"), 16)
            pool.wait_ge(S("veps_done"), 2)
            ts = X_PARTS[1]
            pool.tensor_tensor(rstd_all[:, ts], veps_all[:, ts], half_neg[:, ts], ALU.pow).then_inc(S("rstd_done"), 1)

        @prep.vector
        def _(dve):
            dve.wait_ge(S("ld_x0"), 16)
            norm_stats(dve, X_PARTS[0])
            add_eps(dve, X_PARTS[0])
            dve.wait_ge(S("rstd_done"), 1)
            for t in range(TPB):
                dve.tensor_scalar(xn[0][:, t, :], x_all[:, t, :], mv_all[:, t, 0:1], rstd_all[:, t:t + 1],
                                  ALU.subtract, ALU.mult).then_inc(S("xn_done"), 1)
            dve.wait_ge(S("wkk_mm"), 1)
            dve.tensor_copy(wcat[:, :, KVC:P], bank[4][:, 0:DC * R].rearrange("p (c n) -> p c n", c=DC)).then_inc(S("wkk_sb"), 1)
            dve.wait_ge(S("ld_seg"), 16)
            dve.tensor_copy(seg[:, :, 0], seg_i[:]).then_inc(S("seg_f"), 1)
            dve.wait_ge(S("seg_f"), 1)
            dve.tensor_scalar(seg[:, :, 1], seg[:, :, 0], float(-LOOKBACK), None, ALU.add).then_inc(S("seg_f"), 1)
            dve.tensor_scalar(in_lo[:], seg[:, :, 0], 0.0, None, ALU.is_ge).then_inc(S("seg_f"), 1)
            dve.wait_ge(S("seg_f"), 3)
            dve.scalar_tensor_tensor(out=in_both[:], in0=seg[:, :, 0], scalar=float(P - 1), in1=in_lo[:],
                                     op0=ALU.is_le, op1=ALU.mult).then_inc(S("seg_f"), 1)
            dve.wait_ge(S("seg_f"), 4)
            dve.tensor_reduce(row_ok[:], in_both[:], AX.X, ALU.min).then_inc(S("row_ok_done"), 1)
            dve.wait_ge(S("iota_done"), 1)
            dve.tensor_copy(kidx[:], kidx_i[:]).then_inc(S("kidx_done"), 1)
            dve.wait_ge(S("ld_rope"), 16)
            for i in range(2):
                dve.wait_ge(S("k_mm"), i + 1)
                bs = slice(4 * i, 4 * i + 4)
                rows = bank[i].rearrange("p (b n) -> p b n", b=4)
                dve.tensor_copy(kcat[:, bs, 0:KVC], rows[:, :, 0:KVC]).then_inc(S("kcat_done"), 1)
                kr = rows[:, :, KVC:P]
                cos = ropek[:, 0:1, :].to_broadcast([P, 4, R])
                sin = ropek[:, 1:2, :].to_broadcast([P, 4, R]).rearrange("p b (a n) -> p b a n", a=2)
                if i > 0:
                    dve.wait_ge(S("kcat_done"), 2)
                dve.tensor_tensor(ka[:], kr, cos, ALU.mult).then_inc(S("kparts"), 1)
                dve.tensor_tensor(kb[:].rearrange("p b (a n) -> p b a n", a=2),
                                  kr.rearrange("p b (a n) -> p b a n", a=2)[:, :, ::-1, :], sin, ALU.mult
                                  ).then_inc(S("kparts"), 1)
                dve.wait_ge(S("kparts"), 2 * i + 2)
                dve.tensor_tensor(kcat[:, bs, KVC:P], ka[:], kb[:], ALU.add).then_inc(S("kcat_done"), 1)
            dve.wait_ge(S("ok_mm"), 1)
            dve.tensor_scalar(flag[:], bank[5][0:1, 0:1], float(P), None, ALU.is_ge).then_inc(S("flag_done"), 1)
            dve.wait_ge(S("ld_x1"), 16)
            norm_stats(dve, X_PARTS[1])
            add_eps(dve, X_PARTS[1])
            dve.wait_ge(S("ld_eb_wg"), 32)
            dve.tensor_copy(wg_hl[:, :, 0, :], wg[:]).then_inc(S("wg_done"), 1)
            dve.tensor_copy(eb3[:, 0, :], eb[:]).then_inc(S("eb_step"), 1)
            dve.wait_ge(S("wg_done"), 1)
            dve.tensor_tensor(wg_hl[:, :, 1, :], wg[:], wg_hl[:, :, 0, :].bitcast(F32), ALU.subtract).then_inc(S("wg_done"), 1)
            for r in range(2):
                dve.wait_ge(S("eb_step"), 2 * r + 1)
                src = eb[:] if r == 0 else eb_r[:, 0, :]
                dve.tensor_tensor(eb_r[:, r, :], src, eb3[:, r, :], ALU.subtract).then_inc(S("eb_step"), 1)
                dve.wait_ge(S("eb_step"), 2 * r + 2)
                dve.tensor_copy(eb3[:, r + 1, :], eb_r[:, r, :]).then_inc(S("eb_step"), 1)
            dve.wait_ge(S("wqr_hi_done"), 1)
            dve.tensor_tensor(wq_lo[:, :, KVC:P], wqr[:], wq_hi[:, :, KVC:P].bitcast(F32), ALU.subtract).then_inc(S("wq_lo_done"), 1)
            for i in range(2):
                dve.wait_ge(S("wq_hi_done"), i + 1)
                dve.tensor_tensor(wq_lo[:, 8 * i:8 * i + 8, 0:KVC],
                                  bank[4 + i][0:QC, :].rearrange("p (h n) -> p h n", h=8),
                                  wq_hi[:, 8 * i:8 * i + 8, 0:KVC].bitcast(F32), ALU.subtract).then_inc(S("wq_lo_done"), 1)

        @prep.tensor
        def _(pe):
            pe.wait_ge(S("ident_done"), 1)

            pe.wait_ge(S("ld_kv"), 48)
            for c in range(DC):
                mm = pe.matmul(bank[4][:, R * c:R * c + R], wkvcT[:, P * c:P * c + P], wkr[:], start=True, stop=True)
            mm.then_inc(S("wkk_mm"), 1)
            pe.wait_ge(S("xn_done"), TPB)
            for c in range(DC):
                for t in range(TPB):
                    mm = pe.transpose(bank[6][:, L * c + P * t:L * c + P * t + P], xn[0][:, t, P * c:P * c + P], ident[:])
            mm.then_inc(S("xT_mm"), 1)
            pe.wait_ge(S("ld_ctx"), 16 * DC)
            pe.wait_ge(S("wkk_sb"), 1)
            for b in range(B):
                for c in range(DC):
                    mm = pe.matmul(bank[b // 4][:, P * (b % 4):P * (b % 4) + P], ctxT[:, c, b, :], wcat[:, c, :],
                                   start=(c == 0), stop=(c == DC - 1))
                if b % 4 == 3:
                    mm.then_inc(S("k_mm"), 1)
            pe.wait_ge(S("row_ok_done"), 1)
            pe.wait_ge(S("ones_set"), 3)
            pe.matmul(bank[5][0:1, 0:1], row_ok[:], ones_col[:], start=True, stop=True).then_inc(S("ok_mm"), 1)
            pe.wait_ge(S("ld_wdq"), 16)
            pe.wait_ge(S("xT_sb"), 1)
            for c in range(DC):
                mm = pe.matmul(bank[2][0:QC, 0:L], wdq[:, c, :], xnT[:, c, :], start=(c == 0), stop=(c == DC - 1))
            mm.then_inc(S("qc_mm"), 1)
            pe.wait_ge(S("ld_wuq"), 32)
            pe.wait_ge(S("wkk_sb"), 1)
            pe.wait_ge(S("flag_done"), 1)
            for h in range(H):
                mm = pe.matmul(bank[4 + h // 8][0:QC, KVC * (h % 8):KVC * (h % 8) + KVC], wuqT[:, h, :], wukT[:, h, :],
                               start=True, stop=True)
            mm.then_inc(S("fold_q_mm"), 1)
            pe.wait_ge(S("kcat_done"), 4)
            for b in range(B):
                mm = pe.transpose(bank[b // 4][:, P * (b % 4):P * (b % 4) + P], kcat[:, b, :], ident[:])
            mm.then_inc(S("kT_mm"), 1)

        prep_only.close()

        general_mem = ExitStack()

        def gb(name, shape, dt=F32):
            return general_mem.enter_context(nc.sbuf_tensor(name, shape, dt))

        LP = KCH * P
        ctx_l = gb("ctx_l", [P, DC, LP])
        kcat_l, kT_l = gb("kcat_l", [P, KCH, P]), gb("kT_l", [P, LP])
        rope_l = gb("rope_l", [P, KCH, 2, R])
        kidx_l, mask_l, le_l = gb("kidx_l", [P, LP]), gb("mask_l", [P, LP]), gb("le_l", [P, LP])
        sc_l = gb("sc_l", [P, LP])
        kvT_l = sc_l[0:KVC, :]
        pT_l = le_l[:, :].rearrange("p (k n) -> p k n", k=KCH)
        q_l, q_h, qT_h = gb("q_l", [P, H, P]), gb("q_h", [P, P]), gb("qT_h", [P, P])
        ra_l, rb_l = gb("ra_l", [P, 8, R]), gb("rb_l", [P, 8, R])
        mx_l, sum_l, rec_l = gb("mx_l", [P, 1]), gb("sum_l", [P, 1]), gb("rec_l", [P, 1])
        o_l = gb("o_l", [P, H * KVC])
        oT_hi_l, oT_lo_l = gb("oT_hi_l", [P, PAIRS, P], F32R), gb("oT_lo_l", [P, PAIRS, P], F32R)
        general_mem.close()

        q_sb = [sb(f"q_sb{i}", [P, HG, P]) for i in range(2)]
        rope_a = [sb(f"rope_a{i}", [P, HG, R]) for i in range(2)]
        rope_b = [sb(f"rope_b{i}", [P, HG, R]) for i in range(2)]
        qT_hi = [sb(f"qT_hi{i}", [P, HG, P], F32R) for i in range(2)]
        qT_lo = [sb(f"qT_lo{i}", [P, HG, P], F32R) for i in range(2)]
        nsc = [sb(f"nsc{i}", [P, HG, P]) for i in range(2)]
        nmax = [sb(f"nmax{i}", [P, HG]) for i in range(2)]
        prob = [sb(f"prob{i}", [P, HG, P]) for i in range(2)]
        psum_h = [sb(f"psum_h{i}", [P, HG]) for i in range(2)]
        prec = [sb(f"prec{i}", [P, HG]) for i in range(2)]
        pT_hi = [sb(f"pT_hi{i}", [P, HG, P], F32R) for i in range(2)]
        pT_lo = [sb(f"pT_lo{i}", [P, HG, P], F32R) for i in range(2)]
        oT_hi = [sb(f"oT_hi{i}", [P, 2, P], F32R) for i in range(2)]
        oT_lo = [sb(f"oT_lo{i}", [P, 2, P], F32R) for i in range(2)]
        kT_hl = sb("kT_hl", [P, 2, P], F32R)
        s2m = sb("s2m", [P, HG, P])
        m_after, m_before, mask = sb("m_after", [P, P]), sb("m_before", [P, P]), sb("mask", [P, P])

        B_Q, B_E, B_QT, B_PT, _, _, B_Y, B_X = bank
        B_S = psum[:, 4 * 512:6 * 512].rearrange("p (h a n) -> p h a n", h=HG, a=2)
        B_O = B_X

        general_names = [
            "g_const", "g_rope_ld", "g_ctx_ld", "g_kvT_mm", "g_kvT_sb", "g_rows_mm", "g_rows_nope", "g_rows_parts",
            "g_rows_sb", "g_kT_mm", "g_kT_sb", "g_mask", "g_qc", "g_q_mm", "g_q_parts", "g_q_sb", "g_qh", "g_qhT_mm", "g_qhT_sb",
            "g_s_mm", "g_masked", "g_max", "g_shifted", "g_exp", "g_rec", "g_prob", "g_pT_mm", "g_pT_sb", "g_pv_mm",
            "g_o_sb", "g_oT_mm", "g_oT_hi", "g_oT_lo", "g_y_mm", "g_ln", "g_rstd", "g_x2n", "g_xT_mm", "g_xT_hi", "g_xT_lo",
            "g_gate_mm", "g_topk", "g_gates", "g_e_mm", "g_relu", "g_acc", "g_stored", "g_carried"]
        names = general_names + ["q_done", "qT_done", "s_done", "pT_done", "pv_done", "y_done", "xT_done", "gate_done", "e_done",
                 "nope_copied", "qT_hi_done", "exp_done", "pT_hi_done", "oT_hi_done", "xT_hi_done", "relu_done",
                 "rope_parts", "qT_lo_done", "score_max", "recip_done", "pT_lo_done", "oT_lo_done", "x2_done",
                 "ln_step", "x2n_done", "xT_lo_done", "gates_ready", "gate_step", "logit_part", "qc_split", "mask_step", "k_split",
                 "v_split", "v_hi_done", "x_normed", "x_turned", "x_columns", "latent_mm", "latent_sb", "wo_hi_done",
                 "wo_lo_done", "fold_o_mm", "we_hi_done", "we_lo_done", "k_hi_done", "qc_hi_done", "s2_masked", "waits_passed",
                 "rope_joined", "prob_normed", "rstd2_done", "acc_step", "out_stored0", "out_stored1"]
        m = {n: sem(n) for n in names}

        def at_least(eng, name, n):
            if not isinstance(n, int) or n > 0:
                eng.wait_ge(m[name], n)

        def live(i, end):
            return not isinstance(i, int) or 0 <= i < end

        fold_bank = [B_E, B_Y]

        def fold_o(pe, n):
            pe.wait_ge(S("ld_wuv"), 16)
            pe.wait_ge(S(f"ld_wo{n // 2}"), 16)
            if n > 1:
                pe.wait_ge(m["wo_lo_done"], n - 1)
            for q in range(2):
                for odd in range(2):
                    h = 4 * n + 2 * q + odd
                    mm = pe.matmul(fold_bank[n % 2][64 * odd:64 * odd + 64, D * q:D * q + D], wuvT[:, h, :], wo_raw[:, h, :],
                                   start=True, stop=True)
            mm.then_inc(m["fold_o_mm"], 1)

        def wo_high(act, n):
            act.wait_ge(m["fold_o_mm"], n + 1)
            act.copy(wo_hi[:, 2 * n:2 * n + 2, :], fold_bank[n % 2].rearrange("p (q n) -> p q n", q=2)).then_inc(m["wo_hi_done"], 1)

        def wo_low(dve, n):
            dve.wait_ge(m["wo_hi_done"], n + 1)
            dve.tensor_tensor(wo_lo[:, 2 * n:2 * n + 2, :], fold_bank[n % 2].rearrange("p (q n) -> p q n", q=2),
                              wo_hi[:, 2 * n:2 * n + 2, :].bitcast(F32), ALU.subtract).then_inc(m["wo_lo_done"], 1)

        def late_stats(dve, i):
            dve.wait_ge(S(f"ld_x{i}"), 16)
            norm_stats(dve, X_PARTS[i])
            add_eps(dve, X_PARTS[i])

        def late_rstd(pool, i):
            ts = X_PARTS[i]
            pool.wait_ge(S("veps_done"), i + 1)
            pool.tensor_tensor(rstd_all[:, ts], veps_all[:, ts], half_neg[:, ts], ALU.pow).then_inc(S("rstd_done"), 1)

        def x_norm(dve, n):
            dve.wait_ge(S("rstd_done"), 1 + next(i for i, ts in enumerate(X_PARTS) if ts.stop >= TPB * n + TPB))
            if n > 2:
                dve.wait_ge(m["x_turned"], n - 2)
            for j in range(TPB):
                t = TPB * n + j
                dve.tensor_scalar(xn[n % 2][:, j, :], x_all[:, t, :], mv_all[:, t, 0:1], rstd_all[:, t:t + 1],
                                  ALU.subtract, ALU.mult).then_inc(m["x_normed"], 1)

        def x_turn(pe, n):
            pe.wait_ge(m["x_normed"], TPB * n)
            if n == 1:
                pe.wait_ge(m["wo_lo_done"], FOLDS)
            else:
                pe.wait_ge(m["x_columns"], n - 1)
            for c in range(DC):
                for j in range(TPB):
                    mm = pe.transpose(B_E[:, L * c + P * j:L * c + P * j + P], xn[n % 2][:, j, P * c:P * c + P], ident[:])
            mm.then_inc(m["x_turned"], 1)

        def x_columns(act, n):
            act.wait_ge(m["x_turned"], n)
            if n > 1:
                act.wait_ge(m["latent_mm"], n - 1)
            act.copy(xnT[:].rearrange("p c n -> p (c n)"), B_E).then_inc(m["x_columns"], 1)

        def latent(pe, n):
            pe.wait_ge(m["x_columns"], n)
            if n > 1:
                pe.wait_ge(m["latent_sb"], n - 1)
            for c in range(DC):
                mm = pe.matmul(B_Q[0:QC, 0:L], wdq[:, c, :], xnT[:, c, :], start=(c == 0), stop=(c == DC - 1))
            mm.then_inc(m["latent_mm"], 1)

        def latent_copy(dve, n):
            dve.wait_ge(m["latent_mm"], n)
            dve.tensor_copy(qc_all[:, L * n:L * n + L], B_Q[0:QC, 0:L]).then_inc(m["latent_sb"], 1)

        def expert_piece(n):
            return n % DC, slice(512 * (n // DC), 512 * (n // DC) + 512)

        def we_high(act, n):
            c, cols = expert_piece(n)
            if n == 0:
                act.wait_ge(S("ld_we"), 16)
            act.copy(we_hi[:, c, cols], we_raw[:, c, cols]).then_inc(m["we_hi_done"], 1)

        def we_low(pool, n):
            c, cols = expert_piece(n)
            pool.wait_ge(m["we_hi_done"], n + 1)
            pool.tensor_tensor(we_lo[:, c, cols], we_raw[:, c, cols], we_hi[:, c, cols].bitcast(F32), ALU.subtract
                               ).then_inc(m["we_lo_done"], 1)

        FOLDS, EXPERT_PIECES = PAIRS // 2, DC * NE // 2

        def piece_of(i, count):
            return isinstance(i, int) and 0 <= i < count

        main = ctx.enter_context(nc.Block())

        def expert_bank(f):
            return B_Q if isinstance(f, int) and f > GROUPS - 8 and f % 2 else B_E

        def walk(eng, slot):
            for k in range(-3, 2 * SLOTS):
                slot(k // SLOTS if k > 0 else 0, k % SLOTS if k > 0 else k)
            with eng.Fori(2, B - 1) as b:
                for k in range(SLOTS):
                    slot(b, k)
            for k in range(SLOTS + 9):
                slot(B - 1, k)

        def mm3(pe, out_ap, l_hi, l_lo, r_hi, r_lo, start=True, stop=True):
            pe.matmul(out_ap, l_hi, r_hi, start=start, stop=False)
            pe.matmul(out_ap, l_hi, r_lo, start=False, stop=False)
            return pe.matmul(out_ap, l_lo, r_hi, start=False, stop=stop)

        def gate_product(pe, c, j):
            pe.matmul(B_X[:, D:D + 2 * NE], xT_hi[j][:, c, :], wg_hl[:, c, :, :].rearrange("p a n -> p (a n)"),
                      start=(c == 0), stop=False)
            return pe.matmul(B_X[:, D:D + NE], xT_lo[j][:, c, :], wg_hl[:, c, 0, :], start=False, stop=(c == DC - 1))

        PIECES = [(512 * n, min(512, LP - 512 * n)) for n in range(4)]
        SEEN = [(at, min(n, LK - at)) for at, n in PIECES]
        CHUNKS = [(c, min(P, LK - P * c)) for c in range(KCH)]

        def carry(eng):
            eng.sem_inc(m["g_carried"], 1)

        def tiles(eng, batch_steps, tile_steps):
            with eng.Fori(0, B) as b:
                batch_steps(b)
                for j in range(TPB):
                    tile_steps(b, j, TPB * b + j)

        def no_steps(*_):
            pass

        def general_sp(sp):
            sp.wait_ge(S("ld_bias3"), 48)
            sp.wait_ge(m["latent_mm"], B - 1)
            sp.wait_ge(m["fold_o_mm"], FOLDS)
            sp.wait_ge(m["we_lo_done"], EXPERT_PIECES)
            sp.dma_start(rope_l[:], rope.rearrange("(c p) (a n) -> p c a n", p=P, a=2)).then_inc(m["g_rope_ld"], 16)
            sp.wait_ge(m["g_const"], 2)

            def batch(b):
                sp.wait_ge(m["g_kT_mm"], b)
                carry(sp)
                for c in range(DC):
                    sp.dma_start(ctx_l[:, c, 0:LK], ctx_t[P * c:P * c + P, bass.ds(b, 1), :].rearrange("p a k -> p (a k)")
                                 ).then_inc(m["g_ctx_ld"], 16)

            def tile(b, j, t):
                sp.wait_ge(m["g_acc"], NE * (t + 1))
                carry(sp)
                sp.dma_start(out[bass.ds(t, 1)].rearrange("a p d -> p (a d)"), acc[0][:]).then_inc(m["g_stored"], 16)
                sp.wait_ge(m["g_stored"], 16 * (t + 1))
                carry(sp)
            tiles(sp, batch, tile)

        def general_pe(pe):
            for n in range(FOLDS):
                fold_o(pe, n)
            for n in range(1, B):
                x_turn(pe, n)
                latent(pe, n)
            pe.wait_ge(m["latent_sb"], B - 1)
            pe.wait_ge(m["we_lo_done"], EXPERT_PIECES)
            pe.wait_ge(S("ld_bias3"), 48)

            def batch(b):
                pe.wait_ge(m["g_ctx_ld"], 32 * (b + 1))
                for n, (at, w) in enumerate(PIECES):
                    for c in range(DC):
                        mm = pe.matmul(bank[n][0:KVC, 0:w], wkvc[:, c, :], ctx_l[:, c, at:at + w], start=(c == 0), stop=(c == DC - 1))
                mm.then_inc(m["g_kvT_mm"], 1)
                pe.wait_ge(m["g_kvT_sb"], 4 * (b + 1))
                for k, _ in CHUNKS:
                    at = KVC * (k % 8)
                    for c in range(DC):
                        pe.matmul(bank[4 + k // 8][:, at:at + KVC], ctx_l[:, c, P * k:P * k + P], wkvc[:, c, :],
                                  start=(c == 0), stop=(c == DC - 1))
                    mm = pe.matmul(bank[6 + k // 8][:, at:at + R], kvT_l[:, P * k:P * k + P], wkr[:], start=True, stop=True)
                mm.then_inc(m["g_rows_mm"], 1)
                pe.wait_ge(m["g_rows_sb"], 2 * (b + 1))
                for k, _ in CHUNKS:
                    mm = pe.transpose(bank[k // 4][:, P * (k % 4):P * (k % 4) + P], kcat_l[:, k, :], ident[:])
                mm.then_inc(m["g_kT_mm"], 1)
                pe.wait_ge(m["g_kT_sb"], 4 * (b + 1))

            def tile(b, j, t):
                pe.wait_ge(m["g_qc"], 2 * (t + 1))
                for g in range(GPT):
                    hs = slice(HG * g, HG * g + HG)
                    mm = mm3(pe, bank[g][:, :], qc_hi[0][:], qc_lo[0][:], wq_hi[:, hs, :].rearrange("p h n -> p (h n)"),
                             wq_lo[:, hs, :].rearrange("p h n -> p (h n)"))
                mm.then_inc(m["g_q_mm"], 1)
                pe.wait_ge(m["g_q_sb"], GPT * (t + 1))
                carry(pe)
                with pe.Fori(0, H) as h:
                    n = H * t + h + 1
                    pe.wait_ge(m["g_qh"], n)
                    pe.transpose(bank[4][:, 0:P], q_h[:], ident[:]).then_inc(m["g_qhT_mm"], 1)
                    pe.wait_ge(m["g_qhT_sb"], n)
                    for i, (at, w) in enumerate(SEEN):
                        mm = pe.matmul(bank[i][:, 0:w], qT_h[:], kT_l[:, at:at + w], start=True, stop=True)
                    mm.then_inc(m["g_s_mm"], 1)
                    pe.wait_ge(m["g_prob"], n)
                    for k, w in CHUNKS:
                        mm = pe.transpose(bank[4 + k // 4][0:w, P * (k % 4):P * (k % 4) + P], sc_l[:, P * k:P * k + w], ident[:])
                    mm.then_inc(m["g_pT_mm"], 1)
                    pe.wait_ge(m["g_pT_sb"], KCH * n)
                    for k, w in CHUNKS:
                        mm = pe.matmul(bank[0][:, 0:KVC], pT_l[0:w, k, :], kcat_l[0:w, k, 0:KVC], start=(k == 0), stop=(k == KCH - 1))
                    mm.then_inc(m["g_pv_mm"], 1)
                pe.wait_ge(m["g_o_sb"], H * (t + 1))
                for q in range(PAIRS):
                    mm = pe.transpose(bank[4 + q // 4][:, P * (q % 4):P * (q % 4) + P], o_l[:, P * q:P * q + P], ident[:])
                mm.then_inc(m["g_oT_mm"], 1)
                pe.wait_ge(m["g_oT_lo"], 2 * (t + 1))
                for q in range(PAIRS):
                    mm = mm3(pe, B_Y[:, 0:D], oT_hi_l[:, q, :], oT_lo_l[:, q, :], wo_hi[:, q, :], wo_lo[:, q, :],
                             start=(q == 0), stop=(q == PAIRS - 1))
                mm.then_inc(m["g_y_mm"], 1)
                pe.wait_ge(m["g_x2n"], t + 1)
                for c in range(DC):
                    mm = pe.transpose(B_X[:, P * c:P * c + P], x2n[:, P * c:P * c + P], ident[:])
                mm.then_inc(m["g_xT_mm"], 1)
                pe.wait_ge(m["g_xT_lo"], t + 1)
                for c in range(DC):
                    mm = gate_product(pe, c, 0)
                mm.then_inc(m["g_gate_mm"], 1)
                for kc in range(GPT):
                    cols = slice(512 * kc, 512 * kc + 512)
                    pe.matmul(bank[kc][:, :], ones3[:], bias3[:, cols], start=True, stop=False)
                    for c in range(DC):
                        mm = mm3(pe, bank[kc][:, :], xT_hi[0][:, c, :], xT_lo[0][:, c, :], we_hi[:, c, cols], we_lo[:, c, cols],
                                 start=False, stop=(c == DC - 1))
                mm.then_inc(m["g_e_mm"], 1)
                pe.wait_ge(m["g_relu"], NE * (t + 1))
            tiles(pe, batch, tile)

        def general_act(act):
            for n in range(FOLDS):
                wo_high(act, n)
            for n in range(1, B):
                x_columns(act, n)
            for n in range(EXPERT_PIECES):
                we_high(act, n)

            def batch(b):
                act.wait_ge(m["g_kvT_mm"], b + 1)
                for n, (at, w) in enumerate(PIECES):
                    act.copy(kvT_l[:, at:at + w], bank[n][0:KVC, 0:w]).then_inc(m["g_kvT_sb"], 1)
                act.wait_ge(m["g_kT_mm"], b + 1)
                for n, (at, w) in enumerate(PIECES):
                    act.copy(kT_l[:, at:at + w], bank[n][:, 0:w]).then_inc(m["g_kT_sb"], 1)

            def tile(b, j, t):
                with act.Fori(0, H) as h:
                    n = H * t + h + 1
                    act.wait_ge(m["g_qhT_mm"], n)
                    act.copy(qT_h[:], bank[4][:, 0:P]).then_inc(m["g_qhT_sb"], 1)
                    act.wait_ge(m["g_shifted"], n)
                    act.activation(sc_l[:, 0:LK], sc_l[:, 0:LK], ACT.Exp, accum_out=sum_l[:]).then_inc(m["g_exp"], 1)
                    act.wait_ge(m["g_pT_mm"], n)
                    for k, w in CHUNKS:
                        act.copy(pT_l[0:w, k, :], bank[4 + k // 4][0:w, P * (k % 4):P * (k % 4) + P]).then_inc(m["g_pT_sb"], 1)
                act.wait_ge(m["g_oT_mm"], t + 1)
                for n in range(2):
                    act.copy(oT_hi_l[:, 4 * n:4 * n + 4, :], bank[4 + n][:, :].rearrange("p (q n) -> p q n", q=4)
                             ).then_inc(m["g_oT_hi"], 1)
                act.wait_ge(m["g_xT_mm"], t + 1)
                act.copy(xT_hi[0][:], B_X[:, 0:D].rearrange("p (c n) -> p c n", c=DC)).then_inc(m["g_xT_hi"], 1)
                act.wait_ge(m["g_gates"], t + 1)
                act.wait_ge(m["g_e_mm"], t + 1)
                for e in range(NE):
                    act.wait_ge(m["g_acc"], NE * t + e)
                    act.activation(eout[0][:, 0, :], bank[e // 2][:, O * (e % 2):O * (e % 2) + O], ACT.Relu,
                                   scale=gates[0][:, e:e + 1]).then_inc(m["g_relu"], 1)
            tiles(act, batch, tile)

        def general_pool(pool):
            for i in (2, 3):
                late_rstd(pool, i)
            for n in range(EXPERT_PIECES):
                we_low(pool, n)
            pool.wait_ge(S("ld_bias3"), 48)
            pool.wait_ge(m["latent_mm"], B - 1)
            pool.wait_ge(m["fold_o_mm"], FOLDS)
            pool.wait_ge(m["we_lo_done"], EXPERT_PIECES)
            pool.iota(le_l[:].bitcast(I32), [[1, LP]], base=0, channel_multiplier=0).then_inc(m["g_const"], 1)

            def tile(b, j, t):
                pool.wait_ge(m["g_ln"], 4 * (t + 1))
                pool.tensor_tensor(rstd2[:], veps2[:], half_neg[:, 0:1], ALU.pow).then_inc(m["g_rstd"], 1)
            tiles(pool, no_steps, tile)

        def general_dve(dve, carry_wait, top_two):
            for n in range(FOLDS):
                wo_low(dve, n)
            for i in (2, 3):
                late_stats(dve, i)
            x_norm(dve, 1)
            for n in range(1, B):
                if n < B - 1:
                    x_norm(dve, n + 1)
                latent_copy(dve, n)
            dve.wait_ge(S("ld_bias3"), 48)
            dve.wait_ge(m["latent_mm"], B - 1)
            dve.wait_ge(m["latent_sb"], B - 1)
            dve.wait_ge(m["fold_o_mm"], FOLDS)
            dve.wait_ge(m["we_lo_done"], EXPERT_PIECES)
            for c in range(DC):
                mset = dve.memset(ctx_l[:, c, LK:LP], 0.0)
            mset.then_inc(m["g_const"], 1)
            dve.wait_ge(m["g_const"], 2)
            dve.tensor_copy(kidx_l[:], le_l[:].bitcast(I32)).then_inc(m["g_const"], 1)
            dve.wait_ge(m["g_const"], 3)
            dve.wait_ge(m["g_rope_ld"], 16)

            def rotate(out_ap, src, cos, sin, n, parts, count):
                dve.tensor_tensor(ra_l[:, 0:n, :], src, cos, ALU.mult)
                dve.tensor_tensor(rb_l[:, 0:n, :].rearrange("p h (a n) -> p h a n", a=2),
                                  src.rearrange("p h (a n) -> p h a n", a=2)[:, :, ::-1, :],
                                  sin.rearrange("p h (a n) -> p h a n", a=2), ALU.mult).then_inc(m[parts], 1)
                dve.wait_ge(m[parts], count)
                return dve.tensor_tensor(out_ap, ra_l[:, 0:n, :], rb_l[:, 0:n, :], ALU.add)

            def batch(b):
                dve.wait_ge(m["g_rows_mm"], b + 1)
                for i, n in enumerate((8, KCH - 8)):
                    ks = slice(8 * i, 8 * i + n)
                    rows = bank[4 + i][:, 0:KVC * n].rearrange("p (k n) -> p k n", k=n)
                    dve.tensor_copy(kcat_l[:, ks, 0:KVC], rows).then_inc(m["g_rows_nope"], 1)
                    rot = bank[6 + i][:, 0:R * n].rearrange("p (k n) -> p k n", k=n)
                    rotate(kcat_l[:, ks, KVC:P], rot, rope_l[:, ks, 0, :], rope_l[:, ks, 1, :], n, "g_rows_parts",
                           2 * b + i + 1).then_inc(m["g_rows_sb"], 1)
                    dve.wait_ge(m["g_rows_sb"], 2 * b + i + 1)

            def tile(b, j, t):
                dve.tensor_copy(seg_t[:], seg[:, bass.ds(t, 1), :].rearrange("p a n -> p (a n)")).then_inc(m["g_mask"], 1)
                dve.wait_ge(m["g_mask"], 4 * t + 1)
                dve.tensor_scalar(le_l[:], kidx_l[:], seg_t[:, 0:1], None, ALU.is_le).then_inc(m["g_mask"], 1)
                dve.wait_ge(m["g_mask"], 4 * t + 2)
                dve.scalar_tensor_tensor(out=mask_l[:], in0=kidx_l[:], scalar=seg_t[:, 1:2], in1=le_l[:], op0=ALU.is_ge,
                                         op1=ALU.mult).then_inc(m["g_mask"], 1)
                dve.wait_ge(m["g_mask"], 4 * t + 3)
                dve.tensor_scalar(mask_l[:], mask_l[:], -1.0, -NEG, ALU.add, ALU.mult).then_inc(m["g_mask"], 1)
                q = qc_all[:, bass.ds(P * t, P)]
                dve.tensor_copy(qc_hi[0][:], q).then_inc(m["g_qc"], 1)
                dve.wait_ge(m["g_qc"], 2 * t + 1)
                dve.tensor_tensor(qc_lo[0][:], q, qc_hi[0][:].bitcast(F32), ALU.subtract).then_inc(m["g_qc"], 1)
                dve.wait_ge(m["g_q_mm"], t + 1)
                cos = ropeq[:, j, 0:1, :].to_broadcast([P, HG, R])
                sin = ropeq[:, j, 1:2, :].to_broadcast([P, HG, R])
                for g in range(GPT):
                    hs, src = slice(HG * g, HG * g + HG), bank[g][:, :].rearrange("p (h n) -> p h n", h=HG)
                    dve.tensor_copy(q_l[:, hs, 0:KVC], src[:, :, 0:KVC])
                    rotate(q_l[:, hs, KVC:P], src[:, :, KVC:P], cos, sin, HG, "g_q_parts", GPT * t + g + 1
                           ).then_inc(m["g_q_sb"], 1)
                    dve.wait_ge(m["g_q_sb"], GPT * t + g + 1)
                carry(dve)
                with dve.Fori(0, H) as h:
                    n = H * t + h + 1
                    dve.tensor_copy(q_h[:], q_l[:, bass.ds(h, 1), :].rearrange("p a n -> p (a n)")).then_inc(m["g_qh"], 1)
                    dve.wait_ge(m["g_s_mm"], n)
                    for i, (at, w) in enumerate(SEEN):
                        e = dve.tensor_tensor(sc_l[:, at:at + w], bank[i][:, 0:w], mask_l[:, at:at + w], ALU.add)
                    e.then_inc(m["g_masked"], 1)
                    dve.wait_ge(m["g_masked"], n)
                    dve.tensor_reduce(mx_l[:], sc_l[:, 0:LK], AX.X, ALU.max).then_inc(m["g_max"], 1)
                    dve.wait_ge(m["g_max"], n)
                    dve.tensor_scalar(sc_l[:, 0:LK], sc_l[:, 0:LK], mx_l[:], SCALE, ALU.subtract, ALU.mult
                                      ).then_inc(m["g_shifted"], 1)
                    dve.wait_ge(m["g_exp"], n)
                    dve.reciprocal(rec_l[:], sum_l[:]).then_inc(m["g_rec"], 1)
                    dve.wait_ge(m["g_rec"], n)
                    dve.tensor_scalar(sc_l[:, 0:LK], sc_l[:, 0:LK], rec_l[:], None, ALU.mult).then_inc(m["g_prob"], 1)
                    dve.wait_ge(m["g_pv_mm"], n)
                    dve.tensor_copy(o_l[:, bass.ds(KVC * h, KVC)], bank[0][:, 0:KVC]).then_inc(m["g_o_sb"], 1)
                for n in range(2):
                    dve.wait_ge(m["g_oT_hi"], 2 * (t + 1))
                    dve.tensor_tensor(oT_lo_l[:, 4 * n:4 * n + 4, :], bank[4 + n][:, :].rearrange("p (q n) -> p q n", q=4),
                                      oT_hi_l[:, 4 * n:4 * n + 4, :].bitcast(F32), ALU.subtract).then_inc(m["g_oT_lo"], 1)
                dve.wait_ge(m["g_y_mm"], t + 1)
                dve.tensor_tensor(x2[0][:], B_Y[:, 0:D], x_all[:, bass.ds(t, 1), :].rearrange("p a d -> p (a d)"),
                                  ALU.add).then_inc(m["g_ln"], 1)
                dve.wait_ge(m["g_ln"], 4 * t + 1)
                dve.bn_stats(st2[:], x2[0][:]).then_inc(m["g_ln"], 1)
                dve.wait_ge(m["g_ln"], 4 * t + 2)
                carry_wait()
                dve.bn_aggr(mv2[:], st2[:]).then_inc(m["g_ln"], 1)
                dve.wait_ge(m["g_ln"], 4 * t + 3)
                dve.tensor_scalar(veps2[:], mv2[:, 1:2], EPS, None, ALU.add).then_inc(m["g_ln"], 1)
                dve.wait_ge(m["g_rstd"], t + 1)
                dve.tensor_scalar(x2n[:], x2[0][:], mv2[:, 0:1], rstd2[:], ALU.subtract, ALU.mult).then_inc(m["g_x2n"], 1)
                dve.wait_ge(m["g_xT_hi"], t + 1)
                dve.tensor_tensor(xT_lo[0][:], B_X[:, 0:D].rearrange("p (c n) -> p c n", c=DC), xT_hi[0][:].bitcast(F32),
                                  ALU.subtract).then_inc(m["g_xT_lo"], 1)
                dve.wait_ge(m["g_gate_mm"], t + 1)
                top_two("g_topk", t)
                dve.tensor_scalar(gates[0][:], gt2[:], 0.5, None, ALU.mult).then_inc(m["g_gates"], 1)
                for e in range(NE):
                    dve.wait_ge(m["g_relu"], NE * t + e + 1)
                    if e == 0:
                        dve.wait_ge(m["g_stored"], 16 * t)
                    else:
                        dve.wait_ge(m["g_acc"], NE * t + e)
                    dve.tensor_tensor(acc[0][:], x2[0][:] if e == 0 else acc[0][:], eout[0][:, 0, :], ALU.add
                                      ).then_inc(m["g_acc"], 1)
            tiles(dve, batch, tile)

        @main.tensor
        def _(pe):
            def slot(b, k):
                i, g, t = SLOTS * b + k, k % GPT, TPB * b + k // GPT
                r = k % 2
                if live(i + 1, GROUPS):
                    g1, j1 = (k + 1) % GPT, ((k + 1) // GPT) % 2
                    if g1 == 0:
                        at_least(pe, "qc_split", TPB * b + (k + 1) // GPT + 1)
                    at_least(pe, "nope_copied", i + 1)
                    at_least(pe, "rope_parts", i + 1)
                    if piece_of(i - 2, B - 1):
                        pe.wait_ge(m["latent_sb"], i - 1)
                    hs = slice(HG * g1, HG * g1 + HG)
                    mm3(pe, B_Q[:, :], qc_hi[j1][:], qc_lo[j1][:], wq_hi[:, hs, :].rearrange("p h n -> p (h n)"),
                        wq_lo[:, hs, :].rearrange("p h n -> p (h n)")).then_inc(m["q_done"], 1)
                if live(i, GROUPS):
                    if k % SLOTS == 0:
                        at_least(pe, "k_split", b + k // SLOTS + 1)
                    at_least(pe, "qT_hi_done", i + 1)
                    at_least(pe, "qT_lo_done", i + 1)
                    at_least(pe, "score_max", i)
                    for h in range(HG):
                        pe.matmul(B_S[:, h, :, :], qT_hi[r][:, h, :], kT_hl[:], start=True, stop=False)
                        mm = pe.matmul(B_S[:, h, 0, :], qT_lo[r][:, h, :], kT_hl[:, 0, :], start=False, stop=True)
                    mm.then_inc(m["s_done"], 1)
                if isinstance(i, int) and i == -1:
                    fold_o(pe, 0)
                    fold_o(pe, 1)
                if live(i - 1, GROUPS):
                    at_least(pe, "prob_normed", i)
                    at_least(pe, "pT_hi_done", i - 1)
                    at_least(pe, "pT_lo_done", i - 1)
                    for h in range(HG):
                        mm = pe.transpose(B_PT[:, P * h:P * h + P], prob[1 - r][:, h, :], ident[:])
                    mm.then_inc(m["pT_done"], 1)
                if live(i - 2, GROUPS):
                    gp = (k - 2) % GPT
                    at_least(pe, "oT_hi_done", i - 1)
                    at_least(pe, "oT_lo_done", i - 1)
                    if isinstance(i, int) and i - 2 < FOLDS:
                        pe.wait_ge(m["wo_lo_done"], FOLDS)
                    if gp == 0:
                        at_least(pe, "x2_done", TPB * b + (k - 2) // GPT)
                    for q in range(2):
                        mm = mm3(pe, B_Y[:, 0:D], oT_hi[r][:, q, :], oT_lo[r][:, q, :], wo_hi[:, 2 * gp + q, :],
                                 wo_lo[:, 2 * gp + q, :], start=(gp == 0 and q == 0), stop=(gp == GPT - 1 and q == 1))
                    mm.then_inc(m["y_done"], 1)
                if g == 0 and live(t - 2, TILES):
                    j = (k // GPT - 2) % 2
                    at_least(pe, "xT_hi_done", t - 1)
                    at_least(pe, "xT_lo_done", t - 1)
                    for c in range(DC):
                        mm = gate_product(pe, c, j)
                    mm.then_inc(m["gate_done"], 1)
                if live(i + 1, GROUPS):
                    at_least(pe, "rope_joined", i + 2)
                    at_least(pe, "nope_copied", i + 2)
                    at_least(pe, "qT_hi_done", i + 1)
                    at_least(pe, "qT_lo_done", i + 1)
                    for h in range(HG):
                        mm = pe.transpose(B_QT[:, P * h:P * h + P], q_sb[1 - r][:, h, :], ident[:])
                    mm.then_inc(m["qT_done"], 1)
                if g == 3 and live(t - 1, TILES):
                    at_least(pe, "x2n_done", t)
                    last = i - 1 if not isinstance(i, int) else min(i - 1, GROUPS)
                    at_least(pe, "oT_hi_done", last)
                    at_least(pe, "oT_lo_done", last)
                    for c in range(DC):
                        mm = pe.transpose(B_X[:, P * c:P * c + P], x2n[:, P * c:P * c + P], ident[:])
                    mm.then_inc(m["xT_done"], 1)
                if isinstance(i, int) and i == -1:
                    fold_o(pe, 2)
                    fold_o(pe, 3)
                if piece_of(i - 1, B - 1):
                    at_least(pe, "nope_copied", i + 2)
                    latent(pe, i)
                if piece_of(i, B - 1):
                    x_turn(pe, i + 1)
                f = i - 8
                if live(f, GROUPS):
                    kc, j = (k - 8) % GPT, ((k - 8) // GPT) % 2
                    at_least(pe, "relu_done", f - 1 if isinstance(f, int) and f > GROUPS - 8 else f)
                    if isinstance(f, int) and f < GPT:
                        pe.wait_ge(S("ld_bias3"), 48)
                        pe.wait_ge(m["x_columns"], B - 1)
                        pe.wait_ge(m["we_lo_done"], DC * (f + 1))
                    cols = slice(512 * kc, 512 * kc + 512)
                    z = expert_bank(f)
                    pe.matmul(z, ones3[:], bias3[:, cols], start=True, stop=False)
                    for c in range(DC):
                        mm = mm3(pe, z, xT_hi[j][:, c, :], xT_lo[j][:, c, :], we_hi[:, c, cols], we_lo[:, c, cols],
                                 start=False, stop=(c == DC - 1))
                    mm.then_inc(m["e_done"], 1)
                if live(i - 1, GROUPS):
                    if (k - 1) % SLOTS == 0:
                        at_least(pe, "v_split", b + (k - 1) // SLOTS + 1)
                    at_least(pe, "pT_hi_done", i)
                    at_least(pe, "pT_lo_done", i)
                    at_least(pe, "oT_hi_done", i - 1)
                    at_least(pe, "oT_lo_done", i - 1)
                    if g == 3 and live(t - 1, TILES):
                        at_least(pe, "xT_lo_done", t)
                    if g == 0 and live(t - 2, TILES):
                        at_least(pe, "gate_step", 6 * (t - 2) + 1)
                    q1 = 1 - r
                    o = B_O[:, 0:D]
                    for odd in range(2):
                        w = slice(KVC - KVC * odd, P + KVC - KVC * odd)
                        vh = v_hi[:].rearrange("p a n -> p (a n)")[:, w]
                        vl = v_lo[:].rearrange("p a n -> p (a n)")[:, w]
                        mm = mm3(pe, o, vh, vl, pT_hi[q1][:, odd::2, :], pT_lo[q1][:, odd::2, :],
                                 start=(odd == 0), stop=(odd == 1))
                    mm.then_inc(m["pv_done"], 1)

            near = pe.value_load(flag[0:1, 0:1], min_val=0, max_val=1)
            with pe.If(near == 1):
                walk(pe, slot)
            with pe.Else():
                general_pe(pe)

        @main.scalar
        def _(act):
            def slot(b, k):
                i, g, t = SLOTS * b + k, k % GPT, TPB * b + k // GPT
                r = k % 2
                if isinstance(i, int) and i == 0:
                    wo_high(act, 2)
                    wo_high(act, 3)
                if live(i + 1, GROUPS):
                    at_least(act, "rope_parts", i + 2)
                    at_least(act, "qT_done", i)
                    act.copy(q_sb[1 - r][:, :, 0:KVC],
                             B_Q[:, :].rearrange("p (h n) -> p h n", h=HG)[:, :, 0:KVC]).then_inc(m["nope_copied"], 1)
                if isinstance(i, int) and i == -1:
                    wo_high(act, 0)
                    wo_high(act, 1)
                if live(i - 1, GROUPS):
                    at_least(act, "pT_done", i)
                    at_least(act, "pv_done", i - 2)
                    act.copy(pT_hi[1 - r][:], B_PT[:, :].rearrange("p (h n) -> p h n", h=HG)).then_inc(m["pT_hi_done"], 1)
                if live(i + 1, GROUPS):
                    at_least(act, "qT_done", i + 2)
                    at_least(act, "s_done", i)
                    act.copy(qT_hi[1 - r][:], B_QT[:, :].rearrange("p (h n) -> p h n", h=HG)).then_inc(m["qT_hi_done"], 1)
                if g == 3 and live(t - 1, TILES):
                    j = (k // GPT - 1) % 2
                    at_least(act, "xT_done", t)
                    at_least(act, "e_done", GPT * (t - 2))
                    act.copy(xT_hi[j][:], B_X[:, 0:D].rearrange("p (c n) -> p c n", c=DC)).then_inc(m["xT_hi_done"], 1)
                if live(i, GROUPS):
                    at_least(act, "score_max", i + 1)
                    at_least(act, "pT_done", i - 1)
                    at_least(act, "recip_done", i - 1)
                    for h in range(HG):
                        e = act.activation(prob[r][:, h, :], nsc[r][:, h, :], ACT.Exp, bias=nmax[r][:, h:h + 1], scale=-1.0,
                                           accum_out=psum_h[r][:, h:h + 1])
                    e.then_inc(m["exp_done"], 1)
                if live(i - 1, GROUPS):
                    at_least(act, "pv_done", i)
                    at_least(act, "y_done", i - 2)
                    act.copy(oT_hi[1 - r][:], B_O[:, 0:D].rearrange("p (q n) -> p q n", q=2)).then_inc(m["oT_hi_done"], 1)
                if piece_of(i, B - 1):
                    x_columns(act, i + 1)
                if piece_of(i, EXPERT_PIECES):
                    we_high(act, i)
                f = i - 8
                if live(f, GROUPS):
                    kc, tile = (k - 8) % GPT, TPB * b + (k - 8) // GPT
                    j = ((k - 8) // GPT) % 2
                    at_least(act, "e_done", f + 1)
                    if kc == 0:
                        at_least(act, "gates_ready", tile + 1)
                    at_least(act, "acc_step", 2 * (f - 1))
                    for e in range(2):
                        a = act.activation(eout[r][:, e, :], expert_bank(f)[:, O * e:O * e + O], ACT.Relu,
                                           scale=gates[j][:, 2 * kc + e:2 * kc + e + 1])
                    a.then_inc(m["relu_done"], 1)

            near = act.value_load(flag[0:1, 0:1], min_val=0, max_val=1)
            with act.If(near == 1):
                walk(act, slot)
            with act.Else():
                general_act(act)

        @main.gpsimd
        def _(pool):
            def slot(b, k):
                i, g, t = SLOTS * b + k, k % GPT, TPB * b + k // GPT
                r = k % 2
                if live(i + 1, GROUPS):
                    at_least(pool, "rope_parts", i + 2)
                    at_least(pool, "qT_done", i)
                    pool.tensor_tensor(q_sb[1 - r][:, :, KVC:P], rope_a[1 - r][:], rope_b[1 - r][:],
                                       ALU.add).then_inc(m["rope_joined"], 1)
                if isinstance(i, int) and i in (-1, 0):
                    late_rstd(pool, i + 3)
                if piece_of(i - 1, EXPERT_PIECES):
                    we_low(pool, i - 1)

                def second_norm():
                    if g == 2 and live(t - 1, TILES):
                        at_least(pool, "ln_step", 3 * t)
                        at_least(pool, "x2n_done", t - 1)
                        pool.tensor_tensor(rstd2[:], veps2[:], half_neg[:, 0:1], ALU.pow).then_inc(m["rstd2_done"], 1)

                draining = isinstance(i, int) and i >= GROUPS
                if draining:
                    second_norm()
                f = i - 9
                if live(f, GROUPS):
                    kc, j = (k - 9) % GPT, ((k - 9) // GPT) % 2
                    at_least(pool, "relu_done", f + 1)
                    if kc == 0:
                        at_least(pool, f"out_stored{j}", 16 * (b + (k - 9) // SLOTS))
                    else:
                        at_least(pool, "acc_step", 2 * f)
                    pool.tensor_tensor(acc[j][:], x2[j][:] if kc == 0 else acc[j][:], eout[1 - r][:, 0, :],
                                       ALU.add).then_inc(m["acc_step"], 1)
                    at_least(pool, "acc_step", 2 * f + 1)
                    pool.tensor_tensor(acc[j][:], acc[j][:], eout[1 - r][:, 1, :], ALU.add).then_inc(m["acc_step"], 1)
                if not draining:
                    second_norm()
                tq = TPB * b + k // GPT + 1
                if g == 1 and live(tq, TILES):
                    pool.tensor_copy(seg_t[:], seg[:, bass.ds(tq, 1), :].rearrange("p a n -> p (a n)")).then_inc(m["mask_step"], 1)
                    at_least(pool, "mask_step", 4 * tq + 1)
                    pool.sem_inc(m["waits_passed"], 1)
                    pool.tensor_scalar(m_after[:], kidx[:], seg_t[:, 0:1], NEG, ALU.is_gt, ALU.mult).then_inc(m["mask_step"], 1)
                if g == 2 and live(tq, TILES):
                    at_least(pool, "mask_step", 4 * tq + 1)
                    pool.sem_inc(m["waits_passed"], 1)
                    pool.tensor_scalar(m_before[:], kidx[:], seg_t[:, 1:2], NEG, ALU.is_lt, ALU.mult).then_inc(m["mask_step"], 1)
                if g == 3 and live(tq, TILES):
                    at_least(pool, "mask_step", 4 * tq + 3)
                    at_least(pool, "s2_masked", i + 1)
                    pool.tensor_tensor(mask[:], m_before[:], m_after[:], ALU.add).then_inc(m["mask_step"], 1)
                if live(i, GROUPS):
                    at_least(pool, "recip_done", i + 1)
                    p = prob[r]
                    pool.tensor_tensor(p[:], p[:], prec[r][:, :].unsqueeze(2).to_broadcast([P, HG, P]),
                                       ALU.mult).then_inc(m["prob_normed"], 1)

            near = pool.value_load(flag[0:1, 0:1], min_val=0, max_val=1)
            with pool.If(near == 1):
                walk(pool, slot)
            with pool.Else():
                general_pool(pool)

        @main.vector
        def _(dve):
            dve.wait_ge(S("ld_ropeq"), 16)
            dve.wait_ge(S("ld_gate_bias"), 16)

            def carry_wait():
                dve.sem_inc(m["waits_passed"], 1)

            def top_two(step_sem, tile, steps=range(7)):
                n = 6 * tile
                for step in steps:
                    if step > 0:
                        dve.wait_ge(m[step_sem], n + step)
                    if step == 0:
                        dve.tensor_tensor(logit[:], B_X[:, D:D + NE], gate_bias[:], ALU.add).then_inc(m["logit_part"], 1)
                        dve.wait_ge(m["logit_part"], tile + 1)
                        dve.tensor_tensor(logit[:], logit[:], B_X[:, D + NE:D + 2 * NE], ALU.add).then_inc(m[step_sem], 1)
                    elif step == 1:
                        carry_wait()
                        dve.max(top8[:], logit[:]).then_inc(m[step_sem], 1)
                    elif step == 2:
                        dve.tensor_scalar(need[:], top8[:, 0:1], top8[:, 1:2], 1.0, ALU.is_equal, ALU.add)
                        dve.tensor_scalar(gt2[:], logit[:], top8[:, 1:2], None, ALU.is_gt)
                        dve.tensor_scalar(eq2[:], logit[:], top8[:, 1:2], None, ALU.is_equal).then_inc(m[step_sem], 1)
                    elif step == 3:
                        dve.tensor_tensor_scan(eq_cum[:], ones8[:], eq2[:], 0.0, ALU.mult, ALU.add).then_inc(m[step_sem], 1)
                    elif step == 4:
                        dve.scalar_tensor_tensor(out=eq_in[:], in0=eq_cum[:], scalar=need[:], in1=eq2[:],
                                                 op0=ALU.is_le, op1=ALU.mult).then_inc(m[step_sem], 1)
                    elif step == 5:
                        dve.tensor_tensor(gt2[:], gt2[:], eq_in[:], ALU.add).then_inc(m[step_sem], 1)

            def slot(b, k):
                i, g, t = SLOTS * b + k, k % GPT, TPB * b + k // GPT
                r = k % 2
                bv = b + (k - 1) // SLOTS
                if live(i - 2, GROUPS):
                    at_least(dve, "oT_hi_done", i - 1)
                    at_least(dve, "y_done", i - 3)
                    dve.tensor_tensor(oT_lo[r][:], B_O[:, 0:D].rearrange("p (q n) -> p q n", q=2),
                                      oT_hi[r][:].bitcast(F32), ALU.subtract).then_inc(m["oT_lo_done"], 1)
                if live(i + 1, GROUPS):
                    j1 = ((k + 1) // GPT) % 2
                    at_least(dve, "q_done", i + 2)
                    at_least(dve, "rope_joined", i)
                    a = B_Q[:, :].rearrange("p (h n) -> p h n", h=HG)[:, :, KVC:P]
                    cos = ropeq[:, j1, 0:1, :].to_broadcast([P, HG, R])
                    sin = ropeq[:, j1, 1:2, :].to_broadcast([P, HG, R]).rearrange("p h (a n) -> p h a n", a=2)
                    dve.tensor_tensor(rope_a[1 - r][:], a, cos, ALU.mult)
                    dve.tensor_tensor(rope_b[1 - r][:].rearrange("p h (a n) -> p h a n", a=2),
                                      a.rearrange("p h (a n) -> p h a n", a=2)[:, :, ::-1, :], sin,
                                      ALU.mult).then_inc(m["rope_parts"], 1)
                if (k - 1) % SLOTS == 0 and live(bv, B):
                    at_least(dve, "pv_done", SLOTS * bv)
                    kv = kcat[:, bass.ds(bv, 1), 0:KVC]
                    dve.tensor_copy(v_hi[:, 1:2, :], kv).then_inc(m["v_hi_done"], 1)
                    dve.wait_ge(m["v_hi_done"], bv + 1)
                    dve.tensor_tensor(v_lo[:, 1:2, :], kv, v_hi[:, 1:2, :].bitcast(F32), ALU.subtract).then_inc(m["v_split"], 1)
                if live(i, GROUPS):
                    at_least(dve, "s_done", i + 1)
                    if g == 0:
                        at_least(dve, "mask_step", 4 * (t + 1))
                    dve.tensor_tensor(s2m[:], B_S[:, :, 1, :], mask[:, :].unsqueeze(1).to_broadcast([P, HG, P]),
                                      ALU.add).then_inc(m["s2_masked"], 1)
                if live(i, GROUPS):
                    at_least(dve, "s2_masked", i + 1)
                    at_least(dve, "exp_done", i - 1)
                    carry_wait()
                    for h in range(HG):
                        e = dve.tensor_tensor_reduce(nsc[r][:, h, :], B_S[:, h, 0, :], s2m[:, h, :], -SCALE, BIG,
                                                     ALU.add, ALU.min, nmax[r][:, h:h + 1])
                    e.then_inc(m["score_max"], 1)
                if isinstance(i, int) and i in (-1, 0):
                    wo_low(dve, 2 * i + 2)
                    wo_low(dve, 2 * i + 3)
                if g == 1 and live(t - 1, TILES):
                    j = (k // GPT - 1) % 2
                    at_least(dve, "y_done", GPT * t)
                    at_least(dve, "acc_step", 2 * GPT * (t - 3) + 1)
                    dve.tensor_tensor(x2[j][:], B_Y[:, 0:D], x_all[:, bass.ds(t - 1, 1), :].rearrange("p a d -> p (a d)"),
                                      ALU.add).then_inc(m["x2_done"], 1)
                if g == 0 and live(t - 2, TILES):
                    at_least(dve, "gate_done", t - 1)
                    top_two("gate_step", t - 2, [0])
                if live(i - 1, GROUPS):
                    at_least(dve, "pT_hi_done", i)
                    at_least(dve, "pv_done", i - 2)
                    dve.tensor_tensor(pT_lo[1 - r][:], B_PT[:, :].rearrange("p (h n) -> p h n", h=HG),
                                      pT_hi[1 - r][:].bitcast(F32), ALU.subtract).then_inc(m["pT_lo_done"], 1)
                if g == 0 and live(t - 2, TILES):
                    top_two("gate_step", t - 2, [1])
                if g == 1 and live(t - 1, TILES):
                    dve.wait_ge(m["x2_done"], t)
                    dve.bn_stats(st2[:], x2[j][:]).then_inc(m["ln_step"], 1)
                if g == 3 and live(t - 1, TILES):
                    j = (k // GPT - 1) % 2
                    at_least(dve, "xT_hi_done", t)
                    at_least(dve, "e_done", GPT * (t - 2))
                    dve.tensor_tensor(xT_lo[j][:], B_X[:, 0:D].rearrange("p (c n) -> p c n", c=DC), xT_hi[j][:].bitcast(F32),
                                      ALU.subtract).then_inc(m["xT_lo_done"], 1)
                if live(i + 1, GROUPS):
                    at_least(dve, "qT_hi_done", i + 2)
                    at_least(dve, "s_done", i)
                    dve.tensor_tensor(qT_lo[1 - r][:], B_QT[:, :].rearrange("p (h n) -> p h n", h=HG), qT_hi[1 - r][:].bitcast(F32),
                                      ALU.subtract).then_inc(m["qT_lo_done"], 1)
                if g == 0 and live(t - 2, TILES):
                    top_two("gate_step", t - 2, [2])
                if g == 1 and live(t - 1, TILES):
                    dve.wait_ge(m["ln_step"], 3 * t - 2)
                    at_least(dve, "x2n_done", t - 1)
                    carry_wait()
                    dve.bn_aggr(mv2[:], st2[:]).then_inc(m["ln_step"], 1)
                if g == 0 and live(t - 2, TILES):
                    top_two("gate_step", t - 2, [3, 4])
                bk = b + (k + 1) // SLOTS
                if (k + 1) % SLOTS == 0 and live(bk, B):
                    at_least(dve, "s_done", SLOTS * bk)
                    kk = kT_all[:, bass.ds(bk, 1), :].rearrange("p a n -> p (a n)")
                    dve.tensor_copy(kT_hl[:, 0, :], kk).then_inc(m["k_hi_done"], 1)
                    dve.wait_ge(m["k_hi_done"], bk + 1)
                    dve.tensor_tensor(kT_hl[:, 1, :], kk, kT_hl[:, 0, :].bitcast(F32), ALU.subtract).then_inc(m["k_split"], 1)
                tq = TPB * b + k // GPT + 1
                if g == 2 and live(tq, TILES):
                    jq = (k // GPT + 1) % 2
                    at_least(dve, "q_done", GPT * (tq - 1))
                    if isinstance(tq, int) and tq >= TPB:
                        dve.wait_ge(m["latent_sb"], min(tq // TPB, B - 1))
                    q = qc_all[:, bass.ds(P * tq, P)]
                    dve.tensor_copy(qc_hi[jq][:], q).then_inc(m["qc_hi_done"], 1)
                    dve.wait_ge(m["qc_hi_done"], tq + 1)
                    dve.tensor_tensor(qc_lo[jq][:], q, qc_hi[jq][:].bitcast(F32), ALU.subtract).then_inc(m["qc_split"], 1)
                if g == 1 and live(t - 1, TILES):
                    dve.wait_ge(m["ln_step"], 3 * t - 1)
                    dve.tensor_scalar(veps2[:], mv2[:, 1:2], EPS, None, ALU.add).then_inc(m["ln_step"], 1)
                if piece_of(i - 1, B - 1):
                    latent_copy(dve, i)
                if live(i, GROUPS):
                    at_least(dve, "exp_done", i + 1)
                    at_least(dve, "prob_normed", i - 1)
                    dve.reciprocal(prec[r][:], psum_h[r][:]).then_inc(m["recip_done"], 1)
                if isinstance(i, int) and i in (-2, -1):
                    late_stats(dve, i + 4)
                if piece_of(i + 1, B - 1):
                    x_norm(dve, i + 2)
                if g == 0 and live(t - 2, TILES):
                    j = (k // GPT - 2) % 2
                    top_two("gate_step", t - 2, [5, 6])
                    at_least(dve, "relu_done", GPT * (t - 3))
                    dve.tensor_scalar(gates[j][:], gt2[:], 0.5, None, ALU.mult).then_inc(m["gates_ready"], 1)
                if g == 2 and live(t - 1, TILES):
                    j = (k // GPT - 1) % 2
                    at_least(dve, "rstd2_done", t)
                    at_least(dve, "xT_done", t - 1)
                    dve.tensor_scalar(x2n[:], x2[j][:], mv2[:, 0:1], rstd2[:], ALU.subtract, ALU.mult).then_inc(m["x2n_done"], 1)

            near = dve.value_load(flag[0:1, 0:1], min_val=0, max_val=1)
            with dve.If(near == 1):
                walk(dve, slot)
            with dve.Else():
                general_dve(dve, carry_wait, top_two)

        @main.sync
        def _(sp):
            for r in range(3):
                sp.dma_start(bias3[r:r + 1, :], eb3[:, r, :]).then_inc(S("ld_bias3"), 16)

            near = sp.value_load(flag[0:1, 0:1], min_val=0, max_val=1)
            with sp.If(near == 1):
                with sp.Fori(0, B) as b:
                    for j in range(TPB):
                        sp.wait_ge(m["acc_step"], 2 * GPT * (TPB * b + j) + 2 * GPT)
                        sp.dma_start(out[bass.ds(TPB * b + j, 1)].rearrange("a p d -> p (a d)"),
                                     acc[j][:]).then_inc(m[f"out_stored{j}"], 16)
                for j in range(TPB):
                    sp.wait_ge(m[f"out_stored{j}"], 16 * B)
            with sp.Else():
                general_sp(sp)


_INS = ["x", "ctx_t", "itok", "w_kvc", "w_dq", "w_uq_t", "w_qr", "w_uk_t", "w_kr", "w_uv_t", "w_o",
        "gate_w", "gate_b", "expert_w", "expert_b", "rope", "w_kvc_t"]


def rope_table():
    half = R // 2
    inv_freq = (1.0 / np.power(np.float32(10000.0), np.arange(half, dtype=np.float32) / np.float32(half))).astype(np.float32)
    ang = (np.arange(KCH * P, dtype=np.float32)[:, None] * inv_freq).astype(np.float64)
    cos, sin = np.cos(ang).astype(np.float32), np.sin(ang).astype(np.float32)
    return np.ascontiguousarray(np.concatenate([cos, cos, -sin, sin], axis=1))


def kernel(x, ctx_2048, itok_BxS_0_1023, L0_xattn_W_kvc, L0_xattn_W_dq, L0_xattn_W_uq, L0_xattn_W_qr, L0_xattn_W_uk,
           L0_xattn_W_kr, L0_xattn_W_uv, L0_xattn_W_o, L0_ffn_gate_w, L0_ffn_gate_b, L0_ffn_expert_w, L0_ffn_expert_b):
    import concourse.bacc as bacc
    from concourse.bass_utils import run_bass_kernel_spmd

    arrays = {
        "x": np.asarray(x).reshape(TILES, P, D),
        "ctx_t": np.asarray(ctx_2048).transpose(2, 0, 1),
        "itok": np.asarray(itok_BxS_0_1023).reshape(TILES, P).T,
        "w_kvc": L0_xattn_W_kvc, "w_dq": L0_xattn_W_dq, "w_uq_t": np.asarray(L0_xattn_W_uq).T, "w_qr": L0_xattn_W_qr,
        "w_uk_t": np.asarray(L0_xattn_W_uk).T, "w_kr": L0_xattn_W_kr, "w_uv_t": np.asarray(L0_xattn_W_uv).T,
        "w_o": L0_xattn_W_o, "gate_w": L0_ffn_gate_w, "gate_b": L0_ffn_gate_b, "expert_w": np.asarray(L0_ffn_expert_w).transpose(1, 0, 2).reshape(D, NE * O),
        "expert_b": L0_ffn_expert_b, "rope": rope_table(), "w_kvc_t": np.asarray(L0_xattn_W_kvc).T,
    }
    nc = bacc.Bacc("TRN2", target_bir_lowering=False, num_devices=1)
    arrays = {n: np.ascontiguousarray(arrays[n]) for n in _INS}
    args = [nc.dram_tensor(f"in_{n}", a.shape, mybir.dt.from_np(a.dtype), kind="ExternalInput").ap()
            for n, a in arrays.items()]
    out = nc.dram_tensor("out", (TILES, P, D), F32, kind="ExternalOutput").ap()
    kernel_program(nc, *args, out)
    r = run_bass_kernel_spmd(nc, [{f"in_{n}": a for n, a in arrays.items()}], core_ids=[0])
    return r.results[0]["out"].reshape(B, L, D)
```
